# Optimizing a Trainium2 kernel written in Bass

```python
import numpy as np
import jax
import jax.numpy as jnp

def _softmax(x, axis=-1):
    return jax.nn.softmax(x, axis=axis)

def _gelu(x):
    return jax.nn.gelu(x, approximate=True)

def _silu(x):
    return jax.nn.silu(x)

def _sigmoid(x):
    return jax.nn.sigmoid(x)

def _layernorm(x, axis=-1, eps=1e-05):
    m = jnp.mean(x, axis=axis, keepdims=True)
    v = jnp.var(x, axis=axis, keepdims=True)
    return (x - m) / jnp.sqrt(v + eps)

def _scatter_add(tgt, idx, src, axis=0):
    return tgt.at[idx].add(src)

def _segment_sum(src, seg, n):
    return jax.ops.segment_sum(src, seg, n)
kernel_name = 'mk_decoder_preln_d4_seqx_r8_a273d0'

def setup_inputs(seed: int=0):
    np.random.seed(seed)
    _w = jnp.asarray

    def _rec_inputs():
        import jax
        import jax.numpy as jnp
        _rk = jax.random.key(seed)
        x = -0.0002928 + 1 * jax.random.normal(jax.random.fold_in(_rk, 1), (8, 256, 128), jnp.float32)
        _lenS = 256 - jax.random.randint(jax.random.fold_in(_rk, 7), (8,), 0, max(1, 256 // 4) + 1, jnp.int32)
        _lenS2 = 256 - jax.random.randint(jax.random.fold_in(_rk, 8), (8,), 0, max(1, 256 // 4) + 1, jnp.int32)
        _ctx_1024P = jax.random.normal(jax.random.fold_in(_rk, 11), (8, 16, 128), jnp.float32)
        _ctx_1024c = jax.random.dirichlet(jax.random.fold_in(_rk, 511), 0.3 * jnp.ones((16,), jnp.float32), (8, 256))
        _ctx_1024t = jnp.einsum('bsk,bkd->bsd', _ctx_1024c, _ctx_1024P)
        _ctx_1024t = _ctx_1024t * jax.lax.rsqrt(jnp.mean(jnp.square(_ctx_1024t)) + 1e-12) * 0.953939
        ctx_1024 = -1.39393e-06 + 0.999914 * (_ctx_1024t + 0.3 * jax.random.normal(jax.random.fold_in(_rk, 611), (8, 256, 128), jnp.float32))
        _validS = jnp.arange(256)[None, :] < _lenS[:, None]
        _validS2 = jnp.arange(256)[None, :] < _lenS2[:, None]
        _causal = jnp.tril(jnp.ones((256, 256), dtype=bool))
        mask_Bx1x1xS2_if1 = jnp.where(jnp.ones((8, 1, 1, 256), dtype=bool), 1, 0).astype(jnp.int32)
        mask_BxS2_bk0 = jnp.logical_not(jnp.broadcast_to(_validS2[:, :], (8, 256)))
        mask_BxSxS2_if1 = jnp.where(jnp.ones((8, 256, 256), dtype=bool), 1, 0).astype(jnp.int32)
        return (x, ctx_1024, mask_Bx1x1xS2_if1, mask_BxS2_bk0, mask_BxSxS2_if1)
    x, ctx_1024, mask_Bx1x1xS2_if1, mask_BxS2_bk0, mask_BxSxS2_if1 = _rec_inputs()

    def _L0_attn_setup():
        import jax, jax.numpy as jnp
        import numpy as np
        B, T, D, H = (2, 256, 128, 4)
        DK, DV = (128, 256)
        HK, HV = (DK // H, DV // H)
        LR = 16
        EPS = 1e-05
        GATE_NORM = 16.0

        def _xavier(k, shape, gain):
            fan_in, fan_out = shape
            lim = gain * np.sqrt(6.0 / (fan_in + fan_out))
            return jax.random.uniform(k, shape, jnp.float32, -lim, lim)

        def _gla_scan(q, k, v, g):
            S0 = jnp.zeros((q.shape[-1], v.shape[-1]), q.dtype)

            def step(S, inp):
                qt, kt, vt, gt = inp
                S = jnp.exp(gt)[:, None] * S + kt[:, None] * vt[None, :]
                return (S, qt @ S)
            return jax.lax.scan(step, S0, (q, k, v, g))[1]

        def _forward(x, Wq, Wk, Wv, Wg, gk_w1, gk_w2, gk_b, Wo, rms_w):
            b, t = (x.shape[0], x.shape[1])
            scale = HK ** (-0.5)
            q = (x @ Wq).reshape(b, t, H, HK).transpose(0, 2, 1, 3) * scale
            k = (x @ Wk).reshape(b, t, H, HK).transpose(0, 2, 1, 3)
            v = (x @ Wv).reshape(b, t, H, HV).transpose(0, 2, 1, 3)
            gl = x @ gk_w1 @ gk_w2 + gk_b
            g = jax.nn.log_sigmoid(gl.astype(jnp.float32)) / GATE_NORM
            g = g.reshape(b, t, H, HK).transpose(0, 2, 1, 3)
            o = jax.vmap(jax.vmap(_gla_scan))(q, k, v, g)
            o = o.transpose(0, 2, 1, 3)
            o = o * jax.lax.rsqrt(jnp.mean(o * o, axis=-1, keepdims=True) + EPS) * rms_w
            o = o.reshape(b, t, DV) * jax.nn.silu(x @ Wg)
            return o @ Wo
        key = jax.random.key(seed)
        ks = jax.random.split(key, 10)
        g_qkv = 2 ** (-2.5)
        return {'x': jax.random.normal(ks[0], (B, T, D), jnp.float32), 'Wq': _xavier(ks[1], (D, DK), g_qkv), 'Wk': _xavier(ks[2], (D, DK), g_qkv), 'Wv': _xavier(ks[3], (D, DV), g_qkv), 'Wg': _xavier(ks[4], (D, DV), g_qkv), 'gk_w1': _xavier(ks[5], (D, LR), g_qkv), 'gk_w2': _xavier(ks[6], (LR, DK), g_qkv), 'gk_b': jnp.zeros((DK,), jnp.float32), 'Wo': _xavier(ks[7], (DV, D), 2 ** (-1)), 'rms_w': jnp.ones((HV,), jnp.float32)}
    _L0_attn_all = _L0_attn_setup()
    _L0_attn_in = {k: v for k, v in _L0_attn_all.items() if k in ('Wq', 'Wk', 'Wv', 'Wg', 'gk_w1', 'gk_w2', 'gk_b', 'Wo', 'rms_w')}
    del _L0_attn_all

    def _L0_xattn_setup():
        import jax, jax.numpy as jnp
        import numpy as np
        B, S, DIM, NH = (2, 256, 128, 8)
        DH = DIM // NH
        GATE_SOFT_CAP = 15.0
        BACKEND_EPS = 5e-05
        NORM_EPS = 1e-06

        def _mlstm_parallel(q, k, v, i_pre, f_pre):
            log_fg = jax.nn.log_sigmoid(f_pre)
            lf_cs = jnp.cumsum(log_fg, axis=-1)
            lf = jnp.concatenate([jnp.zeros_like(lf_cs[..., :1]), lf_cs], axis=-1)
            log_d = lf[..., 1:, None] - lf[..., None, 1:] + i_pre[..., None, :]
            t_idx = jnp.arange(q.shape[2])
            mask = t_idx[:, None] >= t_idx[None, :]
            log_d = jnp.where(mask, log_d, -jnp.inf)
            m = jnp.max(log_d, axis=-1, keepdims=True)
            d_mat = jnp.exp(log_d - m)
            scores = jnp.einsum('bhtd,bhsd->bhts', q, k) * (1.0 / np.sqrt(DH))
            s_mat = scores * d_mat
            denom = jnp.maximum(jnp.abs(jnp.sum(s_mat, axis=-1, keepdims=True)), jnp.exp(-m)) + BACKEND_EPS
            return jnp.einsum('bhts,bhsd->bhtd', s_mat, v) / denom
        key = jax.random.key(seed)
        kq, kk, kv, kw = jax.random.split(key, 4)
        q = jax.random.normal(kq, (B, S, DIM), dtype=jnp.float32)
        k = jax.random.normal(kk, (B, S, DIM), dtype=jnp.float32)
        v = jax.random.normal(kv, (B, S, DIM), dtype=jnp.float32)
        ifgate_w = 0.02 * jax.random.normal(kw, (2 * NH, 3 * DIM), dtype=jnp.float32)
        ifgate_b = jnp.concatenate([jnp.full((NH,), -10.0, dtype=jnp.float32), jnp.linspace(3.0, 6.0, NH, dtype=jnp.float32)])
        outnorm_w = jnp.zeros((DIM,), dtype=jnp.float32)
        return {'q': q, 'k': k, 'v': v, 'ifgate_w': ifgate_w, 'ifgate_b': ifgate_b, 'outnorm_w': outnorm_w}
    _L0_xattn_all = _L0_xattn_setup()
    _L0_xattn_in = {k: v for k, v in _L0_xattn_all.items() if k in ('ifgate_w', 'ifgate_b', 'outnorm_w')}
    del _L0_xattn_all

    def _L0_ffn_setup():
        import jax, jax.numpy as jnp
        import numpy as np
        B, S, D, E, F = (4, 256, 128, 8, 512)
        key = jax.random.key(seed)
        k0, k1, k2, k3 = jax.random.split(key, 4)
        x = jax.random.normal(k0, (B, S, D), dtype=jnp.float32)
        wg = jax.random.normal(k1, (D, E), dtype=jnp.float32) * 0.02
        w_gate = jax.random.normal(k2, (E, D, F), dtype=jnp.float32) * 0.02
        w_down = jax.random.normal(k3, (E, F, D), dtype=jnp.float32) * 0.02
        return {'x': x, 'wg': wg, 'w_gate': w_gate, 'w_down': w_down}
    _L0_ffn_all = _L0_ffn_setup()
    _L0_ffn_in = {k: v for k, v in _L0_ffn_all.items() if k in ('wg', 'w_gate', 'w_down')}
    del _L0_ffn_all

    def _L1_attn_setup():
        import jax, jax.numpy as jnp
        import numpy as np
        NUM_HEADS = 16
        WINDOW = 128

        def apply_rope(x):
            S, Dh = (x.shape[-2], x.shape[-1])
            half = Dh // 2
            inv_freq = 1.0 / 10000.0 ** (jnp.arange(half, dtype=jnp.float32) / half)
            ang = jnp.arange(S, dtype=jnp.float32)[:, None] * inv_freq[None, :]
            cos, sin = (jnp.cos(ang), jnp.sin(ang))
            x1, x2 = (x[..., :half], x[..., half:])
            return jnp.concatenate([x1 * cos - x2 * sin, x1 * sin + x2 * cos], axis=-1).astype(x.dtype)
        key = jax.random.key(seed)
        ks = jax.random.split(key, 5)
        D = 128
        B, S = (2, 256)
        w = 0.02
        return {'x': jax.random.normal(ks[0], (B, S, D), dtype=jnp.float32), 'Wq': jax.random.normal(ks[1], (D, D), dtype=jnp.float32) * w, 'bq': jnp.zeros((D,), dtype=jnp.float32), 'Wk': jax.random.normal(ks[2], (D, D), dtype=jnp.float32) * w, 'bk': jnp.zeros((D,), dtype=jnp.float32), 'Wv': jax.random.normal(ks[3], (D, D), dtype=jnp.float32) * w, 'bv': jnp.zeros((D,), dtype=jnp.float32), 'Wo': jax.random.normal(ks[4], (D, D), dtype=jnp.float32) * w, 'bo': jnp.zeros((D,), dtype=jnp.float32)}
    _L1_attn_all = _L1_attn_setup()
    _L1_attn_in = {k: v for k, v in _L1_attn_all.items() if k in ('Wq', 'bq', 'Wk', 'bk', 'Wv', 'bv', 'Wo', 'bo')}
    del _L1_attn_all

    def _L1_xattn_setup():
        import jax, jax.numpy as jnp
        import numpy as np
        N_HEADS = 16
        D_MODEL = 128
        D_K = D_MODEL // N_HEADS
        B, S = (2, 256)
        key = jax.random.key(seed)
        ks = jax.random.split(key, 12)
        sc = 1.0 / np.sqrt(D_MODEL)
        inp = {'query': jax.random.normal(ks[0], (B, S, D_MODEL), jnp.float32), 'key': jax.random.normal(ks[1], (B, S, D_MODEL), jnp.float32), 'value': jax.random.normal(ks[2], (B, S, D_MODEL), jnp.float32), 'mask': jnp.ones((B, 1, 1, S), jnp.int32), 'Wq': jax.random.normal(ks[3], (D_MODEL, D_MODEL), jnp.float32) * sc, 'bq': jnp.zeros((D_MODEL,), jnp.float32), 'Wk': jax.random.normal(ks[4], (D_MODEL, D_MODEL), jnp.float32) * sc, 'bk': jnp.zeros((D_MODEL,), jnp.float32), 'Wv': jax.random.normal(ks[5], (D_MODEL, D_MODEL), jnp.float32) * sc, 'bv': jnp.zeros((D_MODEL,), jnp.float32), 'Wo': jax.random.normal(ks[6], (D_MODEL, D_MODEL), jnp.float32) * sc, 'bo': jnp.zeros((D_MODEL,), jnp.float32)}
        return inp
    _L1_xattn_all = _L1_xattn_setup()
    _L1_xattn_in = {k: v for k, v in _L1_xattn_all.items() if k in ('Wq', 'bq', 'Wk', 'bk', 'Wv', 'bv', 'Wo', 'bo')}
    del _L1_xattn_all

    def _L1_ffn_setup():
        import jax, jax.numpy as jnp
        import numpy as np
        B, S, D = (4, 512, 128)
        E, I = (8, 256)
        CAPACITY = 2
        K = max(1, int(S / E * CAPACITY))
        key = jax.random.key(seed)
        k1, k2, k3, k4, k5 = jax.random.split(key, 5)
        x = jax.random.normal(k1, (B, S, D), dtype=jnp.float32)
        gate_w = jax.random.normal(k2, (D, E), dtype=jnp.float32) * 0.006
        Wg = jax.random.normal(k3, (E, D, I), dtype=jnp.float32) * 0.02
        Wu = jax.random.normal(k4, (E, D, I), dtype=jnp.float32) * 0.02
        Wd = jax.random.normal(k5, (E, I, D), dtype=jnp.float32) * 0.02
        return {'x': x, 'gate_w': gate_w, 'Wg': Wg, 'Wu': Wu, 'Wd': Wd}
    _L1_ffn_all = _L1_ffn_setup()
    _L1_ffn_in = {k: v for k, v in _L1_ffn_all.items() if k in ('gate_w', 'Wg', 'Wu', 'Wd')}
    del _L1_ffn_all

    def _L2_attn_setup():
        import jax, jax.numpy as jnp
        import numpy as np
        N_HEAD = 16
        NEG_INF = jnp.finfo(jnp.float32).min
        key = jax.random.key(seed)
        k1, k2, k3, k4 = jax.random.split(key, 4)
        B, T, C = (4, 256, 128)
        x = jax.random.normal(k1, (B, T, C), dtype=jnp.float32)
        w_attn = jax.random.normal(k2, (C, 3 * C), dtype=jnp.float32) * C ** (-0.5)
        w_proj = jax.random.normal(k3, (C, C), dtype=jnp.float32) * C ** (-0.5)
        decay_raw = jax.random.normal(k4, (N_HEAD,), dtype=jnp.float32)
        return {'x': x, 'w_attn': w_attn, 'w_proj': w_proj, 'decay_raw': decay_raw}
    _L2_attn_all = _L2_attn_setup()
    _L2_attn_in = {k: v for k, v in _L2_attn_all.items() if k in ('w_attn', 'w_proj', 'decay_raw')}
    del _L2_attn_all

    def _L2_xattn_setup():
        import jax, jax.numpy as jnp
        import numpy as np
        B, S, D = (2, 256, 128)
        H, DH = (16, 64)
        INNER = H * DH
        FF = 512
        SCALE = DH ** (-0.5)
        EPS = 1e-05

        def layernorm(x, g, b):
            m = jnp.mean(x, axis=-1, keepdims=True)
            v = jnp.var(x, axis=-1, keepdims=True)
            return (x - m) * jax.lax.rsqrt(v + EPS) * g + b

        def attention(x, ctx, mask, wq, wk, wv, wo, bo):
            b, n, _ = x.shape
            j = ctx.shape[1]
            q = (x @ wq).reshape(b, n, H, DH).transpose(0, 2, 1, 3)
            k = (ctx @ wk).reshape(b, j, H, DH).transpose(0, 2, 1, 3)
            v = (ctx @ wv).reshape(b, j, H, DH).transpose(0, 2, 1, 3)
            sim = jnp.einsum('bhid,bhjd->bhij', q, k) * SCALE
            if mask is not None:
                neg = -jnp.finfo(sim.dtype).max
                sim = jnp.where(mask[:, None, None, :], neg, sim)
            attn = jax.nn.softmax(sim, axis=-1)
            out = jnp.einsum('bhij,bhjd->bhid', attn, v)
            out = out.transpose(0, 2, 1, 3).reshape(b, n, INNER)
            return out @ wo + bo
        key = jax.random.key(seed)
        ks = jax.random.split(key, 26)
        w = lambda k, shp, fan: (jax.random.normal(k, shp, jnp.float32) / np.sqrt(fan)).astype(jnp.float32)
        return {'x': jax.random.normal(ks[0], (B, S, D), jnp.float32), 'enc_output': jax.random.normal(ks[1], (B, S, D), jnp.float32), 'sa_wq': w(ks[2], (D, INNER), D), 'sa_wk': w(ks[3], (D, INNER), D), 'sa_wv': w(ks[4], (D, INNER), D), 'sa_wo': w(ks[5], (INNER, D), INNER), 'sa_bo': jnp.zeros((D,), jnp.float32), 'ca_wq': w(ks[6], (D, INNER), D), 'ca_wk': w(ks[7], (D, INNER), D), 'ca_wv': w(ks[8], (D, INNER), D), 'ca_wo': w(ks[9], (INNER, D), INNER), 'ca_bo': jnp.zeros((D,), jnp.float32), 'ln1_g': jnp.ones((D,), jnp.float32), 'ln1_b': jnp.zeros((D,), jnp.float32), 'ln2_g': jnp.ones((D,), jnp.float32), 'ln2_b': jnp.zeros((D,), jnp.float32), 'ln3_g': jnp.ones((D,), jnp.float32), 'ln3_b': jnp.zeros((D,), jnp.float32), 'fc1_w': w(ks[10], (D, FF), D), 'fc1_b': jnp.zeros((FF,), jnp.float32), 'fc2_w': w(ks[11], (FF, D), FF), 'fc2_b': jnp.zeros((D,), jnp.float32), 'tgt_mask': jax.random.bernoulli(ks[12], 0.1, (B, S)), 'src_mask': jax.random.bernoulli(ks[13], 0.1, (B, S))}
    _L2_xattn_all = _L2_xattn_setup()
    _L2_xattn_in = {k: v for k, v in _L2_xattn_all.items() if k in ('sa_wq', 'sa_wk', 'sa_wv', 'sa_wo', 'sa_bo', 'ca_wq', 'ca_wk', 'ca_wv', 'ca_wo', 'ca_bo', 'ln1_g', 'ln1_b', 'ln2_g', 'ln2_b', 'ln3_g', 'ln3_b', 'fc1_w', 'fc1_b', 'fc2_w', 'fc2_b')}
    del _L2_xattn_all

    def _L2_ffn_setup():
        import jax, jax.numpy as jnp
        import numpy as np
        D, H, E, K = (128, 128, 8, 2)

        def _moe(x, router_w, w_in, b_in, w_out, b_out):
            B, S, Dm = x.shape
            T = B * S
            x2 = x.reshape(T, Dm)
            logits = x2 @ router_w
            probs = jax.nn.softmax(logits, axis=-1)
            top_p, top_e = jax.lax.top_k(probs, K)
            flat_e = top_e.reshape(-1)
            flat_p = top_p.reshape(-1)
            tok = jnp.repeat(jnp.arange(T), K)
            order = jnp.argsort(flat_e)
            se, sp, st = (flat_e[order], flat_p[order], tok[order])
            xd = x2[st]
            N = xd.shape[0]
            h = jnp.zeros((N, H), x.dtype)
            for e in range(E):
                m = (se == e)[:, None]
                h = h + jnp.where(m, jax.nn.gelu(xd @ w_in[e] + b_in[e]), 0.0)
            y = jnp.zeros((N, Dm), x.dtype)
            for e in range(E):
                m = (se == e)[:, None]
                y = y + jnp.where(m, h @ w_out[e] + b_out[e], 0.0)
            y = y * sp[:, None]
            out = jnp.zeros((T, Dm), x.dtype).at[st].add(y)
            return out.reshape(B, S, Dm)
        key = jax.random.key(seed)
        ks = jax.random.split(key, 5)
        s = lambda k, shape, scale: jax.random.normal(k, shape, dtype=jnp.float32) * scale
        return {'input_batch': s(ks[0], (2, 64, D), 1.0), 'router_w': s(ks[1], (D, E), D ** (-0.5)), 'w_in': s(ks[2], (E, D, H), D ** (-0.5)), 'b_in': jnp.zeros((E, H), jnp.float32), 'w_out': s(ks[3], (E, H, D), H ** (-0.5)), 'b_out': jnp.zeros((E, D), jnp.float32)}
    _L2_ffn_all = _L2_ffn_setup()
    _L2_ffn_in = {k: v for k, v in _L2_ffn_all.items() if k in ('router_w', 'w_in', 'b_in', 'w_out', 'b_out')}
    del _L2_ffn_all

    def _L3_attn_setup():
        import jax, jax.numpy as jnp
        import numpy as np
        import math
        B, T, E, H = (4, 256, 128, 16)
        D = E // H
        rng = jax.random.key(seed)
        k1, k2, k3, k4, k5 = jax.random.split(rng, 5)
        scale_w = 1.0 / math.sqrt(E)
        return {'query': jax.random.normal(k1, (B, T, E), jnp.float32), 'key': jax.random.normal(k2, (B, T, E), jnp.float32), 'value': jax.random.normal(k3, (B, T, E), jnp.float32), 'in_proj_weight': jax.random.normal(k4, (3 * E, E), jnp.float32) * scale_w, 'out_proj_weight': jax.random.normal(k5, (E, E), jnp.float32) * scale_w}
    _L3_attn_all = _L3_attn_setup()
    _L3_attn_in = {k: v for k, v in _L3_attn_all.items() if k in ('key', 'value', 'in_proj_weight', 'out_proj_weight')}
    del _L3_attn_all

    def _L3_xattn_setup():
        import jax, jax.numpy as jnp
        import numpy as np
        D_MODEL = 128
        NUM_HEADS = 16
        D_K = D_MODEL // NUM_HEADS
        key = jax.random.key(seed)
        ks = jax.random.split(key, 12)
        B, S = (2, 256)
        s = 1.0 / np.sqrt(D_MODEL)
        inp = {'query': jax.random.normal(ks[0], (B, S, D_MODEL), jnp.float32), 'key': jax.random.normal(ks[1], (B, S, D_MODEL), jnp.float32), 'value': jax.random.normal(ks[2], (B, S, D_MODEL), jnp.float32), 'mask': jnp.ones((B, S, S), jnp.int32), 'Wq': jax.random.normal(ks[3], (D_MODEL, D_MODEL), jnp.float32) * s, 'bq': jax.random.normal(ks[4], (D_MODEL,), jnp.float32) * s, 'Wk': jax.random.normal(ks[5], (D_MODEL, D_MODEL), jnp.float32) * s, 'bk': jax.random.normal(ks[6], (D_MODEL,), jnp.float32) * s, 'Wv': jax.random.normal(ks[7], (D_MODEL, D_MODEL), jnp.float32) * s, 'bv': jax.random.normal(ks[8], (D_MODEL,), jnp.float32) * s, 'Wo': jax.random.normal(ks[9], (D_MODEL, D_MODEL), jnp.float32) * s, 'bo': jax.random.normal(ks[10], (D_MODEL,), jnp.float32) * s}
        return inp
    _L3_xattn_all = _L3_xattn_setup()
    _L3_xattn_in = {k: v for k, v in _L3_xattn_all.items() if k in ('Wq', 'bq', 'Wk', 'bk', 'Wv', 'bv', 'Wo', 'bo')}
    del _L3_xattn_all

    def _L3_ffn_setup():
        import jax, jax.numpy as jnp
        import numpy as np
        E = 8
        TOP_K = 2
        DIM = 128
        HID = 256
        key = jax.random.key(seed)
        k1, k2, k3, k4, k5 = jax.random.split(key, 5)
        s = 0.02
        x = jax.random.normal(k1, (2, 256, DIM), dtype=jnp.float32)
        Wg = jax.random.normal(k2, (DIM, E), dtype=jnp.float32) * s
        W1 = jax.random.normal(k3, (E, DIM, HID), dtype=jnp.float32) * s
        W2 = jax.random.normal(k4, (E, DIM, HID), dtype=jnp.float32) * s
        W3 = jax.random.normal(k5, (E, HID, DIM), dtype=jnp.float32) * s
        return {'x': x, 'Wg': Wg, 'W1': W1, 'W2': W2, 'W3': W3}
    _L3_ffn_all = _L3_ffn_setup()
    _L3_ffn_in = {k: v for k, v in _L3_ffn_all.items() if k in ('Wg', 'W1', 'W2', 'W3')}
    del _L3_ffn_all
    return {'x': x, 'ctx_1024': ctx_1024, 'mask_Bx1x1xS2_if1': mask_Bx1x1xS2_if1, 'mask_BxS2_bk0': mask_BxS2_bk0, 'mask_BxSxS2_if1': mask_BxSxS2_if1, 'L0_attn_Wq': _L0_attn_in['Wq'], 'L0_attn_Wk': _L0_attn_in['Wk'], 'L0_attn_Wv': _L0_attn_in['Wv'], 'L0_attn_Wg': _L0_attn_in['Wg'], 'L0_attn_gk_w1': _L0_attn_in['gk_w1'], 'L0_attn_gk_w2': _L0_attn_in['gk_w2'], 'L0_attn_gk_b': _L0_attn_in['gk_b'], 'L0_attn_Wo': _L0_attn_in['Wo'], 'L0_attn_rms_w': _L0_attn_in['rms_w'], 'L0_xattn_ifgate_w': _L0_xattn_in['ifgate_w'], 'L0_xattn_ifgate_b': _L0_xattn_in['ifgate_b'], 'L0_xattn_outnorm_w': _L0_xattn_in['outnorm_w'], 'L0_ffn_wg': _L0_ffn_in['wg'], 'L0_ffn_w_gate': _L0_ffn_in['w_gate'], 'L0_ffn_w_down': _L0_ffn_in['w_down'], 'L1_attn_Wq': _L1_attn_in['Wq'], 'L1_attn_bq': _L1_attn_in['bq'], 'L1_attn_Wk': _L1_attn_in['Wk'], 'L1_attn_bk': _L1_attn_in['bk'], 'L1_attn_Wv': _L1_attn_in['Wv'], 'L1_attn_bv': _L1_attn_in['bv'], 'L1_attn_Wo': _L1_attn_in['Wo'], 'L1_attn_bo': _L1_attn_in['bo'], 'L1_xattn_Wq': _L1_xattn_in['Wq'], 'L1_xattn_bq': _L1_xattn_in['bq'], 'L1_xattn_Wk': _L1_xattn_in['Wk'], 'L1_xattn_bk': _L1_xattn_in['bk'], 'L1_xattn_Wv': _L1_xattn_in['Wv'], 'L1_xattn_bv': _L1_xattn_in['bv'], 'L1_xattn_Wo': _L1_xattn_in['Wo'], 'L1_xattn_bo': _L1_xattn_in['bo'], 'L1_ffn_gate_w': _L1_ffn_in['gate_w'], 'L1_ffn_Wg': _L1_ffn_in['Wg'], 'L1_ffn_Wu': _L1_ffn_in['Wu'], 'L1_ffn_Wd': _L1_ffn_in['Wd'], 'L2_attn_w_attn': _L2_attn_in['w_attn'], 'L2_attn_w_proj': _L2_attn_in['w_proj'], 'L2_attn_decay_raw': _L2_attn_in['decay_raw'], 'L2_xattn_sa_wq': _L2_xattn_in['sa_wq'], 'L2_xattn_sa_wk': _L2_xattn_in['sa_wk'], 'L2_xattn_sa_wv': _L2_xattn_in['sa_wv'], 'L2_xattn_sa_wo': _L2_xattn_in['sa_wo'], 'L2_xattn_sa_bo': _L2_xattn_in['sa_bo'], 'L2_xattn_ca_wq': _L2_xattn_in['ca_wq'], 'L2_xattn_ca_wk': _L2_xattn_in['ca_wk'], 'L2_xattn_ca_wv': _L2_xattn_in['ca_wv'], 'L2_xattn_ca_wo': _L2_xattn_in['ca_wo'], 'L2_xattn_ca_bo': _L2_xattn_in['ca_bo'], 'L2_xattn_ln1_g': _L2_xattn_in['ln1_g'], 'L2_xattn_ln1_b': _L2_xattn_in['ln1_b'], 'L2_xattn_ln2_g': _L2_xattn_in['ln2_g'], 'L2_xattn_ln2_b': _L2_xattn_in['ln2_b'], 'L2_xattn_ln3_g': _L2_xattn_in['ln3_g'], 'L2_xattn_ln3_b': _L2_xattn_in['ln3_b'], 'L2_xattn_fc1_w': _L2_xattn_in['fc1_w'], 'L2_xattn_fc1_b': _L2_xattn_in['fc1_b'], 'L2_xattn_fc2_w': _L2_xattn_in['fc2_w'], 'L2_xattn_fc2_b': _L2_xattn_in['fc2_b'], 'L2_ffn_router_w': _L2_ffn_in['router_w'], 'L2_ffn_w_in': _L2_ffn_in['w_in'], 'L2_ffn_b_in': _L2_ffn_in['b_in'], 'L2_ffn_w_out': _L2_ffn_in['w_out'], 'L2_ffn_b_out': _L2_ffn_in['b_out'], 'L3_attn_key': _L3_attn_in['key'], 'L3_attn_value': _L3_attn_in['value'], 'L3_attn_in_proj_weight': _L3_attn_in['in_proj_weight'], 'L3_attn_out_proj_weight': _L3_attn_in['out_proj_weight'], 'L3_xattn_Wq': _L3_xattn_in['Wq'], 'L3_xattn_bq': _L3_xattn_in['bq'], 'L3_xattn_Wk': _L3_xattn_in['Wk'], 'L3_xattn_bk': _L3_xattn_in['bk'], 'L3_xattn_Wv': _L3_xattn_in['Wv'], 'L3_xattn_bv': _L3_xattn_in['bv'], 'L3_xattn_Wo': _L3_xattn_in['Wo'], 'L3_xattn_bo': _L3_xattn_in['bo'], 'L3_ffn_Wg': _L3_ffn_in['Wg'], 'L3_ffn_W1': _L3_ffn_in['W1'], 'L3_ffn_W2': _L3_ffn_in['W2'], 'L3_ffn_W3': _L3_ffn_in['W3']}

def reference(x, ctx_1024, mask_Bx1x1xS2_if1, mask_BxS2_bk0, mask_BxSxS2_if1, L0_attn_Wq, L0_attn_Wk, L0_attn_Wv, L0_attn_Wg, L0_attn_gk_w1, L0_attn_gk_w2, L0_attn_gk_b, L0_attn_Wo, L0_attn_rms_w, L0_xattn_ifgate_w, L0_xattn_ifgate_b, L0_xattn_outnorm_w, L0_ffn_wg, L0_ffn_w_gate, L0_ffn_w_down, L1_attn_Wq, L1_attn_bq, L1_attn_Wk, L1_attn_bk, L1_attn_Wv, L1_attn_bv, L1_attn_Wo, L1_attn_bo, L1_xattn_Wq, L1_xattn_bq, L1_xattn_Wk, L1_xattn_bk, L1_xattn_Wv, L1_xattn_bv, L1_xattn_Wo, L1_xattn_bo, L1_ffn_gate_w, L1_ffn_Wg, L1_ffn_Wu, L1_ffn_Wd, L2_attn_w_attn, L2_attn_w_proj, L2_attn_decay_raw, L2_xattn_sa_wq, L2_xattn_sa_wk, L2_xattn_sa_wv, L2_xattn_sa_wo, L2_xattn_sa_bo, L2_xattn_ca_wq, L2_xattn_ca_wk, L2_xattn_ca_wv, L2_xattn_ca_wo, L2_xattn_ca_bo, L2_xattn_ln1_g, L2_xattn_ln1_b, L2_xattn_ln2_g, L2_xattn_ln2_b, L2_xattn_ln3_g, L2_xattn_ln3_b, L2_xattn_fc1_w, L2_xattn_fc1_b, L2_xattn_fc2_w, L2_xattn_fc2_b, L2_ffn_router_w, L2_ffn_w_in, L2_ffn_b_in, L2_ffn_w_out, L2_ffn_b_out, L3_attn_key, L3_attn_value, L3_attn_in_proj_weight, L3_attn_out_proj_weight, L3_xattn_Wq, L3_xattn_bq, L3_xattn_Wk, L3_xattn_bk, L3_xattn_Wv, L3_xattn_bv, L3_xattn_Wo, L3_xattn_bo, L3_ffn_Wg, L3_ffn_W1, L3_ffn_W2, L3_ffn_W3):
    import jax
    import jax.numpy as jnp

    def _L0_attn_ref(x, Wq, Wk, Wv, Wg, gk_w1, gk_w2, gk_b, Wo, rms_w):
        import jax, jax.numpy as jnp
        import numpy as np
        B, T, D, H = (2, 256, 128, 4)
        DK, DV = (128, 256)
        HK, HV = (DK // H, DV // H)
        LR = 16
        EPS = 1e-05
        GATE_NORM = 16.0

        def _xavier(k, shape, gain):
            fan_in, fan_out = shape
            lim = gain * np.sqrt(6.0 / (fan_in + fan_out))
            return jax.random.uniform(k, shape, jnp.float32, -lim, lim)

        def _gla_scan(q, k, v, g):
            S0 = jnp.zeros((q.shape[-1], v.shape[-1]), q.dtype)

            def step(S, inp):
                qt, kt, vt, gt = inp
                S = jnp.exp(gt)[:, None] * S + kt[:, None] * vt[None, :]
                return (S, qt @ S)
            return jax.lax.scan(step, S0, (q, k, v, g))[1]

        def _forward(x, Wq, Wk, Wv, Wg, gk_w1, gk_w2, gk_b, Wo, rms_w):
            b, t = (x.shape[0], x.shape[1])
            scale = HK ** (-0.5)
            q = (x @ Wq).reshape(b, t, H, HK).transpose(0, 2, 1, 3) * scale
            k = (x @ Wk).reshape(b, t, H, HK).transpose(0, 2, 1, 3)
            v = (x @ Wv).reshape(b, t, H, HV).transpose(0, 2, 1, 3)
            gl = x @ gk_w1 @ gk_w2 + gk_b
            g = jax.nn.log_sigmoid(gl.astype(jnp.float32)) / GATE_NORM
            g = g.reshape(b, t, H, HK).transpose(0, 2, 1, 3)
            o = jax.vmap(jax.vmap(_gla_scan))(q, k, v, g)
            o = o.transpose(0, 2, 1, 3)
            o = o * jax.lax.rsqrt(jnp.mean(o * o, axis=-1, keepdims=True) + EPS) * rms_w
            o = o.reshape(b, t, DV) * jax.nn.silu(x @ Wg)
            return o @ Wo
        return _forward(x, Wq, Wk, Wv, Wg, gk_w1, gk_w2, gk_b, Wo, rms_w)

    def _L0_xattn_ref(q, k, v, ifgate_w, ifgate_b, outnorm_w):
        import jax, jax.numpy as jnp
        import numpy as np
        B, S, DIM, NH = (2, 256, 128, 8)
        DH = DIM // NH
        GATE_SOFT_CAP = 15.0
        BACKEND_EPS = 5e-05
        NORM_EPS = 1e-06

        def _mlstm_parallel(q, k, v, i_pre, f_pre):
            log_fg = jax.nn.log_sigmoid(f_pre)
            lf_cs = jnp.cumsum(log_fg, axis=-1)
            lf = jnp.concatenate([jnp.zeros_like(lf_cs[..., :1]), lf_cs], axis=-1)
            log_d = lf[..., 1:, None] - lf[..., None, 1:] + i_pre[..., None, :]
            t_idx = jnp.arange(q.shape[2])
            mask = t_idx[:, None] >= t_idx[None, :]
            log_d = jnp.where(mask, log_d, -jnp.inf)
            m = jnp.max(log_d, axis=-1, keepdims=True)
            d_mat = jnp.exp(log_d - m)
            scores = jnp.einsum('bhtd,bhsd->bhts', q, k) * (1.0 / np.sqrt(DH))
            s_mat = scores * d_mat
            denom = jnp.maximum(jnp.abs(jnp.sum(s_mat, axis=-1, keepdims=True)), jnp.exp(-m)) + BACKEND_EPS
            return jnp.einsum('bhts,bhsd->bhtd', s_mat, v) / denom
        b, s, dim = q.shape
        gate_in = jnp.concatenate([q, k, v], axis=-1)
        pre = gate_in @ ifgate_w.T + ifgate_b
        pre = GATE_SOFT_CAP * jnp.tanh(pre / GATE_SOFT_CAP)
        i_pre = pre[..., :NH].transpose(0, 2, 1)
        f_pre = pre[..., NH:].transpose(0, 2, 1)
        qh = q.reshape(b, s, NH, DH).transpose(0, 2, 1, 3)
        kh = k.reshape(b, s, NH, DH).transpose(0, 2, 1, 3)
        vh = v.reshape(b, s, NH, DH).transpose(0, 2, 1, 3)
        h = _mlstm_parallel(qh, kh, vh, i_pre, f_pre)
        rrms = jax.lax.rsqrt(jnp.mean(h * h, axis=-1, keepdims=True) + NORM_EPS)
        gain = (1.0 + outnorm_w).reshape(1, NH, 1, DH)
        h = h * rrms * gain
        return h.transpose(0, 2, 1, 3).reshape(b, s, dim)

    def _L0_ffn_ref(x, wg, w_gate, w_down):
        import jax, jax.numpy as jnp
        import numpy as np
        B, S, D, E, F = (4, 256, 128, 8, 512)
        Bb, Ss, Dd = x.shape
        Ee = wg.shape[1]
        T = Bb * Ss
        C = 2 * T // Ee
        tokens = x.reshape(T, Dd)
        logits = tokens.astype(jnp.float32) @ wg.astype(jnp.float32)
        gates = jax.nn.softmax(logits, axis=-1)
        idx1 = jnp.argmax(gates, axis=-1)
        mask1 = jax.nn.one_hot(idx1, Ee, dtype=jnp.int32)
        logits_no1 = jnp.where(mask1 > 0, -jnp.inf, logits)
        idx2 = jnp.argmax(logits_no1, axis=-1)
        mask2 = jax.nn.one_hot(idx2, Ee, dtype=jnp.int32)
        g1 = jnp.take_along_axis(gates, idx1[:, None], axis=-1)[:, 0]
        g2 = jnp.take_along_axis(gates, idx2[:, None], axis=-1)[:, 0]
        denom = jnp.clip(g1 + g2, 1e-09, None)
        g1, g2 = (g1 / denom, g2 / denom)
        loc1 = jnp.cumsum(mask1, axis=0) - mask1
        loc2 = jnp.cumsum(mask2, axis=0) - mask2 + jnp.sum(mask1, axis=0, keepdims=True)
        loc1_s = jnp.sum(loc1 * mask1, axis=-1)
        loc2_s = jnp.sum(loc2 * mask2, axis=-1)
        keep1 = (loc1_s < C).astype(x.dtype)
        keep2 = (loc2_s < C).astype(x.dtype)
        f1 = idx1 * C + jnp.minimum(loc1_s, C - 1)
        f2 = idx2 * C + jnp.minimum(loc2_s, C - 1)
        disp = jnp.zeros((Ee * C, Dd), dtype=x.dtype)
        disp = disp.at[f1].add(tokens * keep1[:, None])
        disp = disp.at[f2].add(tokens * keep2[:, None])
        disp = disp.reshape(Ee, C, Dd)
        h = jax.nn.gelu(jnp.einsum('ecd,edf->ecf', disp, w_gate), approximate=False)
        eo = jnp.einsum('ecf,efd->ecd', h, w_down).reshape(Ee * C, Dd)
        out = (g1 * keep1)[:, None].astype(x.dtype) * eo[f1] + (g2 * keep2)[:, None].astype(x.dtype) * eo[f2]
        return out.reshape(Bb, Ss, Dd)

    def _L1_attn_ref(x, Wq, bq, Wk, bk, Wv, bv, Wo, bo):
        import jax, jax.numpy as jnp
        import numpy as np
        NUM_HEADS = 16
        WINDOW = 128

        def apply_rope(x):
            S, Dh = (x.shape[-2], x.shape[-1])
            half = Dh // 2
            inv_freq = 1.0 / 10000.0 ** (jnp.arange(half, dtype=jnp.float32) / half)
            ang = jnp.arange(S, dtype=jnp.float32)[:, None] * inv_freq[None, :]
            cos, sin = (jnp.cos(ang), jnp.sin(ang))
            x1, x2 = (x[..., :half], x[..., half:])
            return jnp.concatenate([x1 * cos - x2 * sin, x1 * sin + x2 * cos], axis=-1).astype(x.dtype)
        B, S, D = x.shape
        H = NUM_HEADS
        Dh = D // H

        def proj(W, b):
            y = jnp.einsum('bsd,ed->bse', x, W) + b
            return y.reshape(B, S, H, Dh).transpose(0, 2, 1, 3)
        q = apply_rope(proj(Wq, bq)) * Dh ** (-0.5)
        k = apply_rope(proj(Wk, bk))
        v = proj(Wv, bv)
        scores = jnp.einsum('bhqd,bhkd->bhqk', q, k)
        idx = jnp.arange(S)
        rel = idx[None, :] - idx[:, None]
        blocked = (rel > 0) | (rel < -WINDOW)
        scores = jnp.where(blocked[None, None], -jnp.inf, scores)
        probs = jax.nn.softmax(scores, axis=-1)
        out = jnp.einsum('bhqk,bhkd->bhqd', probs, v)
        out = out.transpose(0, 2, 1, 3).reshape(B, S, D)
        return jnp.einsum('bsd,ed->bse', out, Wo) + bo

    def _L1_xattn_ref(query, key, value, mask, Wq, bq, Wk, bk, Wv, bv, Wo, bo):
        import jax, jax.numpy as jnp
        import numpy as np
        N_HEADS = 16
        D_MODEL = 128
        D_K = D_MODEL // N_HEADS
        B, S = (2, 256)
        q = query @ Wq.T + bq
        k = key @ Wk.T + bk
        v = value @ Wv.T + bv

        def split_heads(x):
            b, s, _ = x.shape
            return x.reshape(b, s, N_HEADS, D_K).transpose(0, 2, 1, 3)
        q, k, v = (split_heads(q), split_heads(k), split_heads(v))
        att = jnp.einsum('bhqd,bhkd->bhqk', q, k) / jnp.sqrt(jnp.float32(D_K))
        att = jnp.where(mask == 0, -jnp.inf, att)
        scores = jax.nn.softmax(att, axis=-1)
        out = jnp.einsum('bhqk,bhkd->bhqd', scores, v)
        b = out.shape[0]
        out = out.transpose(0, 2, 1, 3).reshape(b, -1, N_HEADS * D_K)
        return out @ Wo.T + bo

    def _L1_ffn_ref(x, gate_w, Wg, Wu, Wd):
        import jax, jax.numpy as jnp
        import numpy as np
        B, S, D = (4, 512, 128)
        E, I = (8, 256)
        CAPACITY = 2
        K = max(1, int(S / E * CAPACITY))
        logits = jnp.einsum('bsd,de->bse', x, gate_w)
        affinity = jax.nn.softmax(logits, axis=-1)
        affinity_T = jnp.transpose(affinity, (0, 2, 1))
        gating, index = jax.lax.top_k(affinity_T, K)
        b_idx = jnp.arange(x.shape[0])[:, None, None]
        x_sel = x[b_idx, index]
        g = jnp.einsum('bekd,edi->beki', x_sel, Wg)
        u = jnp.einsum('bekd,edi->beki', x_sel, Wu)
        h = jax.nn.silu(g) * u
        out = jnp.einsum('beki,eid->bekd', h, Wd)
        contrib = out * gating[..., None]
        x_out = jnp.zeros_like(x).at[b_idx, index].add(contrib)
        return x_out

    def _L2_attn_ref(x, w_attn, w_proj, decay_raw):
        import jax, jax.numpy as jnp
        import numpy as np
        N_HEAD = 16
        NEG_INF = jnp.finfo(jnp.float32).min
        B, T, C = x.shape
        H = N_HEAD
        D = C // H
        qkv = x @ w_attn
        q, k, v = jnp.split(qkv, 3, axis=-1)
        q = q.reshape(B, T, H, D).transpose(0, 2, 1, 3)
        k = k.reshape(B, T, H, D).transpose(0, 2, 1, 3)
        v = v.reshape(B, T, H, D).transpose(0, 2, 1, 3)
        idx = jnp.arange(T)
        causal = jnp.where(idx[None, :] > idx[:, None], NEG_INF, 0.0).astype(jnp.float32)
        decay = jax.nn.softplus(decay_raw)
        dist = jnp.maximum(idx[:, None] - idx[None, :], 0).astype(jnp.float32)
        log1p_dist = jnp.log1p(dist)
        logw = -jnp.log1p(decay[:, None, None] * log1p_dist)
        attn_mask = causal[None, :, :] + logw
        scores = jnp.einsum('bhqd,bhkd->bhqk', q, k) * (1.0 / jnp.sqrt(jnp.float32(D)))
        scores = scores + attn_mask[None]
        att = jax.nn.softmax(scores, axis=-1)
        y = jnp.einsum('bhqk,bhkd->bhqd', att, v)
        y = y.transpose(0, 2, 1, 3).reshape(B, T, C)
        return y @ w_proj

    def _L2_xattn_ref(x, enc_output, sa_wq, sa_wk, sa_wv, sa_wo, sa_bo, ca_wq, ca_wk, ca_wv, ca_wo, ca_bo, ln1_g, ln1_b, ln2_g, ln2_b, ln3_g, ln3_b, fc1_w, fc1_b, fc2_w, fc2_b, tgt_mask, src_mask):
        import jax, jax.numpy as jnp
        import numpy as np
        B, S, D = (2, 256, 128)
        H, DH = (16, 64)
        INNER = H * DH
        FF = 512
        SCALE = DH ** (-0.5)
        EPS = 1e-05

        def layernorm(x, g, b):
            m = jnp.mean(x, axis=-1, keepdims=True)
            v = jnp.var(x, axis=-1, keepdims=True)
            return (x - m) * jax.lax.rsqrt(v + EPS) * g + b

        def attention(x, ctx, mask, wq, wk, wv, wo, bo):
            b, n, _ = x.shape
            j = ctx.shape[1]
            q = (x @ wq).reshape(b, n, H, DH).transpose(0, 2, 1, 3)
            k = (ctx @ wk).reshape(b, j, H, DH).transpose(0, 2, 1, 3)
            v = (ctx @ wv).reshape(b, j, H, DH).transpose(0, 2, 1, 3)
            sim = jnp.einsum('bhid,bhjd->bhij', q, k) * SCALE
            if mask is not None:
                neg = -jnp.finfo(sim.dtype).max
                sim = jnp.where(mask[:, None, None, :], neg, sim)
            attn = jax.nn.softmax(sim, axis=-1)
            out = jnp.einsum('bhij,bhjd->bhid', attn, v)
            out = out.transpose(0, 2, 1, 3).reshape(b, n, INNER)
            return out @ wo + bo
        a = attention(x, x, tgt_mask, sa_wq, sa_wk, sa_wv, sa_wo, sa_bo)
        x = layernorm(x + a, ln1_g, ln1_b)
        a = attention(x, enc_output, src_mask, ca_wq, ca_wk, ca_wv, ca_wo, ca_bo)
        x = layernorm(x + a, ln2_g, ln2_b)
        h = jax.nn.gelu(x @ fc1_w + fc1_b, approximate=False)
        ff = h @ fc2_w + fc2_b
        x = layernorm(x + ff, ln3_g, ln3_b)
        return x

    def _L2_ffn_ref(input_batch, router_w, w_in, b_in, w_out, b_out):
        import jax, jax.numpy as jnp
        import numpy as np
        D, H, E, K = (128, 128, 8, 2)

        def _moe(x, router_w, w_in, b_in, w_out, b_out):
            B, S, Dm = x.shape
            T = B * S
            x2 = x.reshape(T, Dm)
            logits = x2 @ router_w
            probs = jax.nn.softmax(logits, axis=-1)
            top_p, top_e = jax.lax.top_k(probs, K)
            flat_e = top_e.reshape(-1)
            flat_p = top_p.reshape(-1)
            tok = jnp.repeat(jnp.arange(T), K)
            order = jnp.argsort(flat_e)
            se, sp, st = (flat_e[order], flat_p[order], tok[order])
            xd = x2[st]
            N = xd.shape[0]
            h = jnp.zeros((N, H), x.dtype)
            for e in range(E):
                m = (se == e)[:, None]
                h = h + jnp.where(m, jax.nn.gelu(xd @ w_in[e] + b_in[e]), 0.0)
            y = jnp.zeros((N, Dm), x.dtype)
            for e in range(E):
                m = (se == e)[:, None]
                y = y + jnp.where(m, h @ w_out[e] + b_out[e], 0.0)
            y = y * sp[:, None]
            out = jnp.zeros((T, Dm), x.dtype).at[st].add(y)
            return out.reshape(B, S, Dm)
        return _moe(input_batch, router_w, w_in, b_in, w_out, b_out)

    def _L3_attn_ref(query, key, value, in_proj_weight, out_proj_weight):
        import jax, jax.numpy as jnp
        import numpy as np
        import math
        B, T, E, H = (4, 256, 128, 16)
        D = E // H
        b, t, e = query.shape
        qkv = jnp.einsum('bte,fe->btf', query, in_proj_weight).reshape(b, t, 3, H, D)
        q = jnp.transpose(qkv[:, :, 0], (0, 2, 1, 3))
        k = jnp.transpose(qkv[:, :, 1], (0, 2, 1, 3))
        v = jnp.transpose(qkv[:, :, 2], (0, 2, 1, 3))
        q = q / math.sqrt(D)
        scores = jnp.einsum('bhqd,bhkd->bhqk', q, k)
        pos = jnp.arange(t)
        causal = pos[:, None] >= pos[None, :]
        scores = jnp.where(causal[None, None], scores, jnp.float32(-jnp.inf))
        attn = jax.nn.softmax(scores, axis=-1)
        out = jnp.einsum('bhqk,bhkd->bhqd', attn, v)
        out = jnp.transpose(out, (0, 2, 1, 3)).reshape(b, t, e)
        out = jnp.einsum('bte,fe->btf', out, out_proj_weight)
        return out

    def _L3_xattn_ref(query, key, value, mask, Wq, bq, Wk, bk, Wv, bv, Wo, bo):
        import jax, jax.numpy as jnp
        import numpy as np
        D_MODEL = 128
        NUM_HEADS = 16
        D_K = D_MODEL // NUM_HEADS
        B, S, _ = query.shape

        def proj(x, W, b):
            return (x @ W.T + b).reshape(B, -1, NUM_HEADS, D_K).transpose(0, 2, 1, 3)
        q = proj(query, Wq, bq)
        k = proj(key, Wk, bk)
        v = proj(value, Wv, bv)
        scores = jnp.einsum('bhqd,bhkd->bhqk', q, k) / jnp.sqrt(jnp.float32(D_K))
        m = mask[:, None, :, :]
        scores = jnp.where(m == 0, jnp.float32(-1000000000.0), scores)
        attn = jax.nn.softmax(scores, axis=-1)
        x = jnp.einsum('bhqk,bhkd->bhqd', attn, v)
        x = x.transpose(0, 2, 1, 3).reshape(B, S, D_MODEL)
        return x @ Wo.T + bo

    def _L3_ffn_ref(x, Wg, W1, W2, W3):
        import jax, jax.numpy as jnp
        import numpy as np
        E = 8
        TOP_K = 2
        DIM = 128
        HID = 256
        B, T, C = x.shape
        xf = x.reshape(-1, C)
        logits = xf @ Wg
        top_w, top_i = jax.lax.top_k(logits, TOP_K)
        top_w = jax.nn.softmax(top_w, axis=-1)
        one_hot = jax.nn.one_hot(top_i, E, dtype=xf.dtype)
        combine = jnp.einsum('nk,nke->ne', top_w, one_hot)
        h = jnp.einsum('nc,ech->enh', xf, W1)
        g = jnp.einsum('nc,ech->enh', xf, W2)
        y = jnp.einsum('enh,ehc->enc', jax.nn.silu(h) * g, W3)
        out = jnp.einsum('enc,ne->nc', y, combine)
        return out.reshape(B, T, C)
    x = x + _L0_attn_ref(_layernorm(x, axis=-1), L0_attn_Wq, L0_attn_Wk, L0_attn_Wv, L0_attn_Wg, L0_attn_gk_w1, L0_attn_gk_w2, L0_attn_gk_b, L0_attn_Wo, L0_attn_rms_w)
    x = x + _L0_xattn_ref(_layernorm(x, axis=-1), ctx_1024, ctx_1024, L0_xattn_ifgate_w, L0_xattn_ifgate_b, L0_xattn_outnorm_w)
    x = x + _L0_ffn_ref(_layernorm(x, axis=-1), L0_ffn_wg, L0_ffn_w_gate, L0_ffn_w_down)
    x = x + _L1_attn_ref(_layernorm(x, axis=-1), L1_attn_Wq, L1_attn_bq, L1_attn_Wk, L1_attn_bk, L1_attn_Wv, L1_attn_bv, L1_attn_Wo, L1_attn_bo)
    x = x + _L1_xattn_ref(_layernorm(x, axis=-1), ctx_1024, ctx_1024, mask_Bx1x1xS2_if1, L1_xattn_Wq, L1_xattn_bq, L1_xattn_Wk, L1_xattn_bk, L1_xattn_Wv, L1_xattn_bv, L1_xattn_Wo, L1_xattn_bo)
    x = x + _L1_ffn_ref(_layernorm(x, axis=-1), L1_ffn_gate_w, L1_ffn_Wg, L1_ffn_Wu, L1_ffn_Wd)
    x = x + _L2_attn_ref(_layernorm(x, axis=-1), L2_attn_w_attn, L2_attn_w_proj, L2_attn_decay_raw)
    x = x + _L2_xattn_ref(_layernorm(x, axis=-1), ctx_1024, L2_xattn_sa_wq, L2_xattn_sa_wk, L2_xattn_sa_wv, L2_xattn_sa_wo, L2_xattn_sa_bo, L2_xattn_ca_wq, L2_xattn_ca_wk, L2_xattn_ca_wv, L2_xattn_ca_wo, L2_xattn_ca_bo, L2_xattn_ln1_g, L2_xattn_ln1_b, L2_xattn_ln2_g, L2_xattn_ln2_b, L2_xattn_ln3_g, L2_xattn_ln3_b, L2_xattn_fc1_w, L2_xattn_fc1_b, L2_xattn_fc2_w, L2_xattn_fc2_b, mask_BxS2_bk0, mask_BxS2_bk0)
    x = x + _L2_ffn_ref(_layernorm(x, axis=-1), L2_ffn_router_w, L2_ffn_w_in, L2_ffn_b_in, L2_ffn_w_out, L2_ffn_b_out)
    x = x + _L3_attn_ref(_layernorm(x, axis=-1), L3_attn_key, L3_attn_value, L3_attn_in_proj_weight, L3_attn_out_proj_weight)
    x = x + _L3_xattn_ref(_layernorm(x, axis=-1), ctx_1024, ctx_1024, mask_BxSxS2_if1, L3_xattn_Wq, L3_xattn_bq, L3_xattn_Wk, L3_xattn_bk, L3_xattn_Wv, L3_xattn_bv, L3_xattn_Wo, L3_xattn_bo)
    x = x + _L3_ffn_ref(_layernorm(x, axis=-1), L3_ffn_Wg, L3_ffn_W1, L3_ffn_W2, L3_ffn_W3)
    return x

_drawn_inputs = setup_inputs


def setup_inputs(seed=0):
    import zlib

    import numpy as np

    out = dict(_drawn_inputs(seed))
    spreads = {'L0_attn_gk_b': (0.0, 0.8),
     'L0_attn_rms_w': (1.0, 0.6),
     'L0_xattn_outnorm_w': (0.0, 0.1),
     'L1_attn_bq': (0.0, 0.8),
     'L1_attn_bk': (0.0, 0.8),
     'L1_attn_bv': (0.0, 0.436),
     'L1_attn_bo': (0.0, 0.1),
     'L1_xattn_bq': (0.0, 0.527),
     'L1_xattn_bk': (0.0, 0.8),
     'L1_xattn_bv': (0.0, 0.1),
     'L1_xattn_bo': (0.0, 0.1),
     'L2_xattn_sa_bo': (0.0, 0.1),
     'L2_xattn_ca_bo': (0.0, 0.1),
     'L2_xattn_ln1_g': (1.0, 0.2),
     'L2_xattn_ln1_b': (0.0, 0.1),
     'L2_xattn_ln2_g': (1.0, 0.2),
     'L2_xattn_ln2_b': (0.0, 0.1),
     'L2_xattn_ln3_g': (1.0, 0.2),
     'L2_xattn_ln3_b': (0.0, 0.1),
     'L2_xattn_fc1_b': (0.0, 0.303),
     'L2_xattn_fc2_b': (0.0, 0.1),
     'L2_ffn_b_in': (0.0, 0.706),
     'L2_ffn_b_out': (0.0, 0.463)}
    factors = {'L0_attn_gk_w1': 8.0,
     'L0_attn_gk_w2': 8.0,
     'L0_ffn_wg': 2.98,
     'L1_attn_Wq': 8.0,
     'L1_attn_Wk': 8.0,
     'L1_attn_Wv': 7.61,
     'L1_attn_Wo': 2.772,
     'L1_ffn_gate_w': 8.0,
     'L1_ffn_Wg': 8.0,
     'L1_ffn_Wu': 8.0,
     'L1_ffn_Wd': 8.0,
     'L2_attn_decay_raw': 2.994,
     'L3_xattn_bq': 7.207,
     'L3_xattn_bk': 8.0,
     'L3_ffn_Wg': 8.0,
     'L3_ffn_W1': 8.0,
     'L3_ffn_W2': 8.0,
     'L3_ffn_W3': 8.0}
    for name, (base, spread) in spreads.items():
        noise = np.random.default_rng([zlib.crc32(name.encode()), seed]).standard_normal(out[name].shape)
        drawn = base * np.exp(spread * noise) if base else spread * noise
        out[name] = jnp.asarray(drawn.astype(out[name].dtype))
    for name, factor in factors.items():
        out[name] = (out[name] * factor).astype(out[name].dtype)
    return out
```

```python
from contextlib import ExitStack

import numpy as np

import concourse.bass as bass
from concourse import mybir

P = 128
B, S, D = 8, 256, 128
NT = B * S // P
TPB = S // P
H, DH = 16, 8
HP = 32
WINDOW = 128
E = 8
LN_EPS = 1e-5
NEG = -1e30

F32 = mybir.dt.float32
BF16 = mybir.dt.bfloat16
I32 = mybir.dt.int32
U32 = mybir.dt.uint32
ALU = mybir.AluOpType
ACT = mybir.ActivationFunctionType
AX = mybir.AxisListType


class Count:

    def __init__(self, nc, name, per=1):
        self.sem = nc.alloc_semaphore(name)
        self.per = per

    def at(self, b, k=None):
        if isinstance(b, int):
            b = max(b, -1)
        return (b + 1) * self.per + (self.per if k is None else k)


def start(e, counts):
    for c in counts:
        e.sem_inc(c.sem, c.per)


def constants(nc, g):
    with ExitStack() as ctx:
        made = nc.alloc_semaphore("const_made")
        copied = nc.alloc_semaphore("const_copied")
        loaded = g.loaded["x"]
        block = ctx.enter_context(nc.Block())

        @block.sync
        def _(sp):
            for dst, src in g.first_loads:
                sp.dma_start(dst, src).then_inc(loaded, 16)
            for name, pairs in g.weight_loads:
                for dst, src in pairs:
                    sp.dma_start(dst, src).then_inc(g.loaded[name], 16)
            for dst, src, loaded_area in g.first_area_loads:
                sp.dma_start(dst, src).then_inc(loaded_area, 16)
            sp.wait_ge(loaded, 16 * len(g.first_loads))

        @block.gpsimd
        def _(pool):
            pool.memset(g.ident[:, :], 0.0).then_inc(made, 1)
            pool.memset(g.half[:, :], -0.5).then_inc(made, 1)
            pool.memset(g.rowmask[:, :], 1.0).then_inc(made, 1)
            pool.memset(g.sel[:, :, :], 0.0).then_inc(made, 1)
            pool.memset(g.ones_bf[:, :], 1.0).then_inc(made, 1)
            pool.memset(g.ones[:, :], 1.0).then_inc(made, 1)
            pool.wait_ge(made, 6)
            pool.affine_select(out=g.ident[:, :], in_=g.ident[:, :], compare_op=ALU.not_equal, fill=1.0,
                               base=0, pattern=[[-1, P]], channel_multiplier=1).then_inc(made, 1)
            pool.affine_select(out=g.rowmask[:, :], in_=g.rowmask[:, :], compare_op=ALU.is_ge, fill=0.0,
                               base=0, pattern=[[-DH, H]], channel_multiplier=1).then_inc(made, 1)
            pool.wait_ge(made, 8)
            pool.affine_select(out=g.rowmask[:, :], in_=g.rowmask[:, :], compare_op=ALU.is_ge, fill=0.0,
                               base=DH - 1, pattern=[[DH, H]], channel_multiplier=-1).then_inc(made, 1)
            pool.affine_select(out=g.sel[:, :, :], in_=g.sel[:, :, :], compare_op=ALU.not_equal, fill=1.0,
                               base=0, pattern=[[-1, H], [0, P]], channel_multiplier=1).then_inc(made, 1)
            pool.wait_ge(made, 10)
            pool.affine_select(out=g.sel[:, :, :], in_=g.sel[:, :, :], compare_op=ALU.not_equal, fill=1.0,
                               base=-H, pattern=[[-1, H], [0, P]], channel_multiplier=1).then_inc(made, 1)
            pool.iota(g.iota_e[:, :], pattern=[[1, E]], base=0, channel_multiplier=0,
                      allow_small_or_imprecise_dtypes=True).then_inc(made, 1)
            pool.iota(g.back_e[:, :], pattern=[[-1, E]], base=E, channel_multiplier=0,
                      allow_small_or_imprecise_dtypes=True)
            for m in (g.tri_q, g.tri_k, g.band_q, g.band_k):
                pool.memset(m[:, :], 0.0).then_inc(made, 1)
            pool.wait_ge(made, 16)
            pool.affine_select(out=g.tri_q[:, :], in_=g.tri_q[:, :], compare_op=ALU.is_ge, fill=NEG,
                               base=0, pattern=[[-1, P]], channel_multiplier=1).then_inc(made, 1)
            pool.affine_select(out=g.tri_k[:, :], in_=g.tri_k[:, :], compare_op=ALU.is_ge, fill=NEG,
                               base=0, pattern=[[1, P]], channel_multiplier=-1).then_inc(made, 1)
            pool.affine_select(out=g.band_q[:, :], in_=g.band_q[:, :], compare_op=ALU.is_ge, fill=NEG,
                               base=P, pattern=[[-1, S]], channel_multiplier=1).then_inc(made, 1)
            pool.affine_select(out=g.band_k[:, :], in_=g.band_k[:, :], compare_op=ALU.is_ge, fill=NEG,
                               base=0, pattern=[[1, S]], channel_multiplier=-1).then_inc(made, 1)
            pool.wait_ge(made, 20)
            pool.affine_select(out=g.band_q[:, :], in_=g.band_q[:, :], compare_op=ALU.is_ge, fill=NEG,
                               base=WINDOW - P, pattern=[[1, S]], channel_multiplier=-1).then_inc(made, 1)
            pool.affine_select(out=g.band_k[:, :], in_=g.band_k[:, :], compare_op=ALU.is_ge, fill=NEG,
                               base=WINDOW, pattern=[[-1, S]], channel_multiplier=1).then_inc(made, 1)
            pool.wait_ge(made, 22)

        @block.vector
        def _(dve):
            dve.wait_ge(made, 12)
            dve.tensor_copy(g.ident_bf[:, :], g.ident[:, :]).then_inc(copied, 1)
            dve.wait_ge(copied, 1)


KROWS = 3 * 3 * DH
MASK_ROW = 96


def attention(nc, g, name, w, cross=False, rope=False, window=None, causal=False, alibi=False,
              key_mask=None, full_mask=None, prefetch=()):
    scale = DH ** -0.5
    causal = causal or window is not None
    KC = 384 if causal else 512
    biased = "bq" in w
    HH = H // 2
    with ExitStack() as ctx:
        sb = lambda n, shape, dt=F32: ctx.enter_context(nc.sbuf_tensor(f"{name}_{n}", shape, dt))
        ps = lambda n, shape, dt=F32: ctx.enter_context(nc.psum_tensor(f"{name}_{n}", shape, dt))
        count = lambda n, per=1: Count(nc, f"{name}_{n}", per)
        xn = sb("xn", [P, TPB, D])
        xnT = sb("xnT", [P, S])
        ctxT = sb("ctxT", [P, 2, S]) if cross else None
        stats = sb("stats", [P, TPB, 6])
        mv = sb("mv", [P, TPB, 2])
        var_eps = sb("var_eps", [P, TPB])
        rstd = sb("rstd", [P, TPB])
        qk = sb("qk", [P, 2, S])
        parts = [sb(f"parts{i}", [P, 2, 3, S], BF16) for i in range(2)]
        stack = [sb(f"stack{i}", [P, 2, H, S], BF16) for i in range(2)]
        scratch = [g.parts_dram[i] for i in range(2)]
        rot = sb("rot", [P, 4, S]) if rope else None
        vt = sb("vt", [P, TPB, H, DH])
        va = [sb(f"va{i}", [P, TPB, H, HP]) for i in range(2)]
        negm = sb("negm", [P, TPB, H])
        mparts = sb("mparts", [P, TPB, 2, H], BF16)
        mT = sb("mT", [2 * H, S], BF16)
        prob = sb("prob", [P, 8, KC])
        u = sb("u", [P, 4, S])
        rz = sb("rz", [P, TPB, H])
        on = sb("on", [P, TPB, H, DH])
        onT = sb("onT", [P, S])
        if full_mask is not None:
            mi = [sb(f"mi{k}", [P, 2, S], I32) for k in range(2)]
            mb = [[sb(f"mb{k}{i}", [P, 2, S], BF16) for i in range(2)] for k in range(2)]
        if key_mask is not None:
            kmi = sb("kmi", [1, B * S], I32)
            kmb = sb("kmb", [1, B * S], BF16)
        if alibi:
            flat, room = prob[:, :, :].rearrange("p a b -> p (a b)"), iter(range(0, 12 * S, S))
            two = lambda: flat[:, next(room):next(room) + S].rearrange("p (k s) -> p k s", k=2)
            one = lambda: flat[:, next(room):][:, 0:S].unsqueeze(1)
            dist, dist0, logd, dmask, altmp = two(), two(), two(), one(), one()
            logw = flat[:, 8 * S:12 * S].rearrange("p (h k s) -> p h k s", h=2, k=2)
            decay = sb("decay", [P, 2, H])
            al = sb("al", [P, 2, H, S], BF16)
            alw = sb("alw", [P, H, S])
        s1 = [ps(f"s1_{i}", [P, 512]) for i in range(2)]
        s2 = [ps(f"s2_{i}", [P, 512]) for i in range(2)]
        up = ps("up", [P, 4, S])
        pa = ps("pa", [P, 512])
        pb = ps("pb", [P, 512])
        mTp = pa[:, 0:S].bitcast(BF16)
        ut = up[:, :, :].rearrange("p (t a) (h c) -> p t (a h) c", t=TPB, c=HP)

        EV = 6 if rope else 2
        LATE = 9 if rope else 8
        ln_step = count("ln_step", 6)
        rstd_done = count("rstd_done")
        xnT_psum = count("xnT_psum")
        xnT_done = count("xnT_done")
        proj = count("proj", 3 if rope else 2)
        qk_done = count("qk_done", EV + 4)
        v_done = count("v_done")
        va_done = count("va_done")
        s1_done = count("s1_done", H)
        max_done = count("max_done", H)
        mparts_done = count("mparts_done", 2)
        mT_psum = count("mT_psum")
        mT_done = count("mT_done")
        s2_done = count("s2_done", H)
        exp_done = count("exp_done", H)
        av_done = count("av_done", 4)
        u_done = count("u_done", 2)
        ut_psum = count("ut_psum")
        on_step = count("on_step", 2)
        onT_psum = count("onT_psum")
        onT_done = count("onT_done")
        y_psum = count("y_psum")
        x_done = count("x_done")
        bo_done = count("bo_done")
        ctx_in, parts_out = ([nc.alloc_semaphore(f"{name}_{n}{i}") for i in range(2)] for n in ("ctx_in", "parts_out"))
        stack_in = [[nc.alloc_semaphore(f"{name}_stack_in{i}{j}") for j in range(2)] for i in range(2)]
        STACK_DMAS = 4 + (key_mask is not None)
        mask_in = [count(f"mask_in{k}", 16) for k in range(2)]
        mask_done = [count(f"mask_done{k}") for k in range(2)]
        setup = nc.alloc_semaphore(f"{name}_setup")
        setup_v = nc.alloc_semaphore(f"{name}_setup_v")
        setup_a = nc.alloc_semaphore(f"{name}_setup_a")
        setup_d = nc.alloc_semaphore(f"{name}_setup_d")
        POOL_HEADS = range(2, H, 3)
        w_done, wp_done = count("w_done", H - len(POOL_HEADS)), count("wp_done", len(POOL_HEADS))

        def weigh(e, done, b, h):
            e.wait_ge(exp_done.sem, exp_done.at(b, h + 1))
            e.tensor_tensor(prob[:, h % 8, 0:S], prob[:, h % 8, 0:S], alw[:, h, :], ALU.mult)
            e.tensor_tensor(prob[:, h % 8, S:KC], prob[:, h % 8, S:KC], alw[:, h, 0:P], ALU.mult).then_inc(done.sem, 1)

        block = ctx.enter_context(nc.Block())
        n_w = g.n_loads[name]
        SETUP = 4 + (key_mask is not None)

        def turns(e, first, body, last):
            first()
            body(0, 0, False, True, True)
            body(1, 1, True, True, True)
            with e.Fori(2, B - 3, 2) as b:
                body(b, 0, True, True, True)
                body(b + 1, 1, True, True, True)
            body(B - 2, 0, True, True, False)
            body(B - 1, 1, True, False, False)
            last()

        @block.sync
        def _(sp):
            if key_mask is not None:
                sp.dma_start(kmi[:, :], key_mask).then_inc(setup_d, 16)
            for dst, src, s in prefetch:
                sp.dma_start(dst, src).then_inc(s, 16)

            def context(b, i):
                sp.wait_ge(proj.sem, proj.at(b - 2))
                sp.dma_start(ctxT[:, i, :], g.ctxT_dram[:, b, :]).then_inc(ctx_in[i], 16)

            def load_mask(b, k):
                sp.wait_ge(mask_done[k].sem, mask_done[k].at(b - 1))
                sp.dma_start(mi[k][:, :, :], full_mask[k][b]).then_inc(mask_in[k].sem, 16)

            def stacks(b, i, more):
                sp.wait_ge(qk_done.sem, qk_done.at(b))
                for x in range(2):
                    for a in range(3):
                        sp.dma_start(scratch[i][x, a].rearrange("c h s -> h c s"), parts[i][:, x, a, :]).then_inc(parts_out[i], 16)
                if cross and more:
                    context(b + 2, i)
                sp.wait_ge(parts_out[i], 48 * (b - i) + 96)
                for j in range(2):
                    heads = slice(j * HH, (j + 1) * HH)
                    sp.wait_ge(s2_done.sem, s2_done.at(b - 2, (j + 1) * HH))
                    for a in range(3):
                        sp.dma_start(stack[i][a * 3 * DH:(a + 1) * 3 * DH, 0, heads, :].rearrange("r h s -> r (h s)"),
                                     scratch[i][0, a, :, heads, :].rearrange("c h s -> c (h s)").unsqueeze(0).to_broadcast([3, DH, HH * S])
                                     ).then_inc(stack_in[i][j], 16)
                    sp.dma_start(stack[i][0:KROWS, 1, heads, :].rearrange("r h s -> r (h s)"),
                                 scratch[i][1, :, :, heads, :].rearrange("a c h s -> (a c) (h s)").unsqueeze(0).to_broadcast([3, 3 * DH, HH * S])
                                 ).then_inc(stack_in[i][j], 16)
                    if key_mask is not None:
                        sp.dma_start(stack[i][MASK_ROW:MASK_ROW + 1, 1, heads, :],
                                     kmb[:, :].rearrange("p (b s) -> p b s", b=B)[:, b, :].unsqueeze(1).to_broadcast([1, HH, S])
                                     ).then_inc(stack_in[i][j], 16)
                if full_mask is not None:
                    if not (isinstance(b, int) and b + 1 == B):
                        load_mask(b + 1, 0)
                    load_mask(b, 1)

            start(sp, mask_in)
            if full_mask is not None:
                load_mask(0, 0)
            if cross:
                context(0, 0)
                context(1, 1)
            sp.wait_ge(setup, SETUP)
            if key_mask is not None:
                sp.wait_ge(setup_v, 1)
            stacks(0, 0, True)
            stacks(1, 1, True)
            with sp.Fori(2, B - 3, 2) as b:
                stacks(b, 0, True)
                stacks(b + 1, 1, True)
            stacks(B - 2, 0, False)
            stacks(B - 1, 1, False)

        @block.gpsimd
        def _(pool):
            start(pool, [rstd_done, va_done, bo_done, wp_done, *mask_done])
            for i in range(2):
                pool.memset(stack[i][:, :, :, :], 0.0).then_inc(setup, 1)
            if key_mask is not None:
                pool.wait_ge(setup, 2)
                for i in range(2):
                    m = pool.memset(stack[i][MASK_ROW:MASK_ROW + 1, 0, :, :], 1.0)
                m.then_inc(setup, 1)
                pool.wait_ge(setup, 3)
            for i in range(2):
                pool.memset(va[i][:, :, :, :], 0.0).then_inc(setup, 1)
            pool.wait_ge(setup, SETUP)
            for i in range(2):
                m = pool.memset(va[i][:, :, :, DH:2 * DH], 1.0)
            m.then_inc(setup, 1)
            pool.wait_ge(g.loaded[name], 16 * n_w)
            if alibi:
                pool.iota(dist[:, 0, :], pattern=[[-1, S]], base=P, channel_multiplier=1,
                          allow_small_or_imprecise_dtypes=True).then_inc(setup, 1)
                pool.iota(dist[:, 1, :], pattern=[[1, S]], base=0, channel_multiplier=-1,
                          allow_small_or_imprecise_dtypes=True).then_inc(setup, 1)

            def rstds(b):
                pool.wait_ge(ln_step.sem, ln_step.at(b, 5))
                pool.tensor_tensor(rstd[:, :], var_eps[:, :], g.half[:, 0:TPB], ALU.pow).then_inc(rstd_done.sem, 1)

            def mask(b, i, k):
                pool.wait_ge(mask_in[k].sem, mask_in[k].at(b))
                pool.sem_inc(g.spare, 1)
                done = (s1_done, s2_done)[k]
                pool.wait_ge(done.sem, done.at(b - 2))
                pool.sem_inc(g.spare, 1)
                pool.tensor_scalar(mb[k][i][:, :, :], mi[k][:, :, :], 0.0, -1e9, ALU.is_equal, ALU.mult).then_inc(mask_done[k].sem, 1)

            def values(b, i):
                pool.wait_ge(v_done.sem, v_done.at(b))
                pool.sem_inc(g.spare, 1)
                pool.wait_ge(av_done.sem, av_done.at(b - 2))
                pool.sem_inc(g.spare, 1)
                pool.tensor_copy(va[i][:, :, :, 0:DH], vt[:, :, :, :]).then_inc(va_done.sem, 1)

            def first():
                rstds(0)
                values(0, 0)
                rstds(1)
                values(1, 1)
                if full_mask is not None:
                    mask(0, 0, 0)
                    mask(1, 1, 0)
                    mask(0, 0, 1)

            def body(b, i, prev, more1, more2):
                if more2:
                    rstds(b + 2)
                if biased:
                    pool.tensor_tensor(g.x[:, b, :].rearrange("p (t d) -> p t d", t=TPB),
                                       g.x[:, b, :].rearrange("p (t d) -> p t d", t=TPB),
                                       w["bo"][:, :].unsqueeze(1).to_broadcast([P, TPB, D]),
                                       ALU.add).then_inc(bo_done.sem, 1)
                if full_mask is not None:
                    if more1:
                        mask(b + 1, 1 - i, 1)
                    if more2:
                        mask(b + 2, i, 0)
                if alibi:
                    for h in POOL_HEADS:
                        weigh(pool, wp_done, b, h)
                if more2:
                    values(b + 2, i)

            turns(pool, first, body, lambda: None)

        @block.vector
        def _(dve):
            start(dve, [ln_step, qk_done, v_done, max_done, mparts_done, mT_done, on_step, x_done, w_done])
            dve.wait_ge(g.loaded[name], 16 * n_w)
            if key_mask is not None:
                dve.wait_ge(setup_d, 16)
                dve.tensor_scalar(kmb[:, :], kmi[:, :], 0.0, NEG, ALU.is_equal, ALU.mult).then_inc(setup_v, 1)

            def distances():
                dve.wait_ge(setup_a, 3)
                dve.scalar_tensor_tensor(out=decay[:, 1, :], in0=w["decay"][:, :], scalar=0.0, in1=decay[:, 0, :],
                                         op0=ALU.max, op1=ALU.add).then_inc(setup_v, 1)
                dve.wait_ge(setup, SETUP + 3)
                dve.tensor_scalar(dist0[:, :, :], dist[:, :, :], 0.0, None, ALU.max).then_inc(setup_v, 1)
                dve.tensor_scalar(dmask[:, :, :], dist[:, 0:1, :], 0.0, NEG, ALU.is_lt, ALU.mult).then_inc(setup_v, 1)

            def position_bias(h):
                dve.wait_ge(setup_a, 5 + 2 * h + 1)
                if h >= 1:
                    dve.wait_ge(setup_v, 3 + 4 * h)
                dve.scalar_tensor_tensor(out=altmp[:, 0, :], in0=logw[:, h % 2, 0, :], scalar=-1.0, in1=dmask[:, 0, :],
                                         op0=ALU.mult, op1=ALU.add).then_inc(setup_v, 1)
                dve.wait_ge(setup_v, 3 + 4 * h + 1)
                dve.tensor_copy(al[:, 0, h, :], altmp[:, 0, :]).then_inc(setup_v, 1)
                dve.wait_ge(setup_v, 3 + 4 * h + 2)
                dve.tensor_tensor(al[:, 1, h, :], altmp[:, 0, :], al[:, 0, h, :], ALU.subtract).then_inc(setup_v, 1)
                dve.wait_ge(setup_a, 5 + 2 * h + 2)
                dve.reciprocal(alw[:, h, :], logw[:, h % 2, 1, :]).then_inc(setup_v, 1)

            def layer_norm(b):
                xb = lambda t: g.x[:, b, t * D:(t + 1) * D]
                for t in range(TPB):
                    dve.bn_stats(stats[:, t, :], xb(t)).then_inc(ln_step.sem, 1)
                dve.wait_ge(ln_step.sem, ln_step.at(b, 2))
                dve.sem_inc(g.spare, 1)
                for t in range(TPB):
                    dve.bn_aggr(mv[:, t, :], stats[:, t, :]).then_inc(ln_step.sem, 1)
                dve.wait_ge(ln_step.sem, ln_step.at(b, 4))
                dve.tensor_scalar(var_eps[:, :], mv[:, :, 1], LN_EPS, None, ALU.add).then_inc(ln_step.sem, 1)

            def normalised(b):
                xb = lambda t: g.x[:, b, t * D:(t + 1) * D]
                dve.wait_ge(rstd_done.sem, rstd_done.at(b))
                dve.wait_ge(xnT_psum.sem, xnT_psum.at(b - 1))
                for t in range(TPB):
                    m = dve.tensor_scalar(xn[:, t, :], xb(t), mv[:, t, 0:1], rstd[:, t:t + 1], ALU.subtract, ALU.mult)
                m.then_inc(ln_step.sem, 1)

            def projections(b, stage=0):
                if stage == 1:
                    rotated(b)
                    return
                dve.wait_ge(proj.sem, proj.at(b, 1))
                dve.wait_ge(qk_done.sem, qk_done.at(b - 1))
                if rope:
                    for k, (bias, table) in enumerate([(w["bq"], g.cosq), (w["bk"], g.cosk)]):
                        dve.scalar_tensor_tensor(out=rot[:, k, :], in0=pa[:, k * S:(k + 1) * S], scalar=bias[:, 0:1], in1=table[:, :],
                                                 op0=ALU.add, op1=ALU.mult).then_inc(qk_done.sem, 1)
                else:
                    bias = (w["bq"][:, 0:1], w["bk"][:, 0:1]) if biased else (0.0, 0.0)
                    dve.tensor_scalar(qk[:, 0, :], pa[:, 0:S], bias[0], scale, ALU.add, ALU.mult).then_inc(qk_done.sem, 1)
                    dve.tensor_scalar(qk[:, 1, :], pa[:, S:2 * S], bias[1], None, ALU.add).then_inc(qk_done.sem, 1)

            def rotated(b):
                if rope:
                    dve.wait_ge(proj.sem, proj.at(b, 2))
                    for k, (bias, table) in enumerate([(w["bqr"], g.sinq), (w["bkr"], g.sink)]):
                        dve.scalar_tensor_tensor(out=rot[:, 2 + k, :], in0=pa[:, k * S:(k + 1) * S], scalar=bias[:, 0:1], in1=table[:, :],
                                                 op0=ALU.add, op1=ALU.mult).then_inc(qk_done.sem, 1)
                    dve.wait_ge(qk_done.sem, qk_done.at(b, 4))
                    dve.tensor_tensor(qk[:, :, :], rot[:, 0:2, :], rot[:, 2:4, :], ALU.add).then_inc(qk_done.sem, 2)

            def projected_v(b):
                dve.wait_ge(proj.sem, proj.at(b))
                dve.wait_ge(va_done.sem, va_done.at(b - 1))
                v = pb[:, S:2 * S].rearrange("p (t h c) -> p t h c", t=TPB, h=H)
                if biased:
                    dve.tensor_tensor(vt[:, :, :, :], v, w["bv"][:, :].rearrange("p (h c) -> p h c", h=H).unsqueeze(1).to_broadcast([P, TPB, H, DH]),
                                      ALU.add).then_inc(v_done.sem, 1)
                else:
                    dve.tensor_scalar(vt[:, :, :, :], v, 1.0, None, ALU.mult).then_inc(v_done.sem, 1)

            def split(b, i, k):
                if k == 0:
                    dve.wait_ge(s1_done.sem, s1_done.at(b - 2))
                dve.wait_ge(qk_done.sem, qk_done.at(b, EV + k))
                p = parts[i]
                if k % 2 == 0:
                    m = dve.tensor_scalar(p[:, :, k // 2, :], qk[:, :, :], 1.0, None, ALU.mult)
                elif k == 1:
                    m = dve.tensor_tensor(qk[:, :, :], qk[:, :, :], p[:, :, 0, :], ALU.subtract)
                else:
                    m = dve.tensor_tensor(p[:, :, 2, :], qk[:, :, :], p[:, :, 1, :], ALU.subtract)
                m.then_inc(qk_done.sem, 1)

            def maximum(b, h):
                dve.wait_ge(s1_done.sem, s1_done.at(b, h + 1))
                if causal:
                    dve.tensor_reduce(negm[:, 0, h:h + 1], s1[h % 2][:, 0:P], AX.X, ALU.max, negate=True)
                    m = dve.tensor_reduce(negm[:, 1, h:h + 1], s1[h % 2][:, P:KC], AX.X, ALU.max, negate=True)
                else:
                    m = dve.tensor_reduce(negm[:, :, h], s1[h % 2][:, :].rearrange("p (t c) -> p t c", t=TPB),
                                          AX.X, ALU.max, negate=True)
                m.then_inc(max_done.sem, 1)

            def maxima_parts(b):
                dve.wait_ge(max_done.sem, max_done.at(b))
                dve.tensor_scalar(mparts[:, :, 0, :], negm[:, :, :], 1.0, None, ALU.mult).then_inc(mparts_done.sem, 1)
                dve.wait_ge(mparts_done.sem, mparts_done.at(b, 1))
                dve.tensor_tensor(mparts[:, :, 1, :], negm[:, :, :], mparts[:, :, 0, :], ALU.subtract).then_inc(mparts_done.sem, 1)

            def maxima_out(b):
                dve.wait_ge(mT_psum.sem, mT_psum.at(b))
                dve.tensor_scalar(mT[:, :], mTp[0:2 * H, 0:S], 1.0, None, ALU.mult).then_inc(mT_done.sem, 1)

            def outputs(b):
                dve.wait_ge(ut_psum.sem, ut_psum.at(b))
                dve.reciprocal(rz[:, :, :], ut[:, :, :, DH]).then_inc(on_step.sem, 1)
                dve.wait_ge(on_step.sem, on_step.at(b, 1))
                dve.tensor_tensor(on[:, :, :, :], ut[:, :, :, 0:DH], rz[:, :, :].unsqueeze(3).to_broadcast([P, TPB, H, DH]),
                                  ALU.mult).then_inc(on_step.sem, 1)

            def residual(b):
                if biased:
                    dve.wait_ge(bo_done.sem, bo_done.at(b))
                dve.wait_ge(y_psum.sem, y_psum.at(b))
                dve.tensor_tensor(g.x[:, b, :], g.x[:, b, :], pa[:, 0:S], ALU.add).then_inc(x_done.sem, 1)

            def first():
                for b in range(2):
                    layer_norm(b)
                    normalised(b)
                    projections(b)
                    projections(b, 1)
                    projected_v(b)
                    for k in range(4):
                        split(b, b, k)
                if alibi:
                    distances()
                for h in range(H):
                    if alibi:
                        position_bias(h)
                    maximum(0, h)
                maxima_parts(0)
                maxima_out(0)

            def body(b, i, prev, more1, more2):
                if more2:
                    layer_norm(b + 2)
                for h in range(H):
                    if more1:
                        maximum(b + 1, h)
                    if alibi and h not in POOL_HEADS:
                        weigh(dve, w_done, b, h)
                    if h == 0 and more2:
                        normalised(b + 2)
                    if h == 1 and prev:
                        outputs(b - 1)
                    if h == 5 and prev:
                        residual(b - 1)
                    if h == 7 and more2:
                        projections(b + 2)
                    if h == LATE and more2 and rope:
                        projections(b + 2, 1)
                    if LATE <= h < LATE + 4 and more2:
                        split(b + 2, i, h - LATE)
                    if h == LATE + 4 and more2:
                        projected_v(b + 2)
                if more1:
                    maxima_parts(b + 1)
                    maxima_out(b + 1)

            def last():
                outputs(B - 1)
                residual(B - 1)

            turns(dve, first, body, last)

        @block.scalar
        def _(act):
            start(act, [xnT_done, exp_done, u_done, onT_done])
            if alibi:
                act.wait_ge(g.loaded[name], 16 * n_w)
                act.activation(decay[:, 0, :], w["decay"][:, :], ACT.Abs).then_inc(setup_a, 1)
                act.wait_ge(setup_a, 1)
                act.activation(decay[:, 0, :], decay[:, 0, :], ACT.Exp, scale=-1.0).then_inc(setup_a, 1)
                act.wait_ge(setup_a, 2)
                act.activation(decay[:, 0, :], decay[:, 0, :], ACT.Ln, bias=1.0).then_inc(setup_a, 1)

            def position_bias():
                act.wait_ge(setup_v, 3)
                for k in range(2):
                    act.activation(logd[:, k, :], dist0[:, k, :], ACT.Ln, bias=1.0).then_inc(setup_a, 1)
                act.wait_ge(setup_a, 5)
                for h in range(H):
                    if h >= 2:
                        act.wait_ge(setup_v, 3 + 4 * (h - 1))
                    act.activation(logw[:, h % 2, 0, :], logd[:, 0, :], ACT.Ln, bias=1.0,
                                   scale=decay[:, 1, h:h + 1]).then_inc(setup_a, 1)
                    act.activation(logw[:, h % 2, 1, :], logd[:, 1, :], ACT.Identity, bias=1.0,
                                   scale=decay[:, 1, h:h + 1]).then_inc(setup_a, 1)

            def transposed(b):
                act.wait_ge(xnT_psum.sem, xnT_psum.at(b))
                act.activation(xnT[:, :], pb[:, 0:S], ACT.Copy).then_inc(xnT_done.sem, 1)

            def sums(b, q):
                act.wait_ge(av_done.sem, av_done.at(b, 2 * q + 2))
                act.activation(u[:, 2 * q:2 * q + 2, :], up[:, 2 * q:2 * q + 2, :], ACT.Copy).then_inc(u_done.sem, 1)

            def outputs(b):
                act.wait_ge(onT_psum.sem, onT_psum.at(b))
                act.activation(onT[:, :], pb[:, 0:S], ACT.Copy).then_inc(onT_done.sem, 1)

            def first():
                transposed(0)
                transposed(1)
                if alibi:
                    position_bias()

            def body(b, i, prev, more1, more2):
                if prev:
                    sums(b - 1, 1)
                for h in range(H):
                    act.wait_ge(s2_done.sem, s2_done.at(b, h + 1))
                    if h % 4 == 0:
                        act.wait_ge(av_done.sem, av_done.at(b, h // 4 - 1))
                    act.activation(prob[:, h % 8, :], s2[h % 2][:, 0:KC], ACT.Exp).then_inc(exp_done.sem, 1)
                    if h == 2 and prev:
                        outputs(b - 1)
                    if h == 4 and more2:
                        transposed(b + 2)
                    if h == 13:
                        sums(b, 0)

            def last():
                sums(B - 1, 1)
                outputs(B - 1)

            turns(act, first, body, last)

        @block.tensor
        def _(pe):
            start(pe, [xnT_psum, proj, s1_done, mT_psum, s2_done, av_done, ut_psum, onT_psum, y_psum])
            pe.wait_ge(g.loaded[name], 16 * n_w)

            def transposes(b):
                pe.wait_ge(ln_step.sem, ln_step.at(b))
                pe.wait_ge(v_done.sem, v_done.at(b - 1))
                pe.wait_ge(onT_done.sem, onT_done.at(b - 3))
                pe.wait_ge(xnT_done.sem, xnT_done.at(b - 1))
                for t in range(TPB):
                    m = pe.transpose(pb[:, t * P:(t + 1) * P], xn[:, t, :], g.ident[:, :])
                m.then_inc(xnT_psum.sem, 1)

            def projections(b, i, stage=0):
                kv = ctxT[:, i, :] if cross else xnT[:, :]
                if stage == 1:
                    if rope:
                        pe.wait_ge(qk_done.sem, qk_done.at(b, 2))
                        pe.matmul(pa[:, 0:S], w["wqr"][:, :], xnT[:, :], start=True, stop=True)
                        pe.matmul(pa[:, S:2 * S], w["wkr"][:, :], kv, start=True, stop=True).then_inc(proj.sem, 1)
                    for t in range(TPB):
                        m = pe.matmul(pb[:, S + t * P:S + (t + 1) * P], kv[:, t * P:(t + 1) * P], w["wv"][:, :], start=True, stop=True)
                    m.then_inc(proj.sem, 1)
                    return
                pe.wait_ge(xnT_done.sem, xnT_done.at(b))
                if cross:
                    pe.wait_ge(ctx_in[i], 8 * (b - i) + 16)
                pe.wait_ge(v_done.sem, v_done.at(b - 1))
                pe.wait_ge(mT_done.sem, mT_done.at(b - 2))
                pe.wait_ge(x_done.sem, x_done.at(b - 3))
                pe.matmul(pa[:, 0:S], w["wq"][:, :], xnT[:, :], start=True, stop=True)
                pe.matmul(pa[:, S:2 * S], w["wk"][:, :], kv, start=True, stop=True).then_inc(proj.sem, 1)

            def add(out, lhsT, rhs, last=False):
                return pe.matmul(out, lhsT, rhs, start=False, stop=last)

            def scores_q(b, i, h):
                if h % HH == 0:
                    pe.wait_ge(stack_in[i][h // HH], 16 * STACK_DMAS // 2 * (b - i) + 16 * STACK_DMAS)
                if h == 0 and full_mask is not None:
                    pe.wait_ge(mask_done[0].sem, mask_done[0].at(b))
                pe.wait_ge(max_done.sem, max_done.at(b, h - 1))
                bank = s1[h % 2]
                plain = not (causal or full_mask is not None)
                for t in range(TPB):
                    c0, n = (t * S, S) if not causal else (t * P, (t + 1) * P)
                    out = bank[:, c0:c0 + n]
                    m = pe.matmul(out, stack[i][:, 0, h, t * P:(t + 1) * P], stack[i][:, 1, h, 0:n], start=True, stop=plain)
                    if alibi:
                        add(out, g.ident_bf[:, :], al[:, 0, h, S - n:S])
                        m = add(out, g.ident_bf[:, :], al[:, 1, h, S - n:S], last=True)
                    elif window is not None:
                        m = add(out, g.ident_bf[:, :], g.band_q[:, S - n:S], last=True)
                    elif causal:
                        m = add(out[:, n - P:n], g.ident_bf[:, :], g.tri_q[:, :], last=True)
                    elif full_mask is not None:
                        m = add(out, g.ident_bf[:, :], mb[0][i][:, t, :], last=True)
                m.then_inc(s1_done.sem, 1)

            def maxima(b):
                pe.wait_ge(mparts_done.sem, mparts_done.at(b))
                pe.wait_ge(v_done.sem, v_done.at(min(b + 1, B - 1) if isinstance(b, int) else b + 1))
                pe.wait_ge(x_done.sem, x_done.at(b - 2))
                for t in range(TPB):
                    m = pe.transpose(mTp[0:2 * H, t * P:(t + 1) * P], mparts[:, t, :, :].rearrange("p a h -> p (a h)"), g.ident_bf[:, :])
                m.then_inc(mT_psum.sem, 1)

            def scores_k(b, i, h):
                if h == 0 and full_mask is not None:
                    pe.wait_ge(mask_done[1].sem, mask_done[1].at(b))
                pe.wait_ge(exp_done.sem, exp_done.at(b, h - 1))
                bank = s2[h % 2]
                plain = not (causal or full_mask is not None)
                for t in range(TPB):
                    c0, q0 = (t * S, 0 if not causal else t * P)
                    n = S - q0
                    out = bank[:, c0:c0 + n]
                    pe.matmul(out, stack[i][:, 1, h, t * P:(t + 1) * P], stack[i][:, 0, h, q0:S], start=True, stop=False)
                    m = add(out, g.sel[:, h, :], mT[:, q0:S], last=plain)
                    if window is not None:
                        m = add(out, g.ident_bf[:, :], g.band_k[:, 0:n], last=True)
                    elif causal:
                        m = add(out[:, 0:P], g.ident_bf[:, :], g.tri_k[:, :], last=True)
                    elif full_mask is not None:
                        m = add(out, g.ident_bf[:, :], mb[1][i][:, t, :], last=True)
                m.then_inc(s2_done.sem, 1)

            def values(b, i, q):
                if q == 0:
                    pe.wait_ge(va_done.sem, va_done.at(b))
                    pe.wait_ge(on_step.sem, on_step.at(b - 1))
                if alibi:
                    pool_heads = len([h for h in POOL_HEADS if h < 4 * q + 4])
                    pe.wait_ge(w_done.sem, w_done.at(b, 4 * q + 4 - pool_heads))
                    pe.wait_ge(wp_done.sem, wp_done.at(b, pool_heads))
                else:
                    pe.wait_ge(exp_done.sem, exp_done.at(b, 4 * q + 4))
                spans = [(0, 0, S, 0, True, False), (1, 0, S, S, False, True)] if not causal else [
                    (0, 0, P, 0, True, True), (0, P, P, P, True, False), (1, P, P, S, False, True)]
                for kt, q0, n, p0, first, last in spans:
                    for j in range(4):
                        h = 4 * q + j
                        m = pe.matmul(up[HP * j:HP * (j + 1), q, q0:q0 + n], va[i][:, kt, h, :], prob[:, h % 8, p0:p0 + n],
                                      start=first, stop=last, tile_position=(0, HP * j))
                m.then_inc(av_done.sem, 1)

            def tail_transposes(b):
                pe.wait_ge(u_done.sem, u_done.at(b))
                for t in range(TPB):
                    for q in range(4):
                        m = pe.transpose(up[:, 2 * t + q // 2, (q % 2) * P:(q % 2 + 1) * P], u[:, q, t * P:(t + 1) * P], g.ident[:, :])
                m.then_inc(ut_psum.sem, 1)

            def tail_outputs(b):
                pe.wait_ge(on_step.sem, on_step.at(b))
                for t in range(TPB):
                    m = pe.transpose(pb[:, t * P:(t + 1) * P], on[:, t, :, :].rearrange("p h c -> p (h c)"), g.ident[:, :])
                m.then_inc(onT_psum.sem, 1)

            def tail_projection(b):
                pe.wait_ge(onT_done.sem, onT_done.at(b))
                for t in range(TPB):
                    m = pe.matmul(pa[:, t * P:(t + 1) * P], onT[:, t * P:(t + 1) * P], w["wo"][:, :], start=True, stop=True)
                m.then_inc(y_psum.sem, 1)

            def first():
                for b in range(2):
                    transposes(b)
                    projections(b, b)
                    projections(b, b, 1)
                pe.wait_ge(setup, SETUP + 1)
                for h in range(H):
                    if alibi:
                        pe.wait_ge(setup_v, 3 + 4 * (h + 1))
                    scores_q(0, 0, h)
                maxima(0)

            def body(b, i, prev, more1, more2):
                pe.wait_ge(mT_done.sem, mT_done.at(b))
                for h in range(H):
                    scores_k(b, i, h)
                    if more1:
                        scores_q(b + 1, 1 - i, h)
                    if prev:
                        if h == 0:
                            tail_transposes(b - 1)
                        if h == 2:
                            tail_outputs(b - 1)
                        if h == 4:
                            tail_projection(b - 1)
                    if more2:
                        if h == 3:
                            transposes(b + 2)
                        if h == 6:
                            projections(b + 2, i)
                        if h == 8:
                            projections(b + 2, i, 1)
                    if h in (5, 9, 13):
                        values(b, i, (h - 5) // 4)
                values(b, i, 3)
                if more1:
                    maxima(b + 1)

            def last():
                tail_transposes(B - 1)
                tail_outputs(B - 1)
                tail_projection(B - 1)

            turns(pe, first, body, last)


C_TOK = 4 * P
NC = B * S // C_TOK
TPC = C_TOK // P
CAPACITY = 2 * B * S // E
CHOSEN = 128


def experts(nc, g, name, w, hidden, act_fn, glu, routing, biased=False, prefetch=()):
    F = hidden // P
    NE = NT * E
    with ExitStack() as ctx:
        sb = lambda n, shape, dt=F32: ctx.enter_context(nc.sbuf_tensor(f"{name}_{n}", shape, dt))
        ps = lambda n, shape, dt=F32: ctx.enter_context(nc.psum_tensor(f"{name}_{n}", shape, dt))
        count = lambda n, per=1: Count(nc, f"{name}_{n}", per)
        sem = lambda n: nc.alloc_semaphore(f"{name}_{n}")
        xn = sb("xn", [P, TPC, D])
        xnT = sb("xnT", [P, NC, C_TOK])
        xnTs = sb("xnTs", [P, C_TOK])
        stats = sb("stats", [P, TPC, 6])
        mv = sb("mv", [P, TPC, 2])
        var_eps = sb("var_eps", [P, TPC])
        rstd = sb("rstd", [P, TPC])
        logits = sb("logits", [P, NC, TPC * E])
        lg = logits[:, :, :].rearrange("p c (t e) -> p (c t) e", e=E)
        gate = sb("gate", [P, NT, E])
        h = [sb(f"h{i}", [P, F, C_TOK]) for i in range(2)]
        hg = [sb(f"hg{i}", [P, F, C_TOK]) for i in range(2)] if glu else None
        t1, t2, t3 = (sb(n, [P, NT, E]) for n in ("t1", "t2", "t3"))
        mask = sb("mask", [P, 2, NT, E])
        best = sb("best", [P, 3, NT])
        wt = sb("wt", [P, 2, NT])
        ub = [ps(f"ub{i}", [P, C_TOK]) for i in range(4)]
        yb = [ps(f"yb{i}", [P, C_TOK]) for i in range(2)]
        tp = ps("tp", [P, C_TOK])
        lp = ps("lp", [P, C_TOK])

        ln_step = count("ln_step", 2 * TPC + 2)
        rstd_done = count("rstd_done")
        xnT_psum = count("xnT_psum")
        xnT_done = count("xnT_done")
        xnTs_done = count("xnTs_done")
        logit_psum = count("logit_psum")
        logit_done = count("logit_done")
        rv, ra, rp, rg, rdy = (sem(n) for n in ("route_dve", "route_act", "route_pe", "route_pool", "route_ready"))
        ups = 2 * F if glu else F
        up_done = count("up_done", ups * E)
        act_done = count("act_done", F * E)
        h_done = count("h_done", F * E)
        y_done = count("y_done", E)
        acc_done = count("acc_done", TPC * E)
        if routing == "capacity":
            tri = sb("tri", [P, P], BF16)
            mask_bf = sb("mask_bf", [P, 2 * NE], BF16)
            scan = [sb(f"scan{i}", [P, 2 * NT, E]) for i in range(2)]
            tot = sb("tot", [P, 2 * NT, E])
            loc = sb("loc", [P, 2 * NT, E])
        if routing == "choice":
            affT, left = sb("affT", [B * E, S]), sb("left", [B * E, S])
            top8 = sb("top8", [B * E, 8])
            aff = sb("aff", [P, TPB, B, E])
        if biased:
            gT = sb("gT", [NE, P])
            bm = sb("bm", [NE, NT, D])
        block = ctx.enter_context(nc.Block())

        @block.sync
        def _(sp):
            for dst, src, s in prefetch:
                sp.dma_start(dst, src).then_inc(s, 16)

        @block.gpsimd
        def _(pool):
            start(pool, [rstd_done])
            if routing == "capacity":
                pool.memset(tri[:, :], 1.0).then_inc(rg, 1)
                pool.wait_ge(rg, 1)
                pool.affine_select(out=tri[:, :], in_=tri[:, :], compare_op=ALU.is_gt, fill=0.0,
                                   base=0, pattern=[[1, P]], channel_multiplier=-1).then_inc(rg, 1)
            with pool.Fori(0, NC) as c:
                pool.wait_ge(ln_step.sem, ln_step.at(c, 2 * TPC + 1))
                pool.tensor_tensor(rstd[:, :], var_eps[:, :], g.half[:, 0:TPC], ALU.pow).then_inc(rstd_done.sem, 1)

        @block.vector
        def _(dve):
            start(dve, [ln_step, xnTs_done, logit_done, h_done, acc_done])
            dve.wait_ge(g.loaded[name], 16 * g.n_loads[name])
            xt = g.x[:, :, :].rearrange("p b (t d) -> p (b t) d", t=TPB).rearrange("p (c t) d -> p c t d", c=NC)
            with dve.Fori(0, NC) as c:
                for t in range(TPC):
                    dve.bn_stats(stats[:, t, :], xt[:, c, t, :]).then_inc(ln_step.sem, 1)
                dve.wait_ge(ln_step.sem, ln_step.at(c, TPC))
                dve.sem_inc(g.spare, 1)
                for t in range(TPC):
                    dve.bn_aggr(mv[:, t, :], stats[:, t, :]).then_inc(ln_step.sem, 1)
                dve.wait_ge(ln_step.sem, ln_step.at(c, 2 * TPC))
                dve.tensor_scalar(var_eps[:, :], mv[:, :, 1], LN_EPS, None, ALU.add).then_inc(ln_step.sem, 1)
                dve.wait_ge(rstd_done.sem, rstd_done.at(c))
                dve.wait_ge(xnT_psum.sem, xnT_psum.at(c - 1))
                for t in range(TPC):
                    m = dve.tensor_scalar(xn[:, t, :], xt[:, c, t, :], mv[:, t, 0:1], rstd[:, t:t + 1], ALU.subtract, ALU.mult)
                m.then_inc(ln_step.sem, 1)
                dve.wait_ge(xnT_psum.sem, xnT_psum.at(c))
                dve.wait_ge(logit_psum.sem, logit_psum.at(c - 1))
                dve.wait_ge(xnT_done.sem, xnT_done.at(c))
                dve.tensor_scalar(xnTs[:, :], tp[:, :], 1.0, None, ALU.mult).then_inc(xnTs_done.sem, 1)
                dve.wait_ge(logit_psum.sem, logit_psum.at(c))
                dve.tensor_scalar(logits[:, c, :], lp[:, 0:TPC * E], 1.0, None, ALU.mult).then_inc(logit_done.sem, 1)

            n = 0

            def step(m):
                nonlocal n
                m.then_inc(rv, 1)
                n += 1
                dve.wait_ge(rv, n)

            over_e = lambda a: a.unsqueeze(2).to_broadcast([P, NT, E])

            def first_max(values, k, m):
                step(dve.tensor_reduce(best[:, k, :], values, AX.X, ALU.max))
                step(dve.tensor_tensor(t1[:, :, :], values, over_e(best[:, k, :]), ALU.is_equal))
                step(dve.tensor_tensor(t1[:, :, :], t1[:, :, :], g.back_e[:, :].unsqueeze(1).to_broadcast([P, NT, E]), ALU.mult))
                step(dve.tensor_reduce(best[:, 2, :], t1[:, :, :], AX.X, ALU.max))
                step(dve.tensor_tensor(m, t1[:, :, :], over_e(best[:, 2, :]), ALU.is_equal))

            dve.wait_ge(logit_done.sem, logit_done.at(NC - 1))
            if routing != "choice":
                first_max(lg, 0, mask[:, 0, :, :])
                step(dve.scalar_tensor_tensor(out=t2[:, :, :], in0=mask[:, 0, :, :], scalar=-3e38, in1=lg, op0=ALU.mult, op1=ALU.add))
                first_max(t2[:, :, :], 1, mask[:, 1, :, :])
                step(dve.tensor_tensor(wt[:, 1, :], best[:, 1, :], best[:, 0, :], ALU.subtract))
            if routing in ("choice", "probs"):
                if routing == "choice":
                    step(dve.tensor_reduce(best[:, 0, :], lg, AX.X, ALU.max))
                step(dve.tensor_tensor(t3[:, :, :], lg, over_e(best[:, 0, :]), ALU.subtract))
            dve.sem_inc(rdy, 1)
            dve.wait_ge(ra, 1)
            if routing in ("choice", "probs"):
                step(dve.reduce_sum(best[:, 2, :], t3[:, :, :], axis=AX.X))
            elif routing in ("pair", "capacity"):
                step(dve.tensor_scalar(best[:, 2, :], wt[:, 1, :], 1.0, None, ALU.add))
            step(dve.reciprocal(wt[:, 0, :], best[:, 2, :]))
            if routing == "choice":
                step(dve.tensor_tensor(aff[:, :, :, :].rearrange("p t b e -> p b t e"), t3[:, :, :].rearrange("p (b t) e -> p b t e", t=TPB),
                                       wt[:, 0, :].rearrange("p (b t) -> p b t", t=TPB).unsqueeze(3).to_broadcast([P, B, TPB, E]), ALU.mult))
                dve.sem_inc(rdy, 1)
                dve.wait_ge(rp, 1)
                step(dve.tensor_scalar(affT[:, :], tp[0:B * E, 0:S], 1.0, None, ALU.mult))
                step(dve.tensor_scalar(left[:, :], affT[:, :], 1.0, None, ALU.mult))
                for _ in range(CHOSEN // 8):
                    step(dve.max(top8[:, :], left[:, :]))
                    step(dve.match_replace(left[:, :], top8[:, :], left[:, :], -1.0))
                step(dve.scalar_tensor_tensor(out=affT[:, :], in0=left[:, :], scalar=-1.0, in1=affT[:, :], op0=ALU.is_equal, op1=ALU.mult))
                dve.sem_inc(rdy, 1)
                dve.wait_ge(rp, 2)
                step(dve.tensor_scalar(gate[:, :, :].rearrange("p (b t) e -> p t b e", t=TPB),
                                       lp[:, 0:NE].rearrange("p (t b e) -> p t b e", t=TPB, b=B), 1.0, None, ALU.mult))
            else:
                step(dve.tensor_tensor(wt[:, 1, :], wt[:, 1, :], wt[:, 0, :], ALU.mult))
                if routing == "capacity":
                    m2 = mask[:, :, :, :].rearrange("p k t e -> p (k t) e")
                    step(dve.tensor_scalar(mask_bf[:, :], mask[:, :, :, :].rearrange("p k t e -> p (k t e)"), 1.0, None, ALU.mult))
                    dve.sem_inc(rdy, 1)
                    dve.wait_ge(rp, 1)
                    step(dve.tensor_scalar(tot[:, :, :], lp[:, 0:2 * NE].rearrange("p (t e) -> p t e", e=E), 1.0, None, ALU.mult))
                    step(dve.tensor_scalar(scan[0][:, :, :], tot[:, :, :], 1.0, None, ALU.mult))
                    k, d = 0, 1
                    while d < 2 * NT:
                        step(dve.tensor_scalar(scan[1 - k][:, 0:d, :], scan[k][:, 0:d, :], 1.0, None, ALU.mult))
                        step(dve.tensor_tensor(scan[1 - k][:, d:2 * NT, :], scan[k][:, d:2 * NT, :], scan[k][:, 0:2 * NT - d, :], ALU.add))
                        k, d = 1 - k, 2 * d
                    step(dve.tensor_tensor(loc[:, :, :], scan[k][:, :, :], tot[:, :, :], ALU.subtract))
                    step(dve.tensor_tensor(loc[:, :, :], tp[:, 0:2 * NE].rearrange("p (t e) -> p t e", e=E), loc[:, :, :], ALU.add))
                    step(dve.scalar_tensor_tensor(out=m2, in0=loc[:, :, :], scalar=float(CAPACITY), in1=m2, op0=ALU.is_lt, op1=ALU.mult))
                step(dve.tensor_tensor(t1[:, :, :], mask[:, 0, :, :], over_e(wt[:, 0, :]), ALU.mult))
                step(dve.tensor_tensor(t2[:, :, :], mask[:, 1, :, :], over_e(wt[:, 1, :]), ALU.mult))
                step(dve.tensor_tensor(gate[:, :, :], t1[:, :, :], t2[:, :, :], ALU.add))
            if biased:
                dve.sem_inc(rdy, 1)
                for t in range(NT):
                    m = dve.tensor_scalar(bm[:, t, :], w["b_out"][:, :], g.rowmask[:, t:t + 1], None, ALU.mult)
                step(m)
                dve.wait_ge(rp, 1)
                step(dve.tensor_scalar(gT[:, :], tp[:, 0:P], 1.0, None, ALU.mult))
                dve.sem_inc(rdy, 1)
                dve.wait_ge(rp, 2)
                for c in range(NC):
                    m = dve.tensor_tensor(g.x[:, 2 * c:2 * c + 2, :], g.x[:, 2 * c:2 * c + 2, :],
                                          ub[c][:, :].rearrange("p (b n) -> p b n", b=2), ALU.add)
                step(m)
            dve.sem_inc(rdy, 1)

            gt = gate[:, :, :].rearrange("p (c t) e -> p c t e", c=NC)
            with dve.Fori(0, NC) as c:
                def products(e):
                    for f in range(F):
                        dve.wait_ge(act_done.sem, act_done.at(c, e * F + f + 1))
                        dve.wait_ge(up_done.sem, up_done.at(c, 2 * (e * F + f) + 2))
                        dve.wait_ge(y_done.sem, y_done.at(c, e - 1))
                        dve.tensor_tensor(h[e % 2][:, f, :], hg[e % 2][:, f, :], ub[(2 * (e * F + f) + 1) % 4][:, :],
                                          ALU.mult).then_inc(h_done.sem, 1)

                def accumulate(e):
                    dve.wait_ge(y_done.sem, y_done.at(c, e + 1))
                    dve.wait_ge(acc_done.sem, acc_done.at(c, TPC * e))
                    for t in range(TPC):
                        dve.scalar_tensor_tensor(out=xt[:, c, t, :], in0=yb[e % 2][:, t * P:(t + 1) * P], scalar=gt[:, c, t, e:e + 1],
                                                 in1=xt[:, c, t, :], op0=ALU.mult, op1=ALU.add).then_inc(acc_done.sem, 1)

                if glu:
                    products(0)
                for e in range(E):
                    if glu and e + 1 < E:
                        products(e + 1)
                    accumulate(e)

        @block.scalar
        def _(act):
            start(act, [xnT_done, act_done])
            act.wait_ge(g.loaded[name], 16 * g.n_loads[name])
            with act.Fori(0, NC) as c:
                act.wait_ge(xnT_psum.sem, xnT_psum.at(c))
                act.sem_inc(g.spare, 1)
                act.activation(xnT[:, c, :], tp[:, :], ACT.Copy).then_inc(xnT_done.sem, 1)
            act.wait_ge(rdy, 1)
            if routing in ("choice", "probs"):
                m = act.activation(t3[:, :, :], t3[:, :, :], ACT.Exp)
            if routing != "choice":
                m = act.activation(wt[:, 1, :], wt[:, 1, :], ACT.Exp)
            m.then_inc(ra, 1)
            with act.Fori(0, NC) as c:
                for e in range(E):
                    for f in range(F):
                        k = e * F + f
                        b = 2 * k if glu else k
                        act.wait_ge(up_done.sem, up_done.at(c, (2 * k + 2) if glu else k + 1))
                        if glu:
                            act.wait_ge(h_done.sem, h_done.at(c, (e - 1) * F))
                            act.activation(hg[e % 2][:, f, :], ub[b % 4][:, :], act_fn).then_inc(act_done.sem, 1)
                        else:
                            act.wait_ge(y_done.sem, y_done.at(c, e - 1))
                            bias = w["b_in"][:, e:e + 1] if biased else 0.0
                            act.activation(h[e % 2][:, f, :], ub[b % 4][:, :], act_fn, bias=bias).then_inc(act_done.sem, 1)

        @block.tensor
        def _(pe):
            start(pe, [xnT_psum, logit_psum, up_done, y_done])
            pe.wait_ge(g.loaded[name], 16 * g.n_loads[name])
            with pe.Fori(0, NC) as c:
                pe.wait_ge(ln_step.sem, ln_step.at(c))
                pe.wait_ge(xnTs_done.sem, xnTs_done.at(c - 1))
                pe.wait_ge(xnT_done.sem, xnT_done.at(c - 1))
                for t in range(TPC):
                    m = pe.transpose(tp[:, t * P:(t + 1) * P], xn[:, t, :], g.ident[:, :])
                m.then_inc(xnT_psum.sem, 1)
                pe.wait_ge(xnTs_done.sem, xnTs_done.at(c))
                pe.wait_ge(logit_done.sem, logit_done.at(c - 1))
                for t in range(TPC):
                    m = pe.matmul(lp[:, t * E:(t + 1) * E], xnTs[:, t * P:(t + 1) * P], w["router"][:, :], start=True, stop=True)
                m.then_inc(logit_psum.sem, 1)
            if routing == "capacity":
                pe.wait_ge(rdy, 2)
                pe.wait_ge(rg, 2)
                pe.matmul(tp[:, 0:2 * NE], tri[:, :], mask_bf[:, :], start=True, stop=True)
                pe.matmul(lp[:, 0:2 * NE], g.ones_bf[:, 0:P], mask_bf[:, :], start=True, stop=True).then_inc(rp, 1)
            if routing == "choice":
                pe.wait_ge(rdy, 2)
                for t in range(TPB):
                    m = pe.transpose(tp[0:B * E, t * P:(t + 1) * P], aff[:, t, :, :].rearrange("p b e -> p (b e)"), g.ident[:, :])
                m.then_inc(rp, 1)
                pe.wait_ge(rdy, 3)
                for t in range(TPB):
                    m = pe.transpose(lp[:, t * B * E:(t + 1) * B * E], affT[:, t * P:(t + 1) * P], g.ident[0:B * E, 0:B * E])
                m.then_inc(rp, 1)
            if biased:
                pe.wait_ge(rdy, 2)
                pe.transpose(tp[:, 0:P], gate[:, :, :].rearrange("p t e -> p (t e)"), g.ident[:, :]).then_inc(rp, 1)
                pe.wait_ge(rdy, 3)
                for t in range(NT):
                    m = pe.matmul(ub[t // TPC][:, t % TPC * P:(t % TPC + 1) * P], gT[:, :], bm[:, t, :], start=True, stop=True)
                m.then_inc(rp, 1)
                pe.wait_ge(rdy, 4)
            n_up = len(w["up"])

            with pe.Fori(0, NC) as c:
                def up(e):
                    for f in range(F):
                        for j in range(n_up):
                            k = (e * F + f) * n_up + j
                            if glu:
                                pe.wait_ge(h_done.sem, h_done.at(c, e * F + f - 1))
                            else:
                                pe.wait_ge(act_done.sem, act_done.at(c, k - 3))
                            pe.matmul(ub[k % 4][:, :], w["up"][j][:, e, f * P:(f + 1) * P], xnT[:, c, :], start=True,
                                      stop=True).then_inc(up_done.sem, 1)

                def down(e):
                    done = h_done if glu else act_done
                    pe.wait_ge(done.sem, done.at(c, (e + 1) * F))
                    pe.wait_ge(acc_done.sem, acc_done.at(c, TPC * (e - 1)))
                    for t in range(TPC):
                        for f in range(F):
                            m = pe.matmul(yb[e % 2][:, t * P:(t + 1) * P], h[e % 2][:, f, t * P:(t + 1) * P],
                                          w["down"][:, e, f, :], start=f == 0, stop=f == F - 1)
                    m.then_inc(y_done.sem, 1)

                up(0)
                for e in range(E):
                    if e + 1 < E:
                        up(e + 1)
                    down(e)


GH, GK, GV = 4, 32, 64
GV_ALL = GH * GV
LOW = 16
GATE_NORM = 16.0
RMS_EPS = 1e-5


def gated_linear(nc, g, name, w):
    MID = P // 2 - 1
    BPC = C_TOK // S
    with ExitStack() as ctx:
        sb = lambda n, shape, dt=F32: ctx.enter_context(nc.sbuf_tensor(f"{name}_{n}", shape, dt))
        ps = lambda n, shape, dt=F32: ctx.enter_context(nc.psum_tensor(f"{name}_{n}", shape, dt))
        count = lambda n, per=1: Count(nc, f"{name}_{n}", per)
        xn = sb("xn", [P, TPC, D])
        stats = sb("stats", [P, TPC, 6])
        mv = sb("mv", [P, TPC, 2])
        var_eps = sb("var_eps", [P, TPC])
        rstd = sb("rstd", [P, TPC])
        xnT = sb("xnT", [P, C_TOK])
        z = sb("z", [LOW, C_TOK])
        gl, fa, lg, gsum, gmid = (sb(n, [P, C_TOK]) for n in ("gl", "fa", "lg", "gsum", "gmid"))
        restart = sb("restart", [P, C_TOK])
        eq, ek, qt, kt = (sb(n, [P, C_TOK]) for n in ("eq", "ek", "qt", "kt"))
        v = sb("v", [P, TPC, GV_ALL])
        silu = sb("silu", [P, TPC, GV_ALL])
        ktok = sb("ktok", [P, BPC, P])
        fac = sb("fac", [P, BPC])
        own = sb("own", [P, GH, GV])
        tri = sb("tri", [P, P])
        state = sb("state", [P, BPC, GV_ALL])
        am = sb("am", [P, GH, TPC, P])
        sq, on = sb("sq", [P, TPC, GV_ALL]), sb("on", [P, TPC, GV_ALL])
        ss, ms, rr = (sb(n, [P, TPC * GH]) for n in ("ss", "ms", "rr"))
        onT = sb("onT", [P, 2, C_TOK])
        bank = [ps(f"bank{i}", [P, C_TOK]) for i in range(8)]

        ln_step = count("ln_step", 2 * TPC + 2)
        rstd_done = count("rstd_done")
        xnT_psum = count("xnT_psum")
        xnT_done = count("xnT_done")
        z_psum, z_done = count("z_psum"), count("z_done")
        qk_psum = count("qk_psum")
        v_psum, v_done = count("v_psum", 2), count("v_done", 2)
        gl_psum = count("gl_psum")
        gate = count("gate", 6)
        fa_step = count("fa_step", 3)
        e_done = count("e_done", 3)
        qk_done = count("qk_done", 2)
        o_gate_psum = count("o_gate_psum", 2)
        silu_done = count("silu_done", 2)
        silu_w = count("silu_w")
        k_psum, k_done = count("k_psum"), count("k_done")
        kv_psum, state_done = count("kv_psum"), count("state_done", BPC)
        a_psum, a_done = count("a_psum", GH), count("a_done", GH)
        o_psum = count("o_psum", 2)
        sq_done = count("sq_done", 2)
        norm = count("norm", 4)
        on_done = count("on_done")
        rr_done = count("rr_done")
        onT_psum = count("onT_psum", 2)
        onT_done = count("onT_done", 2)
        y_psum, x_done = count("y_psum"), count("x_done")
        made = nc.alloc_semaphore(f"{name}_made")
        block = ctx.enter_context(nc.Block())
        loaded, n_w = g.loaded[name], 16 * g.n_loads[name]
        tiles = lambda a: a.rearrange("p (t n) -> p t n", n=P)

        @block.gpsimd
        def _(pool):
            start(pool, [rstd_done, silu_w, rr_done])
            pool.memset(restart[:, :], 1.0).then_inc(made, 1)
            pool.memset(own[:, :, :], 1.0).then_inc(made, 1)
            pool.memset(tri[:, :], 1.0).then_inc(made, 1)
            pool.wait_ge(made, 3)
            pool.memset(tiles(restart[:, :])[:, :, 0:1], 0.0).then_inc(made, 1)
            pool.affine_select(out=own[:, :, :], in_=own[:, :, :], compare_op=ALU.is_ge, fill=0.0,
                               base=0, pattern=[[-GK, GH], [0, GV]], channel_multiplier=1).then_inc(made, 1)
            pool.affine_select(out=tri[:, :], in_=tri[:, :], compare_op=ALU.is_ge, fill=0.0,
                               base=0, pattern=[[1, P]], channel_multiplier=-1).then_inc(made, 1)
            pool.wait_ge(made, 6)
            pool.affine_select(out=own[:, :, :], in_=own[:, :, :], compare_op=ALU.is_ge, fill=0.0,
                               base=GK - 1, pattern=[[GK, GH], [0, GV]], channel_multiplier=-1).then_inc(made, 1)
            pool.wait_ge(loaded, n_w)
            with pool.Fori(0, NC) as c:
                pool.wait_ge(ln_step.sem, ln_step.at(c, 2 * TPC + 1))
                pool.tensor_tensor(rstd[:, :], var_eps[:, :], g.half[:, 0:TPC], ALU.pow).then_inc(rstd_done.sem, 1)
                pool.wait_ge(silu_done.sem, silu_done.at(c))
                pool.tensor_tensor(silu[:, :, :], silu[:, :, :], w["rms"][:, :].unsqueeze(1).to_broadcast([P, TPC, GV_ALL]),
                                   ALU.mult).then_inc(silu_w.sem, 1)
                pool.wait_ge(norm.sem, norm.at(c, 2))
                pool.tensor_tensor(rr[:, :], ms[:, :], g.half[:, 0:TPC * GH], ALU.pow).then_inc(rr_done.sem, 1)

        @block.vector
        def _(dve):
            start(dve, [ln_step, gate, qk_done, k_done, state_done, a_done, norm, on_done, x_done])
            dve.wait_ge(loaded, n_w)
            dve.wait_ge(made, 7)
            xt = g.x[:, :, :].rearrange("p b (t d) -> p (b t) d", t=TPB).rearrange("p (c t) d -> p c t d", c=NC)
            with dve.Fori(0, NC) as c:
                for t in range(TPC):
                    dve.bn_stats(stats[:, t, :], xt[:, c, t, :]).then_inc(ln_step.sem, 1)
                dve.wait_ge(ln_step.sem, ln_step.at(c, TPC))
                dve.sem_inc(g.spare, 1)
                for t in range(TPC):
                    dve.bn_aggr(mv[:, t, :], stats[:, t, :]).then_inc(ln_step.sem, 1)
                dve.wait_ge(ln_step.sem, ln_step.at(c, 2 * TPC))
                dve.tensor_scalar(var_eps[:, :], mv[:, :, 1], LN_EPS, None, ALU.add).then_inc(ln_step.sem, 1)
                dve.wait_ge(rstd_done.sem, rstd_done.at(c))
                for t in range(TPC):
                    m = dve.tensor_scalar(xn[:, t, :], xt[:, c, t, :], mv[:, t, 0:1], rstd[:, t:t + 1], ALU.subtract, ALU.mult)
                m.then_inc(ln_step.sem, 1)
                dve.wait_ge(gl_psum.sem, gl_psum.at(c))
                dve.tensor_scalar(gl[:, :], bank[2][:, :], w["b"][:, 0:1], None, ALU.add).then_inc(gate.sem, 1)
                dve.wait_ge(fa_step.sem, fa_step.at(c))
                dve.scalar_tensor_tensor(out=lg[:, :], in0=gl[:, :], scalar=0.0, in1=fa[:, :], op0=ALU.min,
                                         op1=ALU.subtract).then_inc(gate.sem, 1)
                dve.wait_ge(gate.sem, gate.at(c, 2))
                dve.tensor_tensor_scan(gsum[:, :], restart[:, :], lg[:, :], 0.0, ALU.mult, ALU.add).then_inc(gate.sem, 1)
                dve.wait_ge(gate.sem, gate.at(c, 3))
                gs = tiles(gsum[:, :])
                dve.tensor_tensor(tiles(gmid[:, :]), gs, gs[:, :, MID:MID + 1].to_broadcast([P, TPC, P]), ALU.subtract).then_inc(gate.sem, 1)
                two = gsum[:, :].rearrange("p (b t n) -> p b t n", b=BPC, t=TPB)
                dve.tensor_tensor(fac[:, :], two[:, :, 0, P - 1], two[:, :, 0, MID], ALU.subtract).then_inc(gate.sem, 1)
                dve.wait_ge(gate.sem, gate.at(c, 5))
                dve.tensor_tensor(fac[:, :], fac[:, :], two[:, :, 1, MID], ALU.add).then_inc(gate.sem, 1)
                dve.wait_ge(qk_psum.sem, qk_psum.at(c))
                dve.wait_ge(e_done.sem, e_done.at(c, 1))
                dve.scalar_tensor_tensor(out=qt[:, :], in0=bank[3][:, :], scalar=GK ** -0.5, in1=eq[:, :], op0=ALU.mult,
                                         op1=ALU.mult).then_inc(qk_done.sem, 1)
                dve.wait_ge(e_done.sem, e_done.at(c, 2))
                dve.tensor_tensor(kt[:, :], bank[4][:, :], ek[:, :], ALU.mult).then_inc(qk_done.sem, 1)
                dve.wait_ge(k_psum.sem, k_psum.at(c))
                dve.tensor_scalar(ktok[:, :, :], bank[1][:, 0:BPC * P].rearrange("p (b n) -> p b n", b=BPC), 1.0, None, ALU.mult).then_inc(k_done.sem, 1)
                for h in range(GH):
                    dve.wait_ge(a_psum.sem, a_psum.at(c, h + 1))
                    dve.scalar_tensor_tensor(out=am[:, h, :, :], in0=tiles(bank[3 + h][:, :]), scalar=3e38,
                                             in1=tri[:, :].unsqueeze(1).to_broadcast([P, TPC, P]), op0=ALU.min, op1=ALU.mult).then_inc(a_done.sem, 1)
                dve.wait_ge(kv_psum.sem, kv_psum.at(c))
                dve.wait_ge(e_done.sem, e_done.at(c, 3))
                for j in range(BPC):
                    dve.scalar_tensor_tensor(out=state[:, j, :], in0=bank[2][:, j * GV_ALL:(j + 1) * GV_ALL], scalar=fac[:, j:j + 1],
                                             in1=own[:, :, :].rearrange("p h n -> p (h n)"), op0=ALU.mult, op1=ALU.mult).then_inc(state_done.sem, 1)
                dve.wait_ge(sq_done.sem, sq_done.at(c))
                dve.tensor_reduce(ss[:, :], sq[:, :, :].rearrange("p t (h n) -> p (t h) n", n=GV), AX.X, ALU.add).then_inc(norm.sem, 1)
                dve.wait_ge(norm.sem, norm.at(c, 1))
                dve.tensor_scalar(ms[:, :], ss[:, :], 1.0 / GV, RMS_EPS, ALU.mult, ALU.add).then_inc(norm.sem, 1)
                dve.wait_ge(rr_done.sem, rr_done.at(c))
                for j in range(2):
                    dve.tensor_tensor(on[:, 2 * j:2 * j + 2, :].rearrange("p t (h n) -> p (t h) n", n=GV),
                                      bank[(7, 0)[j]][:, :].rearrange("p (k n) -> p k n", n=GV),
                                      rr[:, 8 * j:8 * j + 8].unsqueeze(2).to_broadcast([P, 8, GV]), ALU.mult).then_inc(norm.sem, 1)
                dve.wait_ge(norm.sem, norm.at(c, 4))
                dve.wait_ge(silu_w.sem, silu_w.at(c))
                dve.tensor_tensor(on[:, :, :], on[:, :, :], silu[:, :, :], ALU.mult).then_inc(on_done.sem, 1)
                dve.wait_ge(y_psum.sem, y_psum.at(c))
                dve.tensor_tensor(xt[:, c, :, :], xt[:, c, :, :], tiles(bank[3][:, :]), ALU.add).then_inc(x_done.sem, 1)

        @block.scalar
        def _(act):
            start(act, [xnT_done, z_done, v_done, fa_step, e_done, silu_done, sq_done, onT_done])
            with act.Fori(0, NC) as c:
                act.wait_ge(xnT_psum.sem, xnT_psum.at(c))
                act.activation(xnT[:, :], bank[0][:, :], ACT.Copy).then_inc(xnT_done.sem, 1)
                act.wait_ge(z_psum.sem, z_psum.at(c))
                act.activation(z[:, :], bank[1][0:LOW, :], ACT.Copy).then_inc(z_done.sem, 1)
                for j in range(2):
                    act.wait_ge(v_psum.sem, v_psum.at(c, j + 1))
                    act.activation(v[:, 2 * j:2 * j + 2, :].rearrange("p t n -> p (t n)"), bank[5 + j][:, :], ACT.Copy).then_inc(v_done.sem, 1)
                act.wait_ge(gate.sem, gate.at(c, 1))
                act.activation(fa[:, :], gl[:, :], ACT.Abs).then_inc(fa_step.sem, 1)
                act.wait_ge(fa_step.sem, fa_step.at(c, 1))
                act.activation(fa[:, :], fa[:, :], ACT.Exp, scale=-1.0).then_inc(fa_step.sem, 1)
                act.wait_ge(fa_step.sem, fa_step.at(c, 2))
                act.activation(fa[:, :], fa[:, :], ACT.Ln, bias=1.0).then_inc(fa_step.sem, 1)
                act.wait_ge(gate.sem, gate.at(c, 4))
                act.activation(eq[:, :], gmid[:, :], ACT.Exp, scale=1.0 / GATE_NORM).then_inc(e_done.sem, 1)
                act.activation(ek[:, :], gmid[:, :], ACT.Exp, scale=-1.0 / GATE_NORM).then_inc(e_done.sem, 1)
                act.wait_ge(gate.sem, gate.at(c, 6))
                act.activation(fac[:, :], fac[:, :], ACT.Exp, scale=1.0 / GATE_NORM).then_inc(e_done.sem, 1)
                for j in range(2):
                    act.wait_ge(o_gate_psum.sem, o_gate_psum.at(c, j + 1))
                    act.activation(silu[:, 2 * j:2 * j + 2, :].rearrange("p t n -> p (t n)"), bank[(7, 0)[j]][:, :], ACT.Silu).then_inc(silu_done.sem, 1)
                for j in range(2):
                    act.wait_ge(o_psum.sem, o_psum.at(c, j + 1))
                    act.activation(sq[:, 2 * j:2 * j + 2, :].rearrange("p t n -> p (t n)"), bank[(7, 0)[j]][:, :], ACT.Square).then_inc(sq_done.sem, 1)
                for j in range(2):
                    act.wait_ge(onT_psum.sem, onT_psum.at(c, j + 1))
                    act.activation(onT[:, j, :], bank[1 + j][:, :], ACT.Copy).then_inc(onT_done.sem, 1)

        @block.tensor
        def _(pe):
            start(pe, [xnT_psum, z_psum, qk_psum, v_psum, gl_psum, o_gate_psum, k_psum, kv_psum, a_psum, o_psum, onT_psum, y_psum])
            pe.wait_ge(loaded, n_w)
            with pe.Fori(0, NC) as c:
                pe.wait_ge(ln_step.sem, ln_step.at(c))
                pe.wait_ge(norm.sem, norm.at(c - 1))
                for t in range(TPC):
                    m = pe.transpose(bank[0][:, t * P:(t + 1) * P], xn[:, t, :], g.ident[:, :])
                m.then_inc(xnT_psum.sem, 1)
                pe.wait_ge(xnT_done.sem, xnT_done.at(c))
                pe.wait_ge(onT_done.sem, onT_done.at(c - 1))
                pe.matmul(bank[1][0:LOW, :], w["w1"][:, :], xnT[:, :], start=True, stop=True).then_inc(z_psum.sem, 1)
                pe.wait_ge(x_done.sem, x_done.at(c - 1))
                pe.matmul(bank[3][:, :], w["wq"][:, :], xnT[:, :], start=True, stop=True)
                pe.matmul(bank[4][:, :], w["wk"][:, :], xnT[:, :], start=True, stop=True).then_inc(qk_psum.sem, 1)
                pe.wait_ge(z_done.sem, z_done.at(c))
                pe.sem_inc(g.spare, 1)
                pe.matmul(bank[2][:, :], w["w2"][:, :], z[:, :], start=True, stop=True).then_inc(gl_psum.sem, 1)
                for j in range(2):
                    for t in range(2):
                        tok = (2 * j + t) * P
                        m = pe.matmul(bank[5 + j][:, t * GV_ALL:(t + 1) * GV_ALL], xnT[:, tok:tok + P], w["wv"][:, :], start=True, stop=True)
                    m.then_inc(v_psum.sem, 1)
                for j in range(2):
                    for t in range(2):
                        tok = (2 * j + t) * P
                        m = pe.matmul(bank[(7, 0)[j]][:, t * GV_ALL:(t + 1) * GV_ALL], xnT[:, tok:tok + P], w["wg"][:, :], start=True, stop=True)
                    m.then_inc(o_gate_psum.sem, 1)
                pe.wait_ge(qk_done.sem, qk_done.at(c))
                for j in range(BPC):
                    m = pe.transpose(bank[1][:, j * P:(j + 1) * P], kt[:, 2 * j * P:(2 * j + 1) * P], g.ident[:, :])
                m.then_inc(k_psum.sem, 1)
                pe.wait_ge(v_done.sem, v_done.at(c))
                pe.sem_inc(g.spare, 1)
                for t in range(TPC):
                    for h in range(GH):
                        rows = slice(h * GK, (h + 1) * GK)
                        m = pe.matmul(bank[3 + h][:, t * P:(t + 1) * P], kt[rows, t * P:(t + 1) * P], qt[rows, t * P:(t + 1) * P],
                                      start=True, stop=True, tile_position=(h * GK, 0))
                        if t == TPC - 1:
                            m.then_inc(a_psum.sem, 1)
                pe.wait_ge(k_done.sem, k_done.at(c))
                for j in range(BPC):
                    m = pe.matmul(bank[2][:, j * GV_ALL:(j + 1) * GV_ALL], ktok[:, j, :], v[:, 2 * j, :], start=True, stop=True)
                m.then_inc(kv_psum.sem, 1)
                for t in range(TPC):
                    j, second = t // 2, t % 2
                    if not second:
                        pe.wait_ge(silu_done.sem, silu_done.at(c, j + 1))
                    pe.wait_ge(a_done.sem, a_done.at(c))
                    out = bank[(7, 0)[j]][:, second * GV_ALL:(second + 1) * GV_ALL]
                    if second:
                        pe.wait_ge(state_done.sem, state_done.at(c, j + 1))
                        pe.matmul(out, qt[:, t * P:(t + 1) * P], state[:, j, :], start=True, stop=False)
                    for h in range(GH):
                        m = pe.matmul(out[:, h * GV:(h + 1) * GV], am[:, h, t, :], v[:, t, h * GV:(h + 1) * GV],
                                      start=not second, stop=not second or h == GH - 1)
                    if second:
                        m.then_inc(o_psum.sem, 1)
                pe.wait_ge(on_done.sem, on_done.at(c))
                for j in range(2):
                    for t in range(TPC):
                        m = pe.transpose(bank[1 + j][:, t * P:(t + 1) * P], on[:, t, j * P:(j + 1) * P], g.ident[:, :])
                    m.then_inc(onT_psum.sem, 1)
                pe.wait_ge(onT_done.sem, onT_done.at(c))
                for t in range(TPC):
                    for j in range(2):
                        m = pe.matmul(bank[3][:, t * P:(t + 1) * P], onT[:, j, t * P:(t + 1) * P], w["wo"][:, j, :], start=j == 0, stop=j == 1)
                m.then_inc(y_psum.sem, 1)


MH, MD = 8, 16
SOFT_CAP = 15.0
MLSTM_EPS, MLSTM_NORM_EPS = 5e-5, 1e-6


def matrix_lstm(nc, g, name, w, ctx_tokens, prefetch=()):
    K2 = 384
    R = TPB * B * MH
    with ExitStack() as ctx:
        sb = lambda n, shape, dt=F32: ctx.enter_context(nc.sbuf_tensor(f"{name}_{n}", shape, dt))
        ps = lambda n, shape, dt=F32: ctx.enter_context(nc.psum_tensor(f"{name}_{n}", shape, dt))
        count = lambda n, per=1: Count(nc, f"{name}_{n}", per)
        sem = lambda n: nc.alloc_semaphore(f"{name}_{n}")
        xn = sb("xn", [P, TPC, D])
        xnT = sb("xnT", [P, NC, C_TOK])
        ctxT = sb("ctxT", [P, NC, C_TOK])
        ctx_tok = sb("ctx_tok", [P, B, TPB * D])
        stats = sb("stats", [P, TPC, 6])
        mv = sb("mv", [P, TPC, 2])
        var_eps = sb("var_eps", [P, TPC])
        rstd = sb("rstd", [P, TPC])
        bias15 = sb("bias15", [2 * MH, 1])
        thT = sb("thT", [2 * MH, C_TOK])
        th = sb("th", [P, NC, TPC * 2 * MH])
        ig, lf, fa, a_sb, c_tok, em = (sb(n, [P, TPB, B, MH]) for n in ("ig", "lf", "fa", "a_sb", "c_tok", "em"))
        c_row, m_row, rest = (sb(n, [R, P]) for n in ("c_row", "m_row", "rest"))
        carry = sb("carry", [P, 1])
        part = sb("part", [R, 3, P], BF16)
        gain = sb("gain", [P, D])
        mparts = sb("mparts", [96, B, S], BF16)
        sel3 = sb("sel3", [96, MH, P], BF16)
        trif = sb("trif", [P, P])
        rowmask = sb("rowmask", [P, MH])
        kTm = [sb(f"kTm{i}", [P, MH, S]) for i in range(2)]
        va = [sb(f"va{i}", [P, TPB, MH, HP]) for i in range(2)]
        cs = [sb(f"cs{i}", [P, TPB, MH]) for i in range(2)]
        dmat = sb("dmat", [P, 2, K2])
        smat = sb("smat", [P, 8, K2])
        u = sb("u", [P, 2, S])
        den = sb("den", [P, TPB, MH])
        hv, sq = sb("hv", [P, TPB, MH, MD]), sb("sq", [P, TPB, MH, MD])
        ms, rr, rz = (sb(n, [P, TPB, MH]) for n in ("ms", "rr", "rz"))
        eb = [ps(f"eb{i}", [P, 512]) for i in range(2)]
        s2 = [ps(f"s2_{i}", [P, 512]) for i in range(2)]
        up = ps("up", [P, 2, S])
        utp = ps("utp", [P, 512])
        tp = ps("tp", [P, C_TOK])
        lp = ps("lp", [P, C_TOK])
        ut = utp[:, :].rearrange("p (t h c) -> p t h c", t=TPB, c=HP)

        ln_step = count("ln_step", 2 * TPC + 2)
        rstd_done = count("rstd_done")
        xnT_psum = count("xnT_psum")
        xnT_done = count("xnT_done")
        gates_psum = count("gates_psum")
        tanh_done = count("tanh_done")
        th_psum = count("th_psum")
        th_done = count("th_done")
        rv, ra, rp, setup = (sem(n) for n in ("scan_dve", "scan_act", "scan_pe", "setup"))
        rdy = sem("scan_ready")
        parts_out, parts_in = sem("parts_out"), sem("parts_in")
        k_done = count("k_done", MH)
        c_done = count("c_done")
        va_done = count("va_done")
        e_psum = count("e_psum", MH)
        d_done = count("d_done", MH)
        s_psum = count("s_psum", MH)
        s_done = count("s_done", MH)
        av_done = count("av_done", 2)
        u_done = count("u_done")
        ut_psum = count("ut_psum")
        tail = count("tail", 12)
        rr_done = count("rr_done")
        block = ctx.enter_context(nc.Block())

        def turns(e, first, body, last):
            first()
            body(0, 0, True, False)
            body(1, 1, True, True)
            with e.Fori(2, B - 3, 2) as b:
                body(b, 0, True, True)
                body(b + 1, 1, True, True)
            body(B - 2, 0, True, True)
            body(B - 1, 1, False, True)
            last()

        @block.sync
        def _(sp):
            sp.dma_start(ctxT[:, :, :], g.ctxT_dram.rearrange("d b s -> d (b s)").rearrange("d (c n) -> d c n", c=NC)).then_inc(g.ctx_loaded, 16)
            sp.dma_start(ctx_tok[:, :, :].rearrange("p b (t d) -> p b t d", t=TPB),
                         ctx_tokens.rearrange("b (t p) d -> p b t d", p=P)).then_inc(g.ctx_loaded, 16)
            for dst, src, s in prefetch:
                sp.dma_start(dst, src).then_inc(s, 16)
            sp.wait_ge(rdy, 5)
            sp.wait_ge(setup, 1)
            sp.dma_start(g.scratch, part[:, :, :]).then_inc(parts_out, 16)
            sp.wait_ge(parts_out, 16)
            for k in range(3):
                for t in range(TPB):
                    sp.dma_start(mparts[32 * k:32 * k + MH, :, t * P:(t + 1) * P],
                                 g.scratch.rearrange("(t b h) k s -> t k h b s", t=TPB, b=B)[t, k]).then_inc(parts_in, 16)
            sp.wait_ge(parts_in, 16 * 6)

        @block.gpsimd
        def _(pool):
            start(pool, [rstd_done, va_done, rr_done])
            pool.memset(mparts[:, :, :], 0.0).then_inc(setup, 1)
            with pool.Fori(0, NC) as c:
                pool.wait_ge(ln_step.sem, ln_step.at(c, 2 * TPC + 1))
                pool.tensor_tensor(rstd[:, :], var_eps[:, :], g.half[:, 0:TPC], ALU.pow).then_inc(rstd_done.sem, 1)
            pool.memset(trif[:, :], 1.0).then_inc(setup, 1)
            pool.memset(rowmask[:, :], 1.0).then_inc(setup, 1)
            pool.memset(sel3[:, :, :], 0.0).then_inc(setup, 1)
            for i in range(2):
                pool.memset(va[i][:, :, :, :], 1.0).then_inc(setup, 1)
            pool.wait_ge(setup, 6)
            pool.affine_select(out=trif[:, :], in_=trif[:, :], compare_op=ALU.is_ge, fill=0.0,
                               base=0, pattern=[[1, P]], channel_multiplier=-1).then_inc(setup, 1)
            pool.affine_select(out=rowmask[:, :], in_=rowmask[:, :], compare_op=ALU.is_ge, fill=0.0,
                               base=0, pattern=[[-MD, MH]], channel_multiplier=1).then_inc(setup, 1)
            pool.wait_ge(setup, 8)
            pool.affine_select(out=rowmask[:, :], in_=rowmask[:, :], compare_op=ALU.is_ge, fill=0.0,
                               base=MD - 1, pattern=[[MD, MH]], channel_multiplier=-1).then_inc(setup, 1)
            for k in range(3):
                pool.affine_select(out=sel3[:, :, :], in_=sel3[:, :, :], compare_op=ALU.not_equal, fill=1.0,
                                   base=-32 * k, pattern=[[-1, MH], [0, P]], channel_multiplier=1).then_inc(setup, 1)
                pool.wait_ge(setup, 10 + k)
            pool.wait_ge(g.ctx_loaded, 32)

            def values(b, i):
                pool.wait_ge(av_done.sem, av_done.at(b - 2))
                pool.sem_inc(g.spare, 1)
                pool.tensor_copy(va[i][:, :, :, 0:MD], ctx_tok[:, b, :].rearrange("p (t h c) -> p t h c", t=TPB, h=MH)).then_inc(va_done.sem, 1)

            def norm(b):
                pool.wait_ge(tail.sem, tail.at(b, 9))
                pool.tensor_tensor(rr[:, :, :], ms[:, :, :], g.half[:, 0:TPB * MH].rearrange("p (t h) -> p t h", t=TPB), ALU.pow).then_inc(rr_done.sem, 1)

            def body(b, i, more, tail_too):
                if tail_too:
                    norm(b - 1)
                if more:
                    values(b + 1, 1 - i)

            turns(pool, lambda: values(0, 0), body, lambda: norm(B - 1))

        @block.vector
        def _(dve):
            start(dve, [ln_step, th_done, k_done, c_done, s_done, tail])
            dve.wait_ge(g.loaded[name], 16 * g.n_loads[name])
            dve.tensor_scalar(bias15[:, :], w["bias"][:, :], 1.0 / SOFT_CAP, None, ALU.mult).then_inc(rdy, 1)
            dve.tensor_scalar(gain[:, :], w["outnorm"][:, :], 1.0, None, ALU.add)
            xt = g.x[:, :, :].rearrange("p b (t d) -> p (b t) d", t=TPB).rearrange("p (c t) d -> p c t d", c=NC)
            with dve.Fori(0, NC) as c:
                for t in range(TPC):
                    dve.bn_stats(stats[:, t, :], xt[:, c, t, :]).then_inc(ln_step.sem, 1)
                dve.wait_ge(ln_step.sem, ln_step.at(c, TPC))
                dve.sem_inc(g.spare, 1)
                for t in range(TPC):
                    dve.bn_aggr(mv[:, t, :], stats[:, t, :]).then_inc(ln_step.sem, 1)
                dve.wait_ge(ln_step.sem, ln_step.at(c, 2 * TPC))
                dve.tensor_scalar(var_eps[:, :], mv[:, :, 1], LN_EPS, None, ALU.add).then_inc(ln_step.sem, 1)
                dve.wait_ge(rstd_done.sem, rstd_done.at(c))
                dve.wait_ge(xnT_psum.sem, xnT_psum.at(c - 1))
                for t in range(TPC):
                    m = dve.tensor_scalar(xn[:, t, :], xt[:, c, t, :], mv[:, t, 0:1], rstd[:, t:t + 1], ALU.subtract, ALU.mult)
                m.then_inc(ln_step.sem, 1)
                dve.wait_ge(th_psum.sem, th_psum.at(c))
                dve.tensor_scalar(th[:, c, :], lp[:, 0:TPC * 2 * MH], SOFT_CAP, None, ALU.mult).then_inc(th_done.sem, 1)

            n = 0

            def step(m):
                nonlocal n
                m.then_inc(rv, 1)
                n += 1
                dve.wait_ge(rv, n)

            gates = th[:, :, :].rearrange("p c (a k) -> p (c a) k", k=2 * MH).rearrange("p (b t) k -> p t b k", t=TPB)
            flat = lambda a: a[:, :, :, :].rearrange("p t b h -> p (t b h)")
            dve.wait_ge(th_done.sem, th_done.at(NC - 1))
            step(dve.tensor_scalar(ig[:, :, :, :], gates[:, :, :, 0:MH], 1.0, None, ALU.mult))
            step(dve.tensor_scalar(lf[:, :, :, :], gates[:, :, :, MH:2 * MH], 1.0, None, ALU.mult))
            dve.sem_inc(rdy, 1)
            dve.wait_ge(ra, 3)
            step(dve.scalar_tensor_tensor(out=flat(lf), in0=flat(lf), scalar=0.0, in1=flat(fa), op0=ALU.min, op1=ALU.subtract))
            dve.sem_inc(rdy, 1)
            dve.wait_ge(rp, 1)
            step(dve.tensor_scalar(flat(a_sb), tp[:, 0:R], 1.0, None, ALU.mult))
            step(dve.tensor_tensor(flat(c_tok), flat(ig), flat(a_sb), ALU.subtract))
            dve.sem_inc(rdy, 1)
            dve.wait_ge(rp, 2)
            step(dve.tensor_scalar(c_row[:, :], lp[:, 0:P], 1.0, None, ALU.mult))
            step(dve.tensor_tensor_scan(m_row[:, :], c_row[:, :], c_row[:, :], -3e38, ALU.max, ALU.max))
            half = R // 2
            step(dve.tensor_scalar(carry[half:R, :], m_row[0:half, P - 1:P], 1.0, None, ALU.mult))
            step(dve.tensor_scalar(m_row[half:R, :], m_row[half:R, :], carry[half:R, 0:1], None, ALU.max))
            step(dve.tensor_scalar(rest[:, :], m_row[:, :], -1.0, None, ALU.mult))
            for k in range(3):
                step(dve.tensor_scalar(part[:, k, :], rest[:, :], 1.0, None, ALU.mult))
                if k < 2:
                    step(dve.tensor_tensor(rest[:, :], rest[:, :], part[:, k, :], ALU.subtract))
            dve.sem_inc(rdy, 1)
            dve.wait_ge(rp, 3)
            step(dve.tensor_tensor(flat(em), tp[:, 0:R], flat(a_sb), ALU.add))
            dve.sem_inc(rdy, 1)
            dve.wait_ge(ra, 4)
            dve.wait_ge(setup, 12)
            dve.wait_ge(g.ctx_loaded, 32)

            def keys(b, i):
                dve.wait_ge(av_done.sem, av_done.at(b - 2))
                for h in range(MH):
                    dve.tensor_scalar(kTm[i][:, h, :], ctxT[:, :, :].rearrange("p c n -> p (c n)").rearrange("p (b n) -> p b n", b=B)[:, b, :],
                                      rowmask[:, h:h + 1], MD ** -0.5, ALU.mult, ALU.mult).then_inc(k_done.sem, 1)
                dve.tensor_scalar(cs[i][:, :, :], c_tok[:, :, b, :], 1.0, None, ALU.mult).then_inc(c_done.sem, 1)

            def weigh(b, lo, hi):
                for h in range(lo, hi):
                    dve.wait_ge(d_done.sem, d_done.at(b, h + 1))
                    dve.wait_ge(s_psum.sem, s_psum.at(b, h + 1))
                    dve.tensor_tensor(smat[:, h, :], s2[h % 2][:, 0:K2], dmat[:, h % 2, :], ALU.mult).then_inc(s_done.sem, 1)

            def finish(b):
                over_d = lambda a: a[:, :, :].unsqueeze(3).to_broadcast([P, TPB, MH, MD])
                k = 0

                def chain(m):
                    nonlocal k
                    m.then_inc(tail.sem, 1)
                    k += 1
                    dve.wait_ge(tail.sem, tail.at(b, k))

                dve.wait_ge(ut_psum.sem, ut_psum.at(b))
                chain(dve.tensor_scalar(den[:, :, :], ut[:, :, :, MD], 1.0, None, ALU.mult))
                chain(dve.scalar_tensor_tensor(out=den[:, :, :], in0=den[:, :, :], scalar=-1.0, in1=den[:, :, :], op0=ALU.mult, op1=ALU.max))
                chain(dve.tensor_tensor(den[:, :, :], den[:, :, :], em[:, :, b, :], ALU.max))
                chain(dve.tensor_scalar(den[:, :, :], den[:, :, :], MLSTM_EPS, None, ALU.add))
                chain(dve.reciprocal(rz[:, :, :], den[:, :, :]))
                chain(dve.tensor_tensor(hv[:, :, :, :], ut[:, :, :, 0:MD], over_d(rz), ALU.mult))
                chain(dve.tensor_tensor(sq[:, :, :, :], hv[:, :, :, :], hv[:, :, :, :], ALU.mult))
                chain(dve.tensor_reduce(den[:, :, :], sq[:, :, :, :], AX.X, ALU.add))
                chain(dve.tensor_scalar(ms[:, :, :], den[:, :, :], 1.0 / MD, MLSTM_NORM_EPS, ALU.mult, ALU.add))
                dve.wait_ge(rr_done.sem, rr_done.at(b))
                chain(dve.tensor_tensor(hv[:, :, :, :], hv[:, :, :, :], over_d(rr), ALU.mult))
                chain(dve.tensor_tensor(hv[:, :, :, :], hv[:, :, :, :], gain[:, :].rearrange("p (h c) -> p h c", h=MH).unsqueeze(1).to_broadcast([P, TPB, MH, MD]), ALU.mult))
                dve.tensor_tensor(g.x[:, b, :], g.x[:, b, :], hv[:, :, :, :].rearrange("p t h c -> p (t h c)"), ALU.add).then_inc(tail.sem, 1)

            def body(b, i, more, tail_too):
                weigh(b, 0, 3)
                if more:
                    keys(b + 1, 1 - i)
                weigh(b, 3, 5)
                if tail_too:
                    finish(b - 1)
                weigh(b, 5, MH)

            turns(dve, lambda: keys(0, 0), body, lambda: finish(B - 1))

        @block.scalar
        def _(act):
            start(act, [xnT_done, tanh_done, d_done, u_done])
            act.wait_ge(rdy, 1)
            with act.Fori(0, NC) as c:
                act.wait_ge(xnT_psum.sem, xnT_psum.at(c))
                act.sem_inc(g.spare, 1)
                act.activation(xnT[:, c, :], tp[:, :], ACT.Copy).then_inc(xnT_done.sem, 1)
                act.wait_ge(th_psum.sem, th_psum.at(c - 1))
                act.wait_ge(gates_psum.sem, gates_psum.at(c))
                act.activation(thT[:, :], eb[0][0:2 * MH, :], ACT.Tanh, bias=bias15[:, 0:1], scale=1.0 / SOFT_CAP).then_inc(tanh_done.sem, 1)
            act.wait_ge(rdy, 2)
            act.activation(fa[:, :, :, :], lf[:, :, :, :], ACT.Abs).then_inc(ra, 1)
            act.wait_ge(ra, 1)
            act.activation(fa[:, :, :, :], fa[:, :, :, :], ACT.Exp, scale=-1.0).then_inc(ra, 1)
            act.wait_ge(ra, 2)
            act.activation(fa[:, :, :, :], fa[:, :, :, :], ACT.Ln, bias=1.0).then_inc(ra, 1)
            act.wait_ge(rdy, 6)
            act.activation(em[:, :, :, :], em[:, :, :, :], ACT.Exp, scale=-1.0).then_inc(ra, 1)

            def sums(b):
                act.wait_ge(av_done.sem, av_done.at(b))
                act.wait_ge(ut_psum.sem, ut_psum.at(b - 1))
                act.activation(u[:, :, :], up[:, :, :], ACT.Copy).then_inc(u_done.sem, 1)

            def body(b, i, more, tail_too):
                act.wait_ge(c_done.sem, c_done.at(b))
                for h in range(MH):
                    act.wait_ge(e_psum.sem, e_psum.at(b, h + 1))
                    act.wait_ge(s_done.sem, s_done.at(b, h - 1))
                    act.activation(dmat[:, h % 2, 0:S], eb[h % 2][:, 0:S], ACT.Exp, bias=cs[i][:, 0, h:h + 1])
                    act.activation(dmat[:, h % 2, S:K2], eb[h % 2][:, S:K2], ACT.Exp, bias=cs[i][:, 1, h:h + 1]).then_inc(d_done.sem, 1)
                    if h == 2 and tail_too:
                        sums(b - 1)

            turns(act, lambda: None, body, lambda: sums(B - 1))

        @block.tensor
        def _(pe):
            start(pe, [xnT_psum, gates_psum, th_psum, e_psum, s_psum, av_done, ut_psum])
            pe.wait_ge(g.loaded[name], 16 * g.n_loads[name])
            pe.wait_ge(g.ctx_loaded, 32)
            with pe.Fori(0, NC) as c:
                pe.wait_ge(ln_step.sem, ln_step.at(c))
                pe.wait_ge(xnT_done.sem, xnT_done.at(c - 1))
                for t in range(TPC):
                    m = pe.transpose(tp[:, t * P:(t + 1) * P], xn[:, t, :], g.ident[:, :])
                m.then_inc(xnT_psum.sem, 1)
                pe.wait_ge(xnT_done.sem, xnT_done.at(c))
                pe.wait_ge(tanh_done.sem, tanh_done.at(c - 1))
                pe.matmul(eb[0][0:2 * MH, :], w["gq"][:, :], xnT[:, c, :], start=True, stop=False)
                pe.matmul(eb[0][0:2 * MH, :], w["gk"][:, :], ctxT[:, c, :], start=False, stop=False)
                pe.matmul(eb[0][0:2 * MH, :], w["gv"][:, :], ctxT[:, c, :], start=False, stop=True).then_inc(gates_psum.sem, 1)
                pe.wait_ge(tanh_done.sem, tanh_done.at(c))
                pe.wait_ge(th_done.sem, th_done.at(c - 1))
                pe.sem_inc(g.spare, 1)
                for t in range(TPC):
                    m = pe.transpose(lp[:, t * 2 * MH:(t + 1) * 2 * MH], thT[:, t * P:(t + 1) * P], g.ident[0:2 * MH, 0:2 * MH])
                m.then_inc(th_psum.sem, 1)
            pe.wait_ge(rdy, 3)
            pe.wait_ge(setup, 12)
            ls = lf[:, :, :, :].rearrange("p t b h -> p t (b h)")
            pe.matmul(tp[:, 0:R // 2], trif[:, :], ls[:, 0, :], start=True, stop=True)
            pe.matmul(tp[:, R // 2:R], trif[:, :], ls[:, 1, :], start=True, stop=False)
            pe.matmul(tp[:, R // 2:R], g.ones[:, :], ls[:, 0, :], start=False, stop=True).then_inc(rp, 1)
            pe.wait_ge(rdy, 4)
            pe.transpose(lp[:, 0:P], c_tok[:, :, :, :].rearrange("p t b h -> p (t b h)"), g.ident[:, :]).then_inc(rp, 1)
            pe.wait_ge(rdy, 5)
            pe.transpose(tp[:, 0:R], m_row[:, :], g.ident[:, :]).then_inc(rp, 1)
            pe.wait_ge(parts_in, 16 * 6)
            xb = xnT[:, :, :].rearrange("p c n -> p (c n)").rearrange("p (b n) -> p b n", b=B)

            def head(b, i, h):
                pe.wait_ge(d_done.sem, d_done.at(b, h - 1))
                e = eb[h % 2]
                for t, (c0, n) in enumerate([(0, S), (S, P)]):
                    pe.matmul(e[:, c0:c0 + n], sel3[:, h, :], mparts[:, b, S - n:S], start=True, stop=False)
                    m = pe.matmul(e[:, c0:c0 + P], g.ident_bf[:, :], g.tri_k[:, :], start=False, stop=True)
                m.then_inc(e_psum.sem, 1)
                pe.wait_ge(k_done.sem, k_done.at(b, h + 1))
                pe.wait_ge(s_done.sem, s_done.at(b, h - 1))
                for t, (c0, n) in enumerate([(0, S), (S, P)]):
                    m = pe.matmul(s2[h % 2][:, c0:c0 + n], kTm[i][:, h, t * P:(t + 1) * P], xb[:, b, S - n:S], start=True, stop=True)
                m.then_inc(s_psum.sem, 1)

            def values(b, i, q):
                if q == 0:
                    pe.wait_ge(u_done.sem, u_done.at(b - 1))
                    pe.wait_ge(va_done.sem, va_done.at(b))
                pe.wait_ge(s_done.sem, s_done.at(b, 4 * q + 4))
                for kt, q0, n, p0, first, last in [(0, 0, P, 0, True, True), (0, P, P, P, True, False), (1, P, P, S, False, True)]:
                    for j in range(4):
                        h = 4 * q + j
                        m = pe.matmul(up[HP * j:HP * (j + 1), q, q0:q0 + n], va[i][:, kt, h, :], smat[:, h, p0:p0 + n],
                                      start=first, stop=last, tile_position=(0, HP * j))
                m.then_inc(av_done.sem, 1)

            def sums(b):
                pe.wait_ge(u_done.sem, u_done.at(b))
                pe.wait_ge(tail.sem, tail.at(b - 1, 6))
                for t in range(TPB):
                    for q in range(2):
                        m = pe.transpose(utp[:, (2 * t + q) * P:(2 * t + q + 1) * P], u[:, q, t * P:(t + 1) * P], g.ident[:, :])
                m.then_inc(ut_psum.sem, 1)

            def body(b, i, more, tail_too):
                for h in range(MH):
                    head(b, i, h)
                    if h == 4 and tail_too:
                        sums(b - 1)
                    if h == 5:
                        values(b, i, 0)
                values(b, i, 1)

            turns(pe, lambda: None, body, lambda: sums(B - 1))


WH, WD = 16, 64
INNER = WH * WD
WFF = 512


def decoder(nc, g, name, w, mask, prefetch=()):
    CH = INNER // P
    JOBS = 4
    FC = WFF // P
    with ExitStack() as ctx:
        sb = lambda n, shape, dt=F32: ctx.enter_context(nc.sbuf_tensor(f"{name}_{n}", shape, dt))
        ps = lambda n, shape, dt=F32: ctx.enter_context(nc.psum_tensor(f"{name}_{n}", shape, dt))
        count = lambda n, per=1: Count(nc, f"{name}_{n}", per)
        y = sb("y", [P, 2, TPB, D])
        yT = sb("yT", [P, 2, S])
        ctxT = sb("ctxT", [P, 2, S])
        stats = sb("stats", [P, TPB, 6])
        mv = sb("mv", [P, TPB, 2])
        var_eps = sb("var_eps", [P, TPB])
        rstd = sb("rstd", [P, TPB])
        qT = sb("qT", [P, CH, S])
        kTm = sb("kTm", [P, WH, S])
        va = sb("va", [P, TPB, WH, WD + 1])
        negm = sb("negm", [P, 2, TPB])
        prob = sb("prob", [P, 2, TPB, S])
        probT = sb("probT", [P, 2, TPB, S])
        rz = sb("rz", [P, TPB, 2])
        on = [sb(f"on{i}", [P, TPB, WH, WD]) for i in range(2)]
        onT = sb("onT", [P, CH, S])
        hT = sb("hT", [P, FC, S])
        mu = sb("mu", [1, B * S], mybir.dt.uint8)
        mb = sb("mb", [1, B, S], BF16)
        s1 = [ps(f"s1_{i}", [P, 512]) for i in range(2)]
        pt = [ps(f"pt_{i}", [P, 512]) for i in range(2)]
        pr = [ps(f"pr_{i}", [P, 512]) for i in range(2)]
        ob = [ps(f"ob_{i}", [P, TPB, 2, WD + 1]) for i in range(2)]

        ln_step = count("ln_step", 8 * 8)
        rstd_done = count("rstd_done", 8)
        yT_psum, yT_done = count("yT_psum", 6), count("yT_done", 6)
        qk_psum = count("qk_psum", 4 * JOBS)
        q_done, k_done = count("q_done", 4 * JOBS), count("k_done", 4 * JOBS)
        v_psum, v_done = count("v_psum", 4 * JOBS), count("v_done", 4 * JOBS)
        s1_psum = count("s1_psum", WH * JOBS)
        max_done = count("max_done", WH * JOBS)
        exp_done = count("exp_done", WH * JOBS)
        pt_psum, pt_done = count("pt_psum", WH * JOBS), count("pt_done", WH * JOBS)
        av_done = count("av_done", WH * JOBS)
        rz_done, on_done = count("rz_done", WH // 2 * JOBS), count("on_done", WH // 2 * JOBS)
        onT_psum, onT_done = count("onT_psum", 4 * JOBS), count("onT_done", 4 * JOBS)
        a_psum = count("a_psum", JOBS)
        bias_done = count("bias_done", 6)
        added = count("added", 6)
        h_psum, h_done = count("h_psum", 4), count("h_done", 4)
        f_psum = count("f_psum", 2)
        x_done = count("x_done", 2)
        ctx_in = [nc.alloc_semaphore(f"{name}_ctx_in{i}") for i in range(2)]
        mask_in = nc.alloc_semaphore(f"{name}_mask_in")
        made = nc.alloc_semaphore(f"{name}_made")
        masked = nc.alloc_semaphore(f"{name}_masked")
        block = ctx.enter_context(nc.Block())
        loaded, n_w = g.loaded[name], 16 * g.n_loads[name]

        @block.sync
        def _(sp):
            sp.dma_start(mu[:, :], mask).then_inc(mask_in, 16)
            for dst, src, s in prefetch:
                sp.dma_start(dst, src).then_inc(s, 16)
            with sp.Fori(0, B // 2) as p:
                for i in range(2):
                    sp.wait_ge(v_psum.sem, v_psum.at(p - 1, 4 * (2 + i) + 4))
                    sp.dma_start(ctxT[:, i, :], g.ctxT_dram[:, 2 * p + i, :]).then_inc(ctx_in[i], 16)

        @block.gpsimd
        def _(pool):
            start(pool, [rstd_done, bias_done])
            pool.memset(kTm[:, :, :], 0.0).then_inc(made, 1)
            pool.memset(va[:, :, :, :], 1.0).then_inc(made, 1)
            pool.wait_ge(loaded, n_w)
            with pool.Fori(0, B // 2) as p:
                def rstds(n):
                    pool.wait_ge(ln_step.sem, ln_step.at(p, 8 * n + 5))
                    pool.tensor_tensor(rstd[:, :], var_eps[:, :], g.half[:, 0:TPB], ALU.pow).then_inc(rstd_done.sem, 1)

                def bias(n, i, row):
                    pool.wait_ge(yT_psum.sem, yT_psum.at(p, n + 1))
                    pool.tensor_tensor(y[:, i, :, :], y[:, i, :, :], row[:, :].unsqueeze(1).to_broadcast([P, TPB, D]),
                                       ALU.add).then_inc(bias_done.sem, 1)

                rstds(0)
                rstds(1)
                bias(0, 0, w["sa_bo"])
                bias(1, 1, w["sa_bo"])
                rstds(2)
                bias(2, 0, w["ca_bo"])
                rstds(3)
                bias(3, 1, w["ca_bo"])
                rstds(4)
                bias(4, 0, w["fc2_b"])
                rstds(5)
                bias(5, 1, w["fc2_b"])
                rstds(6)
                rstds(7)

        @block.vector
        def _(dve):
            start(dve, [ln_step, k_done, max_done, pt_done, rz_done, on_done, added, x_done])
            dve.wait_ge(mask_in, 16)
            dve.tensor_scalar(mb[:, :, :].rearrange("p b s -> p (b s)"), mu[:, :], NEG, None, ALU.mult).then_inc(masked, 1)
            dve.wait_ge(loaded, n_w)
            dve.wait_ge(made, 2)
            with dve.Fori(0, B // 2) as p:
                def norm_start(n, src):
                    at = lambda k: ln_step.at(p, 8 * n + k)
                    for t in range(TPB):
                        dve.bn_stats(stats[:, t, :], src(t)).then_inc(ln_step.sem, 1)
                    dve.wait_ge(ln_step.sem, at(2))
                    dve.sem_inc(g.spare, 1)
                    for t in range(TPB):
                        dve.bn_aggr(mv[:, t, :], stats[:, t, :]).then_inc(ln_step.sem, 1)
                    dve.wait_ge(ln_step.sem, at(4))
                    dve.tensor_scalar(var_eps[:, :], mv[:, :, 1], LN_EPS, None, ALU.add).then_inc(ln_step.sem, 1)

                def norm_end(n, i, src, gain=None):
                    at = lambda k: ln_step.at(p, 8 * n + k)
                    dve.wait_ge(rstd_done.sem, rstd_done.at(p, n + 1))
                    for t in range(TPB):
                        m = dve.tensor_scalar(y[:, i, t, :], src(t), mv[:, t, 0:1], rstd[:, t:t + 1], ALU.subtract, ALU.mult)
                    if gain is None:
                        m.then_inc(ln_step.sem, 3)
                        return
                    m.then_inc(ln_step.sem, 1)
                    for k, op in enumerate((ALU.mult, ALU.add)):
                        dve.wait_ge(ln_step.sem, at(6 + k))
                        dve.tensor_tensor(y[:, i, :, :], y[:, i, :, :], w[gain + "gb"[k]][:, :].unsqueeze(1).to_broadcast([P, TPB, D]),
                                          op).then_inc(ln_step.sem, 1)

                def keys(a):
                    for r in range(4):
                        dve.wait_ge(qk_psum.sem, qk_psum.at(p, 4 * a + r + 1))
                        kb = (pr, pt)[r % 2][1][:, :].rearrange("p (c n) -> p c n", c=2)
                        for j in range(2):
                            rows = slice(j * WD, (j + 1) * WD)
                            m = dve.tensor_scalar(kTm[rows, :, :].rearrange("p (c j) n -> p c j n", j=2)[:, 2 * r:2 * r + 2, j, :], kb[rows, :, :],
                                                  1.0, None, ALU.mult)
                        m.then_inc(k_done.sem, 1)

                def add(n, i, bank, psum, k):
                    dve.wait_ge(bias_done.sem, bias_done.at(p, n + 1))
                    dve.wait_ge(psum.sem, psum.at(p, k))
                    dve.tensor_tensor(y[:, i, :, :], y[:, i, :, :], bank[:, 0:S].rearrange("p (t d) -> p t d", t=TPB),
                                      ALU.add).then_inc(added.sem, 1)
                    dve.wait_ge(added.sem, added.at(p, n + 1))

                def of_y(i):
                    return lambda t: y[:, i, t, :]

                def tail_add(a):
                    add(a, a % 2, pr[0], a_psum, a + 1)
                    norm_start(2 + a, of_y(a % 2))

                def tail_norm(a):
                    norm_end(2 + a, a % 2, of_y(a % 2), ("ln1_", "ln2_")[a // 2])

                def heads(a, tail):
                    for h in range(WH + 2):
                        if h < WH:
                            dve.wait_ge(s1_psum.sem, s1_psum.at(p, WH * a + h + 1))
                            dve.tensor_reduce(negm[:, h % 2, :], s1[h % 2][:, :].rearrange("p (t c) -> p t c", t=TPB), AX.X, ALU.max,
                                              negate=True).then_inc(max_done.sem, 1)
                        if 1 <= h <= WH:
                            k = h - 1
                            dve.wait_ge(pt_psum.sem, pt_psum.at(p, WH * a + k + 1))
                            dve.wait_ge(av_done.sem, av_done.at(p, WH * a + k - 1))
                            dve.tensor_scalar(probT[:, k % 2, :, :].rearrange("p t n -> p (t n)"), pt[k % 2][:, :], 1.0, None, ALU.mult).then_inc(pt_done.sem, 1)
                        if h >= 3 and h % 2:
                            q = (h - 3) // 2
                            o = ob[q % 2]
                            dve.wait_ge(av_done.sem, av_done.at(p, WH * a + h - 1))
                            dve.reciprocal(rz[:, :, :], o[:, :, :, WD]).then_inc(rz_done.sem, 1)
                            dve.wait_ge(rz_done.sem, rz_done.at(p, WH // 2 * a + q + 1))
                            for t in range(TPB):
                                m = dve.tensor_tensor(on[a % 2][:, t, 2 * q:2 * q + 2, :], o[:, t, :, 0:WD],
                                                      rz[:, t, :].unsqueeze(2).to_broadcast([P, 2, WD]), ALU.mult)
                            m.then_inc(on_done.sem, 1)
                        if h == 8 and tail:
                            tail_add(a - 1)
                        if h == 10 and tail:
                            tail_norm(a - 1)

                def of_x(i):
                    return lambda t: g.x[:, 2 * p + i, t * D:(t + 1) * D]

                for i in range(2):
                    norm_start(i, of_x(i))
                    norm_end(i, i, of_x(i))
                for a in range(JOBS):
                    keys(a)
                    heads(a, a > 0)
                tail_add(JOBS - 1)
                tail_norm(JOBS - 1)
                for i in range(2):
                    add(4 + i, i, pt[i], f_psum, i + 1)
                    norm_start(6 + i, of_y(i))
                    norm_end(6 + i, i, of_y(i), "ln3_")
                    dve.wait_ge(ln_step.sem, ln_step.at(p, 8 * (7 + i)))
                    dve.tensor_tensor(g.x[:, 2 * p + i, :], g.x[:, 2 * p + i, :], y[:, i, :, :].rearrange("p t d -> p (t d)"),
                                      ALU.add).then_inc(x_done.sem, 1)
                    dve.wait_ge(x_done.sem, x_done.at(p, i + 1))

        @block.scalar
        def _(act):
            start(act, [yT_done, q_done, v_done, exp_done, onT_done, h_done])
            act.wait_ge(loaded, n_w)
            act.wait_ge(made, 2)
            with act.Fori(0, B // 2) as p:
                def transposed(n, i):
                    act.wait_ge(yT_psum.sem, yT_psum.at(p, n + 1))
                    act.activation(yT[:, i, :], pr[1][:, 0:S], ACT.Copy).then_inc(yT_done.sem, 1)

                def projected(a):
                    for r in range(4):
                        act.wait_ge(qk_psum.sem, qk_psum.at(p, 4 * a + r + 1))
                        act.activation(qT[:, 2 * r:2 * r + 2, :].rearrange("p c n -> p (c n)"), (pr, pt)[r % 2][0][:, :], ACT.Copy,
                                       scale=WD ** -0.5).then_inc(q_done.sem, 1)
                    for r in range(4):
                        t, u = r // 2, r % 2
                        act.wait_ge(v_psum.sem, v_psum.at(p, 4 * a + r + 1))
                        act.activation(va[:, t, 8 * u:8 * u + 8, 0:WD], s1[r % 2][:, :].rearrange("p (h c) -> p h c", h=8),
                                       ACT.Copy).then_inc(v_done.sem, 1)

                def tail_transposed(a, r):
                    act.wait_ge(onT_psum.sem, onT_psum.at(p, 4 * a + r + 1))
                    act.activation(onT[:, 2 * r:2 * r + 2, :].rearrange("p c n -> p (c n)"), pr[r % 2][:, :], ACT.Copy).then_inc(onT_done.sem, 1)

                def heads(a, tail):
                    for h in range(WH):
                        act.wait_ge(max_done.sem, max_done.at(p, WH * a + h + 1))
                        act.wait_ge(pt_psum.sem, pt_psum.at(p, WH * a + h - 1))
                        for t in range(TPB):
                            m = act.activation(prob[:, h % 2, t, :], s1[h % 2][:, t * S:(t + 1) * S], ACT.Exp, bias=negm[:, h % 2, t:t + 1])
                        m.then_inc(exp_done.sem, 1)
                        if tail and h in (3, 5):
                            tail_transposed(a - 1, h - 3)
                            tail_transposed(a - 1, h - 2)
                        if tail and h == 13:
                            transposed(1 + a, (a - 1) % 2)

                for i in range(2):
                    transposed(i, i)
                for a in range(JOBS):
                    projected(a)
                    heads(a, a > 0)
                for r in range(4):
                    tail_transposed(JOBS - 1, r)
                transposed(5, 1)
                for i in range(2):
                    for k in range(FC):
                        if k % 2 == 0:
                            act.wait_ge(h_psum.sem, h_psum.at(p, 2 * i + k // 2 + 1))
                            if k == 0:
                                act.wait_ge(f_psum.sem, f_psum.at(p, i))
                        m = act.activation(hT[:, k, :], s1[k // 2][:, k % 2 * S:(k % 2 + 1) * S], ACT.Gelu, bias=w["fc1_b"][:, k:k + 1])
                        if k % 2:
                            m.then_inc(h_done.sem, 1)

        @block.tensor
        def _(pe):
            start(pe, [yT_psum, qk_psum, v_psum, s1_psum, pt_psum, av_done, onT_psum, a_psum, h_psum, f_psum])
            pe.wait_ge(loaded, n_w)
            pe.wait_ge(masked, 1)
            with pe.Fori(0, B // 2) as p:
                def transposes(n, i):
                    pe.wait_ge(ln_step.sem, ln_step.at(p, 8 * (n + 1)))
                    pe.wait_ge(yT_done.sem, yT_done.at(p, n))
                    for t in range(TPB):
                        m = pe.transpose(pr[1][:, t * P:(t + 1) * P], y[:, i, t, :], g.ident[:, :])
                    m.then_inc(yT_psum.sem, 1)

                def projections(a):
                    i, kind = a % 2, ("sa_w", "ca_w")[a // 2]
                    kv = yT[:, i, :] if a < 2 else ctxT[:, i, :]
                    pe.wait_ge(yT_done.sem, yT_done.at(p, max(a + 1, 2)))
                    if a >= 2:
                        pe.wait_ge(ctx_in[i], 16 * (p + 1))
                    for r in range(4):
                        banks = (pr, pt)[r % 2]
                        if r == 1:
                            pe.wait_ge(pt_done.sem, pt_done.at(p, WH * a))
                        if r >= 2:
                            pe.wait_ge(q_done.sem, q_done.at(p, 4 * a + r - 1))
                            pe.wait_ge(k_done.sem, k_done.at(p, 4 * a + r - 1))
                        for c in range(2):
                            cols = slice((2 * r + c) * P, (2 * r + c + 1) * P)
                            pe.matmul(banks[0][:, c * S:(c + 1) * S], w[kind + "q"][:, cols], yT[:, i, :], start=True, stop=True)
                            m = pe.matmul(banks[1][:, c * S:(c + 1) * S], w[kind + "k"][:, cols], kv, start=True, stop=True)
                        m.then_inc(qk_psum.sem, 1)
                    pe.wait_ge(exp_done.sem, exp_done.at(p, WH * a))
                    pe.wait_ge(h_done.sem, h_done.at(p - 1))
                    for r in range(4):
                        t, u = r // 2, r % 2
                        if r >= 2:
                            pe.wait_ge(v_done.sem, v_done.at(p, 4 * a + r - 1))
                        pe.matmul(s1[r % 2][:, :], kv[:, t * P:(t + 1) * P], w[kind + "v"][:, u * 512:(u + 1) * 512], start=True,
                                  stop=True).then_inc(v_psum.sem, 1)

                def tail_transposes(a, r):
                    if r == 0:
                        pe.wait_ge(on_done.sem, on_done.at(p, WH // 2 * (a + 1)))
                    if r >= 2:
                        pe.wait_ge(onT_done.sem, onT_done.at(p, 4 * a + r - 1))
                    for c in range(2):
                        for t in range(TPB):
                            k = 2 * r + c
                            m = pe.transpose(pr[r % 2][:, (2 * c + t) * P:(2 * c + t + 1) * P],
                                             on[a % 2][:, t, 2 * k:2 * k + 2, :].rearrange("p h c -> p (h c)"), g.ident[:, :])
                    m.then_inc(onT_psum.sem, 1)

                def tail_output(a):
                    pe.wait_ge(onT_done.sem, onT_done.at(p, 4 * a + 4))
                    for t in range(TPB):
                        for k in range(CH):
                            m = pe.matmul(pr[0][:, t * P:(t + 1) * P], onT[:, k, t * P:(t + 1) * P], w[("sa_wo", "ca_wo")[a // 2]][:, k, :],
                                          start=k == 0, stop=k == CH - 1)
                    m.then_inc(a_psum.sem, 1)

                def heads(a, tail):
                    i = a % 2
                    for h in range(WH + 2):
                        if h < WH:
                            if h % 4 == 0:
                                pe.wait_ge(q_done.sem, q_done.at(p, 4 * a + 4))
                                pe.wait_ge(k_done.sem, k_done.at(p, 4 * a + 4))
                            if h == 0:
                                pe.wait_ge(v_done.sem, v_done.at(p, 4 * a + 4))
                            if h >= 2:
                                pe.wait_ge(exp_done.sem, exp_done.at(p, WH * a + h - 1))
                            for t in range(TPB):
                                out = s1[h % 2][:, t * S:(t + 1) * S]
                                pe.matmul(out, qT[:, h // 2, t * P:(t + 1) * P], kTm[:, h, :], start=True, stop=False)
                                m = pe.matmul(out, g.ones_bf[0:1, 0:P], mb[:, 2 * p + i, :], start=False, stop=True)
                            m.then_inc(s1_psum.sem, 1)
                        if 1 <= h <= WH:
                            k = h - 1
                            pe.wait_ge(exp_done.sem, exp_done.at(p, WH * a + k + 1))
                            if k >= 2:
                                pe.wait_ge(pt_done.sem, pt_done.at(p, WH * a + k - 1))
                            for kt in range(TPB):
                                for t in range(TPB):
                                    m = pe.transpose(pt[k % 2][:, kt * S + t * P:kt * S + (t + 1) * P], prob[:, k % 2, t, kt * P:(kt + 1) * P],
                                                     g.ident[:, :])
                            m.then_inc(pt_psum.sem, 1)
                        if h >= 2:
                            k = h - 2
                            pe.wait_ge(pt_done.sem, pt_done.at(p, WH * a + k + 1))
                            pe.wait_ge(on_done.sem, on_done.at(p, WH // 2 * a + k // 2 - 1))
                            for t in range(TPB):
                                for kt in range(TPB):
                                    m = pe.matmul(ob[k // 2 % 2][:, t, k % 2, :], probT[:, k % 2, kt, t * P:(t + 1) * P], va[:, kt, k, :],
                                                  start=kt == 0, stop=kt == TPB - 1)
                            m.then_inc(av_done.sem, 1)
                        if tail:
                            if h in (2, 4):
                                tail_transposes(a - 1, h - 2)
                                tail_transposes(a - 1, h - 1)
                            if h == 6:
                                tail_output(a - 1)
                            if h == 12:
                                transposes(1 + a, (a - 1) % 2)

                for i in range(2):
                    transposes(i, i)
                for a in range(JOBS):
                    projections(a)
                    heads(a, a > 0)
                for r in range(4):
                    tail_transposes(JOBS - 1, r)
                tail_output(JOBS - 1)
                transposes(5, 1)
                for i in range(2):
                    pe.wait_ge(yT_done.sem, yT_done.at(p, 5 + i))
                    pe.wait_ge(exp_done.sem, exp_done.at(p))
                    pe.wait_ge(h_done.sem, h_done.at(p, 2 * i))
                    for k in range(FC):
                        m = pe.matmul(s1[k // 2][:, k % 2 * S:(k % 2 + 1) * S], w["fc1"][:, k * P:(k + 1) * P], yT[:, i, :], start=True, stop=True)
                        if k % 2:
                            m.then_inc(h_psum.sem, 1)
                    pe.wait_ge(h_done.sem, h_done.at(p, 2 * i + 2))
                    pe.wait_ge(pt_done.sem, pt_done.at(p))
                    for t in range(TPB):
                        for k in range(FC):
                            m = pe.matmul(pt[i][:, t * P:(t + 1) * P], hT[:, k, t * P:(t + 1) * P], w["fc2"][:, k, :], start=k == 0, stop=k == FC - 1)
                    m.then_inc(f_psum.sem, 1)


class Shared:
    pass


def rope_tables():
    half = DH // 2
    freq = (1.0 / 10000.0 ** (np.arange(half, dtype=np.float32) / half)).astype(np.float32)
    ang = np.arange(S, dtype=np.float32)[None, :] * np.tile(freq, 2 * H)[:, None]
    sign = np.tile(np.repeat(np.array([-1.0, 1.0], np.float32), half), H)[:, None]
    return np.cos(ang).astype(np.float32), (np.sin(ang) * sign).astype(np.float32)


def build(nc, ins, out, layers=range(12)):
    g = Shared()
    with ExitStack() as ctx:
        sb = lambda n, shape, dt=F32: ctx.enter_context(nc.sbuf_tensor(n, shape, dt))
        g.x = sb("x", [P, B, TPB * D])
        g.ident = sb("ident", [P, P])
        g.ident_bf = sb("ident_bf", [P, P], BF16)
        g.half = sb("half", [P, NT])
        g.rowmask = sb("rowmask", [P, H])
        g.sel = sb("sel", [2 * H, H, P], BF16)
        g.ones_bf = sb("ones_bf", [P, S], BF16)
        g.ones = sb("ones", [P, P])
        g.iota_e = sb("iota_e", [P, E])
        g.back_e = sb("back_e", [P, E])
        g.tri_q, g.tri_k = sb("tri_q", [P, P], BF16), sb("tri_k", [P, P], BF16)
        g.band_q, g.band_k = sb("band_q", [P, S], BF16), sb("band_k", [P, S], BF16)
        g.cosq, g.cosk, g.sinq, g.sink = (sb(n, [P, S]) for n in ("cosq", "cosk", "sinq", "sink"))
        g.ctxT_dram = ins["ctxT"]
        g.first_loads = [(g.x[:, :, :], ins["x"].rearrange("b (t p) d -> p b t d", p=P))] + [
            (t[:, :], ins[n]) for t, n in ((g.cosq, "cosq"), (g.cosk, "cosk"), (g.sinq, "sinq"), (g.sink, "sink"))]
        g.first_loads[0] = (g.x[:, :, :].rearrange("p b (t d) -> p b t d", t=TPB), g.first_loads[0][1])
        g.loaded = {"x": ctx.enter_context(nc.semaphore("x_loaded"))}
        g.weight_loads, g.n_loads = [], {}
        g.spare = ctx.enter_context(nc.semaphore("spare"))

        def weights(name, **shapes):
            w, pairs = {}, []
            for n, (src, shape) in shapes.items():
                w[n] = sb(f"w_{name}_{n}", shape)
                pairs.append((w[n][:], ins[src]))
            g.loaded[name] = ctx.enter_context(nc.semaphore(f"{name}_loaded"))
            g.weight_loads.append((name, pairs))
            g.n_loads[name] = len(pairs)
            return w

        dd, col = [P, D], [P, 1]
        w_l1a = weights("l1a", wq=("L1_attn_WqT", dd), wk=("L1_attn_WkT", dd), wqr=("L1_attn_WqrT", dd), wkr=("L1_attn_WkrT", dd),
                        wv=("L1_attn_WvT", dd), wo=("L1_attn_WoT", dd), bq=("L1_attn_bq", col), bk=("L1_attn_bk", col),
                        bqr=("L1_attn_bqr", col), bkr=("L1_attn_bkr", col), bv=("L1_attn_bv", dd), bo=("L1_attn_bo", dd))
        w_l1x, w_l3x = (weights(n, wq=(f"{L}_xattn_WqT", dd), wk=(f"{L}_xattn_WkT", dd), wv=(f"{L}_xattn_WvT", dd),
                                wo=(f"{L}_xattn_WoT", dd), bq=(f"{L}_xattn_bq", col), bk=(f"{L}_xattn_bk", col),
                                bv=(f"{L}_xattn_bv", dd), bo=(f"{L}_xattn_bo", dd)) for n, L in (("l1x", "L1"), ("l3x", "L3")))
        w_l2a = weights("l2a", wq=("L2_attn_Wq", dd), wk=("L2_attn_Wk", dd), wv=("L2_attn_Wv", dd), wo=("L2_attn_w_proj", dd),
                        decay=("L2_attn_decay", [P, H]))
        w_l3a = weights("l3a", wq=("L3_attn_WqT", dd), wk=("L3_attn_WkT", dd), wv=("L3_attn_WvT", dd), wo=("L3_attn_WoT", dd))
        area_a, area_b = sb("area_a", [P, 9216]), sb("area_b", [P, 6144])

        def parts(area, name, *shapes):
            got, at = [], 0
            g.loaded[name] = g.loaded.get(name) or ctx.enter_context(nc.semaphore(f"{name}_loaded"))
            pairs = []
            for src, shape in shapes:
                n = int(np.prod(shape))
                names = "abc"[:len(shape)]
                flat = area[:, at:at + n]
                dims = dict(zip(names, shape))
                t = flat.rearrange(f"p ({' '.join(names)}) -> p {' '.join(names)}", **dims)
                got.append(t)
                pairs.append((t, ins[src]))
                at += n
            g.n_loads[name] = g.n_loads.get(name, 0) + len(pairs)
            return got, [(d, s_, g.loaded[name]) for d, s_ in pairs]

        w_l0a = weights("l0a", w1=("L0_attn_gk_w1", [P, LOW]), w2=("L0_attn_gk_w2", [LOW, P]), b=("L0_attn_gk_b", col),
                        wo=("L0_attn_Wo", [P, 2, D]), rms=("L0_attn_rms_w", [P, GV_ALL]))
        w_l0x = weights("l0x", gq=("L0_xattn_gq", [P, 2 * MH]), gk=("L0_xattn_gk", [P, 2 * MH]), gv=("L0_xattn_gv", [P, 2 * MH]),
                        bias=("L0_xattn_bias", [2 * MH, 1]), outnorm=("L0_xattn_outnorm", [P, D]))
        g.ctx_loaded = ctx.enter_context(nc.semaphore("ctx_loaded"))
        g.parts_dram = [nc.dram_tensor(f"qk_parts{i}", [2, 3, DH, H, S], BF16, kind="Internal").ap() for i in range(2)]
        g.scratch = nc.dram_tensor("m_parts", [P, 3, P], BF16, kind="Internal").ap()
        w_l0f = weights("l0f", router=("L0_ffn_wg", [P, E]))
        w_l1f = weights("l1f", router=("L1_ffn_gate_w", [P, E]))
        w_l2f = weights("l2f", router=("L2_ffn_router_w", [P, E]), b_in=("L2_ffn_b_in", [P, E]), b_out=("L2_ffn_b_out", [P, D]))
        w_l3f = weights("l3f", router=("L3_ffn_Wg", [P, E]))
        (up0, w_l0f["down"]), load_l0f = parts(area_a, "l0f", ("L0_ffn_w_gate", (E, 512)), ("L0_ffn_w_down", (E, 4, D)))
        proj0, load_l0a = parts(area_a[:, 8192:9216], "l0a", *[(f"L0_attn_{n}", (m,)) for n, m in
                                                               (("Wq", D), ("Wk", D), ("Wv", GV_ALL), ("Wg", GV_ALL))])
        w_l0a.update(zip(("wq", "wk", "wv", "wg"), proj0))
        (g1, u1, w_l1f["down"]), load_l1f = parts(area_b, "l1f", ("L1_ffn_Wg", (E, 256)), ("L1_ffn_Wu", (E, 256)), ("L1_ffn_Wd", (E, 2, D)))
        (up2, w_l2f["down"]), load_l2f = parts(area_b, "l2f", ("L2_ffn_w_in", (E, 128)), ("L2_ffn_w_out", (E, 1, D)))
        (g3, u3, w_l3f["down"]), load_l3f = parts(area_a, "l3f", ("L3_ffn_W1", (E, 256)), ("L3_ffn_W2", (E, 256)), ("L3_ffn_W3", (E, 2, D)))
        rows = lambda *names: {n: (f"L2_xattn_{n}", dd) for n in names}
        w_l2x = weights("l2x", fc1_b=("L2_xattn_fc1_b", [P, WFF // P]),
                        **rows("sa_bo", "ca_bo", "fc2_b", "ln1_g", "ln1_b", "ln2_g", "ln2_b", "ln3_g", "ln3_b"))
        big = ["sa_wq", "sa_wk", "sa_wv", "ca_wq", "ca_wk", "ca_wv"]
        got, load_l2x = parts(area_a, "l2x", *[(f"L2_xattn_{n}", (INNER,)) for n in big], ("L2_xattn_fc1", (WFF,)),
                              ("L2_xattn_sa_wo", (INNER // P, D)), ("L2_xattn_ca_wo", (INNER // P, D)), ("L2_xattn_fc2", (WFF // P, D)))
        w_l2x.update(zip(big + ["fc1", "sa_wo", "ca_wo", "fc2"], got))
        w_l0f["up"], w_l1f["up"], w_l2f["up"], w_l3f["up"] = [up0], [g1, u1], [up2], [g3, u3]
        loads = {"l0a": (0, None, load_l0a), "l0f": (2, None, load_l0f), "l1f": (5, None, load_l1f), "l2x": (7, 3, load_l2x), "l2f": (8, 6, load_l2f),
                 "l3f": (11, 8, load_l3f)}
        g.first_area_loads = [l for user, at, ls in loads.values() if user in layers and at not in layers for l in ls]
        constants(nc, g)
        for n in layers:
            fetch = [l for user, at, ls in loads.values() if at == n and user in layers for l in ls]
            with nc.cleanup_on_exit():
                if n == 0:
                    gated_linear(nc, g, "l0a", w_l0a)
                if n == 1:
                    matrix_lstm(nc, g, "l0x", w_l0x, ins["ctx"])
                if n == 2:
                    experts(nc, g, "l0f", w_l0f, 512, ACT.Gelu, False, "capacity")
                if n == 3:
                    attention(nc, g, "l1a", w_l1a, rope=True, window=WINDOW, prefetch=fetch)
                if n == 4:
                    attention(nc, g, "l1x", w_l1x, cross=True, key_mask=ins["key_mask"])
                if n == 5:
                    experts(nc, g, "l1f", w_l1f, 256, ACT.Silu, True, "choice")
                if n == 6:
                    attention(nc, g, "l2a", w_l2a, causal=True, alibi=True, prefetch=fetch)
                if n == 7:
                    decoder(nc, g, "l2x", w_l2x, ins["bool_mask"])
                if n == 8:
                    experts(nc, g, "l2f", w_l2f, 128, ACT.Gelu_apprx_tanh, False, "probs", biased=True, prefetch=fetch)
                if n == 9:
                    attention(nc, g, "l3a", w_l3a, causal=True)
                if n == 10:
                    attention(nc, g, "l3x", w_l3x, cross=True, full_mask=(ins["mask_q"], ins["mask_k"]))
                if n == 11:
                    experts(nc, g, "l3f", w_l3f, 256, ACT.Silu, True, "pair")

        stored = ctx.enter_context(nc.semaphore("stored"))
        block = ctx.enter_context(nc.Block())

        @block.sync
        def _(sp):
            sp.dma_start(out.rearrange("b (t p) d -> p b t d", p=P),
                         g.x[:, :, :].rearrange("p b (t d) -> p b t d", t=TPB)).then_inc(stored, 16)
            sp.wait_ge(stored, 16)


def layout(i):
    a = {"x": i["x"]}
    a["ctx"] = i["ctx_1024"]
    for n in ("Wq", "Wk", "Wv", "Wg", "gk_w1", "gk_w2"):
        a[f"L0_attn_{n}"] = i[f"L0_attn_{n}"]
    a["L0_attn_gk_b"] = i["L0_attn_gk_b"].reshape(P, 1)
    a["L0_attn_Wo"] = i["L0_attn_Wo"].reshape(2, P, D).transpose(1, 0, 2)
    a["L0_attn_rms_w"] = np.tile(i["L0_attn_rms_w"], (P, GH))
    for n, o in (("gq", 0), ("gk", D), ("gv", 2 * D)):
        a[f"L0_xattn_{n}"] = i["L0_xattn_ifgate_w"][:, o:o + D].T
    a["L0_xattn_bias"] = i["L0_xattn_ifgate_b"].reshape(2 * MH, 1)
    a["L0_xattn_outnorm"] = np.repeat(i["L0_xattn_outnorm_w"].reshape(1, D), P, 0)
    a["ctxT"] = np.transpose(i["ctx_1024"], (2, 0, 1))
    cos, sin = rope_tables()
    scale = np.float32(DH ** -0.5)
    a["cosq"], a["cosk"], a["sinq"], a["sink"] = cos * scale, cos, sin * scale, sin
    swap = np.arange(D).reshape(H, 2, DH // 2)[:, ::-1].reshape(D)
    rows = lambda v: np.repeat(v.reshape(1, -1), P, 0)
    for L, kind in (("L1", "attn"), ("L1", "xattn"), ("L3", "xattn")):
        for n in "qkvo":
            a[f"{L}_{kind}_W{n}T"] = i[f"{L}_{kind}_W{n}"].T
        for n in "qk":
            a[f"{L}_{kind}_b{n}"] = i[f"{L}_{kind}_b{n}"].reshape(D, 1)
        for n in "vo":
            a[f"{L}_{kind}_b{n}"] = rows(i[f"{L}_{kind}_b{n}"])
    for n in "qk":
        a[f"L1_attn_W{n}rT"] = i[f"L1_attn_W{n}"][swap].T
        a[f"L1_attn_b{n}r"] = i[f"L1_attn_b{n}"][swap].reshape(D, 1)
    for k, n in enumerate("qkv"):
        a[f"L2_attn_W{n}"] = i["L2_attn_w_attn"][:, k * D:(k + 1) * D]
        a[f"L3_attn_W{n}T"] = i["L3_attn_in_proj_weight"][k * D:(k + 1) * D].T
    a["L2_attn_w_proj"] = i["L2_attn_w_proj"]
    a["L3_attn_WoT"] = i["L3_attn_out_proj_weight"].T
    for n, src in (("L0_ffn_w_gate", 0), ("L1_ffn_Wg", 0), ("L1_ffn_Wu", 0), ("L2_ffn_w_in", 0), ("L3_ffn_W1", 0), ("L3_ffn_W2", 0)):
        a[n] = i[n].transpose(1, 0, 2)
    for n in ("L0_ffn_w_down", "L1_ffn_Wd", "L2_ffn_w_out", "L3_ffn_W3"):
        a[n] = i[n].reshape(E, -1, P, D).transpose(2, 0, 1, 3)
    for n in ("L0_ffn_wg", "L1_ffn_gate_w", "L2_ffn_router_w", "L3_ffn_Wg"):
        a[n] = i[n]
    a["L2_ffn_b_in"] = i["L2_ffn_b_in"].T
    a["L2_ffn_b_out"] = np.tile(i["L2_ffn_b_out"], (NT, 1))
    a["L2_attn_decay"] = rows(i["L2_attn_decay_raw"])
    for n in ("sa", "ca"):
        for k in ("wq", "wk", "wv"):
            a[f"L2_xattn_{n}_{k}"] = i[f"L2_xattn_{n}_{k}"]
        a[f"L2_xattn_{n}_wo"] = i[f"L2_xattn_{n}_wo"].reshape(-1, P, D).transpose(1, 0, 2)
    a["L2_xattn_fc1"] = i["L2_xattn_fc1_w"]
    a["L2_xattn_fc2"] = i["L2_xattn_fc2_w"].reshape(-1, P, D).transpose(1, 0, 2)
    a["L2_xattn_fc1_b"] = i["L2_xattn_fc1_b"].reshape(-1, P).T
    for n in ("sa_bo", "ca_bo", "fc2_b", "ln1_g", "ln1_b", "ln2_g", "ln2_b", "ln3_g", "ln3_b"):
        a[f"L2_xattn_{n}"] = rows(i[f"L2_xattn_{n}"])
    a["bool_mask"] = i["mask_BxS2_bk0"].reshape(1, B * S)
    a["key_mask"] = i["mask_Bx1x1xS2_if1"].reshape(1, B * S)
    m = i["mask_BxSxS2_if1"]
    a["mask_q"] = m.reshape(B, TPB, P, S).transpose(0, 2, 1, 3)
    a["mask_k"] = m.transpose(0, 2, 1).reshape(B, TPB, P, S).transpose(0, 2, 1, 3)
    return {k: np.ascontiguousarray(v) for k, v in a.items()}


def kernel(**inputs):
    import concourse.bacc as bacc
    from concourse.bass_utils import run_bass_kernel_spmd

    arrays = layout({n: np.asarray(v) for n, v in inputs.items()})
    nc = bacc.Bacc("TRN2", target_bir_lowering=False, num_devices=1)
    ins = {n: nc.dram_tensor(f"in_{n}", a.shape, mybir.dt.from_np(a.dtype), kind="ExternalInput").ap() for n, a in arrays.items()}
    out = nc.dram_tensor("out", (B, S, D), F32, kind="ExternalOutput").ap()
    build(nc, ins, out)
    r = run_bass_kernel_spmd(nc, [{f"in_{n}": a for n, a in arrays.items()}], core_ids=[0])
    return r.results[0]["out"]
```

```python
from contextlib import ExitStack

import numpy as np

import concourse.bass as bass
from concourse import mybir

P = 128
B, S, D = 8, 256, 128
NT = B * S // P
TPB = S // P
H, DH = 16, 8
HP = 32
WINDOW = 128
E = 8
LN_EPS = 1e-5
NEG = -1e30

F32 = mybir.dt.float32
BF16 = mybir.dt.bfloat16
I32 = mybir.dt.int32
U32 = mybir.dt.uint32
ALU = mybir.AluOpType
ACT = mybir.ActivationFunctionType
AX = mybir.AxisListType


class Count:

    def __init__(self, nc, name, per=1):
        self.sem = nc.alloc_semaphore(name)
        self.per = per

    def at(self, b, k=None):
        if isinstance(b, int):
            b = max(b, -1)
        return (b + 1) * self.per + (self.per if k is None else k)


def start(e, counts):
    for c in counts:
        e.sem_inc(c.sem, c.per)


def constants(nc, g):
    with ExitStack() as ctx:
        made = nc.alloc_semaphore("const_made")
        copied = nc.alloc_semaphore("const_copied")
        loaded = g.loaded["x"]
        block = ctx.enter_context(nc.Block())

        @block.sync
        def _(sp):
            sp.dma_start(*g.x_load).then_inc(loaded, 16)
            for dst, src, s in g.first_loads:
                sp.dma_start(dst, src).then_inc(s, 16)
            sp.wait_ge(loaded, 16)

        @block.gpsimd
        def _(pool):
            pool.memset(g.ident[:, :], 0.0).then_inc(made, 1)
            pool.memset(g.half[:, :], -0.5).then_inc(made, 1)
            pool.memset(g.rowmask[:, :], 1.0).then_inc(made, 1)
            pool.memset(g.sel[:, :, :], 0.0).then_inc(made, 1)
            pool.memset(g.ones_bf[:, :], 1.0).then_inc(made, 1)
            pool.memset(g.ones[:, :], 1.0).then_inc(made, 1)
            pool.wait_ge(made, 6)
            pool.affine_select(out=g.ident[:, :], in_=g.ident[:, :], compare_op=ALU.not_equal, fill=1.0,
                               base=0, pattern=[[-1, P]], channel_multiplier=1).then_inc(made, 1)
            pool.affine_select(out=g.rowmask[:, :], in_=g.rowmask[:, :], compare_op=ALU.is_ge, fill=0.0,
                               base=0, pattern=[[-DH, H]], channel_multiplier=1).then_inc(made, 1)
            pool.wait_ge(made, 8)
            pool.affine_select(out=g.rowmask[:, :], in_=g.rowmask[:, :], compare_op=ALU.is_ge, fill=0.0,
                               base=DH - 1, pattern=[[DH, H]], channel_multiplier=-1).then_inc(made, 1)
            pool.affine_select(out=g.sel[:, :, :], in_=g.sel[:, :, :], compare_op=ALU.not_equal, fill=1.0,
                               base=0, pattern=[[-1, H], [0, P]], channel_multiplier=1).then_inc(made, 1)
            pool.wait_ge(made, 10)
            pool.affine_select(out=g.sel[:, :, :], in_=g.sel[:, :, :], compare_op=ALU.not_equal, fill=1.0,
                               base=-H, pattern=[[-1, H], [0, P]], channel_multiplier=1).then_inc(made, 1)
            pool.iota(g.iota_e[:, :], pattern=[[1, E]], base=0, channel_multiplier=0,
                      allow_small_or_imprecise_dtypes=True).then_inc(made, 1)
            pool.iota(g.back_e[:, :], pattern=[[-1, E]], base=E, channel_multiplier=0,
                      allow_small_or_imprecise_dtypes=True)
            for m in (g.tri_q, g.tri_k, g.band_q, g.band_k):
                pool.memset(m[:, :], 0.0).then_inc(made, 1)
            pool.wait_ge(made, 16)
            pool.affine_select(out=g.tri_q[:, :], in_=g.tri_q[:, :], compare_op=ALU.is_ge, fill=NEG,
                               base=0, pattern=[[-1, P]], channel_multiplier=1).then_inc(made, 1)
            pool.affine_select(out=g.tri_k[:, :], in_=g.tri_k[:, :], compare_op=ALU.is_ge, fill=NEG,
                               base=0, pattern=[[1, P]], channel_multiplier=-1).then_inc(made, 1)
            pool.affine_select(out=g.band_q[:, :], in_=g.band_q[:, :], compare_op=ALU.is_ge, fill=NEG,
                               base=P, pattern=[[-1, S]], channel_multiplier=1).then_inc(made, 1)
            pool.affine_select(out=g.band_k[:, :], in_=g.band_k[:, :], compare_op=ALU.is_ge, fill=NEG,
                               base=0, pattern=[[1, S]], channel_multiplier=-1).then_inc(made, 1)
            pool.wait_ge(made, 20)
            pool.affine_select(out=g.band_q[:, :], in_=g.band_q[:, :], compare_op=ALU.is_ge, fill=NEG,
                               base=WINDOW - P, pattern=[[1, S]], channel_multiplier=-1).then_inc(made, 1)
            pool.affine_select(out=g.band_k[:, :], in_=g.band_k[:, :], compare_op=ALU.is_ge, fill=NEG,
                               base=WINDOW, pattern=[[-1, S]], channel_multiplier=1).then_inc(made, 1)
            pool.wait_ge(made, 22)

        @block.vector
        def _(dve):
            dve.wait_ge(made, 12)
            dve.tensor_copy(g.ident_bf[:, :], g.ident[:, :]).then_inc(copied, 1)
            dve.wait_ge(copied, 1)


KROWS = 3 * 3 * DH
MASK_ROW = 96


def attention(nc, g, name, w, cross=False, rope=False, window=None, causal=False, alibi=False,
              key_mask=None, full_mask=None, prefetch=()):
    scale = DH ** -0.5
    causal = causal or window is not None
    KC = 384 if causal else 512
    biased = "bq" in w
    HH = H // 2
    with ExitStack() as ctx:
        sb = lambda n, shape, dt=F32: ctx.enter_context(nc.sbuf_tensor(f"{name}_{n}", shape, dt))
        ps = lambda n, shape, dt=F32: ctx.enter_context(nc.psum_tensor(f"{name}_{n}", shape, dt))
        count = lambda n, per=1: Count(nc, f"{name}_{n}", per)
        xn = sb("xn", [P, TPB, D])
        xnT = sb("xnT", [P, S])
        ctxT = sb("ctxT", [P, 2, S]) if cross else None
        stats = sb("stats", [P, TPB, 6])
        mv = sb("mv", [P, TPB, 2])
        var_eps = sb("var_eps", [P, TPB])
        rstd = sb("rstd", [P, TPB])
        qk = sb("qk", [P, 2, S])
        parts = [sb(f"parts{i}", [P, 2, 3, S], BF16) for i in range(2)]
        stack = [sb(f"stack{i}", [P, 2, H, S], BF16) for i in range(2)]
        scratch = [g.parts_dram[i] for i in range(2)]
        rot = sb("rot", [P, 4, S]) if rope else None
        vt = sb("vt", [P, TPB, H, DH])
        va = [sb(f"va{i}", [P, TPB, H, HP]) for i in range(2)]
        negm = sb("negm", [P, TPB, H])
        mparts = sb("mparts", [P, TPB, 2, H], BF16)
        mT = [sb(f"mT{i}", [2 * H, S], BF16) for i in range(2)]
        prob = sb("prob", [P, 8, KC])
        u = sb("u", [P, 4, S])
        rz = sb("rz", [P, TPB, H])
        on = sb("on", [P, TPB, H, DH])
        onT = sb("onT", [P, S])
        if full_mask is not None:
            mi = [sb(f"mi{k}", [P, 2, S], I32) for k in range(2)]
            mb = [[sb(f"mb{k}{i}", [P, 2, S], BF16) for i in range(2)] for k in range(2)]
        if key_mask is not None:
            kmi = sb("kmi", [1, B * S], I32)
            kmb = sb("kmb", [1, B * S], BF16)
        if alibi:
            flat, room = prob[:, :, :].rearrange("p a b -> p (a b)"), iter(range(0, 12 * S, S))
            two = lambda: flat[:, next(room):next(room) + S].rearrange("p (k s) -> p k s", k=2)
            one = lambda: flat[:, next(room):][:, 0:S].unsqueeze(1)
            dist, dist0, logd, dmask, altmp = two(), two(), two(), one(), one()
            logw = flat[:, 8 * S:12 * S].rearrange("p (h k s) -> p h k s", h=2, k=2)
            decay = sb("decay", [P, 2, H])
            al = sb("al", [P, 2, H, S], BF16)
            alw = sb("alw", [P, H, S])
        s1 = [ps(f"s1_{i}", [P, 512]) for i in range(2)]
        s2 = [ps(f"s2_{i}", [P, 512]) for i in range(2)]
        up = ps("up", [P, 4, S])
        pa = ps("pa", [P, 512])
        pb = ps("pb", [P, 512])
        mTp = pa[:, 0:S].bitcast(BF16)
        ut = up[:, :, :].rearrange("p (t a) (h c) -> p t (a h) c", t=TPB, c=HP)

        EV = 6 if rope else 2
        LATE = 5 if rope else 4
        ln_step = count("ln_step", 6)
        rstd_done = count("rstd_done")
        xnT_psum = count("xnT_psum")
        xnT_done = count("xnT_done")
        proj = count("proj", 2 if rope else 1)
        v_psum = count("v_psum")
        qk_done = count("qk_done", EV + 4)
        v_done = count("v_done")
        va_done = count("va_done")
        s1_done = count("s1_done", H)
        max_done = count("max_done", H)
        mparts_done = count("mparts_done", 2)
        mT_psum = count("mT_psum")
        mT_done = count("mT_done")
        s2_done = count("s2_done", H)
        exp_done = count("exp_done", H)
        av_done = count("av_done", 4)
        u_done = count("u_done", 2)
        ut_psum = count("ut_psum")
        on_step = count("on_step", 2)
        onT_psum = count("onT_psum")
        onT_done = count("onT_done")
        y_psum = count("y_psum")
        x_done = count("x_done")
        bo_done = count("bo_done")
        ctx_in, parts_out = ([nc.alloc_semaphore(f"{name}_{n}{i}") for i in range(2)] for n in ("ctx_in", "parts_out"))
        stack_in = [[nc.alloc_semaphore(f"{name}_stack_in{i}{j}") for j in range(2)] for i in range(2)]
        STACK_DMAS = 4 + (key_mask is not None)
        mask_in = [count(f"mask_in{k}", 16) for k in range(2)]
        mask_done = [count(f"mask_done{k}") for k in range(2)]
        setup = nc.alloc_semaphore(f"{name}_setup")
        setup_v = nc.alloc_semaphore(f"{name}_setup_v")
        setup_a = nc.alloc_semaphore(f"{name}_setup_a")
        setup_p = nc.alloc_semaphore(f"{name}_setup_p")
        setup_d = nc.alloc_semaphore(f"{name}_setup_d")
        POOL_HEADS = range(2, H, 3)
        w_done, wp_done = count("w_done", H - len(POOL_HEADS)), count("wp_done", len(POOL_HEADS))

        def weigh(e, done, b, h):
            e.wait_ge(exp_done.sem, exp_done.at(b, h + 1))
            e.tensor_tensor(prob[:, h % 8, 0:S], prob[:, h % 8, 0:S], alw[:, h, :], ALU.mult)
            e.tensor_tensor(prob[:, h % 8, S:KC], prob[:, h % 8, S:KC], alw[:, h, 0:P], ALU.mult).then_inc(done.sem, 1)

        block = ctx.enter_context(nc.Block())
        n_w = g.n_loads[name]
        SETUP = 4 + (key_mask is not None)

        def turns(e, first, body, last):
            first()
            body(0, 0, False, True, True)
            body(1, 1, True, True, True)
            with e.Fori(2, B - 3, 2) as b:
                body(b, 0, True, True, True)
                body(b + 1, 1, True, True, True)
            body(B - 2, 0, True, True, False)
            body(B - 1, 1, True, False, False)
            last()

        def ahead(h):
            return range(4 * h // 3, min(4 * (h + 1) // 3, H))

        @block.sync
        def _(sp):
            if key_mask is not None:
                sp.dma_start(kmi[:, :], key_mask).then_inc(setup_d, 16)
            for dst, src, s in prefetch:
                sp.dma_start(dst, src).then_inc(s, 16)

            def context(b, i):
                sp.wait_ge(v_psum.sem, v_psum.at(b - 2))
                sp.dma_start(ctxT[:, i, :], g.ctxT_dram[:, b, :]).then_inc(ctx_in[i], 16)

            def load_mask(b, k):
                sp.wait_ge(mask_done[k].sem, mask_done[k].at(b - 1))
                sp.dma_start(mi[k][:, :, :], full_mask[k][b]).then_inc(mask_in[k].sem, 16)

            def stacks(b, i, more):
                for a in range(3):
                    sp.wait_ge(qk_done.sem, qk_done.at(b, EV + (1, 3, 4)[a]))
                    for x in range(2):
                        sp.dma_start(scratch[i][x, a].rearrange("c h s -> h c s"), parts[i][:, x, a, :]).then_inc(parts_out[i], 16)
                if cross and more:
                    context(b + 2, i)
                sp.wait_ge(parts_out[i], 48 * (b - i) + 96)
                for j in range(2):
                    heads = slice(j * HH, (j + 1) * HH)
                    sp.wait_ge(s2_done.sem, s2_done.at(b - 2, (j + 1) * HH))
                    for a in range(3):
                        sp.dma_start(stack[i][a * 3 * DH:(a + 1) * 3 * DH, 0, heads, :].rearrange("r h s -> r (h s)"),
                                     scratch[i][0, a, :, heads, :].rearrange("c h s -> c (h s)").unsqueeze(0).to_broadcast([3, DH, HH * S])
                                     ).then_inc(stack_in[i][j], 16)
                    sp.dma_start(stack[i][0:KROWS, 1, heads, :].rearrange("r h s -> r (h s)"),
                                 scratch[i][1, :, :, heads, :].rearrange("a c h s -> (a c) (h s)").unsqueeze(0).to_broadcast([3, 3 * DH, HH * S])
                                 ).then_inc(stack_in[i][j], 16)
                    if key_mask is not None:
                        sp.dma_start(stack[i][MASK_ROW:MASK_ROW + 1, 1, heads, :],
                                     kmb[:, :].rearrange("p (b s) -> p b s", b=B)[:, b, :].unsqueeze(1).to_broadcast([1, HH, S])
                                     ).then_inc(stack_in[i][j], 16)
                if full_mask is not None:
                    if not (isinstance(b, int) and b + 1 == B):
                        load_mask(b + 1, 0)
                    load_mask(b, 1)

            start(sp, mask_in)
            if full_mask is not None:
                load_mask(0, 0)
            if cross:
                context(0, 0)
                context(1, 1)
            sp.wait_ge(setup, SETUP)
            if key_mask is not None:
                sp.wait_ge(setup_v, 1)
            stacks(0, 0, True)
            stacks(1, 1, True)
            with sp.Fori(2, B - 3, 2) as b:
                stacks(b, 0, True)
                stacks(b + 1, 1, True)
            stacks(B - 2, 0, False)
            stacks(B - 1, 1, False)

        @block.gpsimd
        def _(pool):
            start(pool, [rstd_done, va_done, bo_done, wp_done, *mask_done])
            pool.wait_ge(g.loaded[name], 16 * n_w)

            def buffers():
                for i in range(2):
                    pool.memset(stack[i][:, :, :, :].rearrange("p x h s -> p (x h s)").bitcast(F32), 0.0).then_inc(setup, 1)
                if key_mask is not None:
                    pool.wait_ge(setup, 2)
                    for i in range(2):
                        m = pool.memset(stack[i][MASK_ROW:MASK_ROW + 1, 0, :, :], 1.0)
                    m.then_inc(setup, 1)
                    pool.wait_ge(setup, 3)
                for i in range(2):
                    pool.memset(va[i][:, :, :, :], 0.0).then_inc(setup, 1)
                pool.wait_ge(setup, SETUP)
                for i in range(2):
                    m = pool.memset(va[i][:, :, :, DH:2 * DH], 1.0)
                m.then_inc(setup, 1)
                if alibi:
                    pool.iota(dist[:, 0, :], pattern=[[-1, S]], base=P, channel_multiplier=1,
                              allow_small_or_imprecise_dtypes=True).then_inc(setup, 1)
                    pool.iota(dist[:, 1, :], pattern=[[1, S]], base=0, channel_multiplier=-1,
                              allow_small_or_imprecise_dtypes=True).then_inc(setup, 1)

            def rstds(b):
                pool.wait_ge(ln_step.sem, ln_step.at(b, 5))
                pool.tensor_tensor(rstd[:, :], var_eps[:, :], g.half[:, 0:TPB], ALU.pow).then_inc(rstd_done.sem, 1)

            def mask(b, i, k):
                pool.wait_ge(mask_in[k].sem, mask_in[k].at(b))
                pool.sem_inc(g.spare, 1)
                done = (s1_done, s2_done)[k]
                pool.wait_ge(done.sem, done.at(b - 2))
                pool.sem_inc(g.spare, 1)
                pool.tensor_scalar(mb[k][i][:, :, :], mi[k][:, :, :], 0.0, -1e9, ALU.is_equal, ALU.mult).then_inc(mask_done[k].sem, 1)

            def values(b, i):
                pool.wait_ge(v_done.sem, v_done.at(b))
                pool.sem_inc(g.spare, 1)
                pool.wait_ge(av_done.sem, av_done.at(b - 2))
                pool.sem_inc(g.spare, 1)
                pool.tensor_copy(va[i][:, :, :, 0:DH], vt[:, :, :, :]).then_inc(va_done.sem, 1)

            def first():
                rstds(0)
                buffers()
                values(0, 0)
                rstds(1)
                values(1, 1)
                if alibi:
                    pool.wait_ge(setup_a, 5)
                    for h in range(H):
                        if h >= 2:
                            pool.wait_ge(setup_v, 3 + 4 * (h - 1))
                        pool.tensor_scalar(logw[:, h % 2, 1, :], logd[:, 1, :], decay[:, 1, h:h + 1], 1.0, ALU.mult, ALU.add).then_inc(setup_p, 1)
                if full_mask is not None:
                    mask(0, 0, 0)
                    mask(1, 1, 0)
                    mask(0, 0, 1)

            def body(b, i, prev, more1, more2):
                if more2:
                    rstds(b + 2)
                if biased:
                    pool.tensor_tensor(g.x[:, b, :].rearrange("p (t d) -> p t d", t=TPB),
                                       g.x[:, b, :].rearrange("p (t d) -> p t d", t=TPB),
                                       w["bo"][:, :].unsqueeze(1).to_broadcast([P, TPB, D]),
                                       ALU.add).then_inc(bo_done.sem, 1)
                if full_mask is not None:
                    if more1:
                        mask(b + 1, 1 - i, 1)
                    if more2:
                        mask(b + 2, i, 0)
                if alibi:
                    for h in POOL_HEADS:
                        weigh(pool, wp_done, b, h)
                if more2:
                    values(b + 2, i)

            turns(pool, first, body, lambda: None)

        @block.vector
        def _(dve):
            start(dve, [ln_step, qk_done, v_done, max_done, mparts_done, mT_done, on_step, x_done, w_done])
            dve.wait_ge(g.loaded[name], 16 * n_w)
            if key_mask is not None:
                dve.wait_ge(setup_d, 16)
                dve.tensor_scalar(kmb[:, :], kmi[:, :], 0.0, NEG, ALU.is_equal, ALU.mult).then_inc(setup_v, 1)

            def distances():
                dve.wait_ge(setup_a, 3)
                dve.scalar_tensor_tensor(out=decay[:, 1, :], in0=w["decay"][:, :], scalar=0.0, in1=decay[:, 0, :],
                                         op0=ALU.max, op1=ALU.add).then_inc(setup_v, 1)
                dve.wait_ge(setup, SETUP + 3)
                dve.tensor_scalar(dist0[:, :, :], dist[:, :, :], 0.0, None, ALU.max).then_inc(setup_v, 1)
                dve.tensor_scalar(dmask[:, :, :], dist[:, 0:1, :], 0.0, NEG, ALU.is_lt, ALU.mult).then_inc(setup_v, 1)

            def position_bias(h):
                dve.wait_ge(setup_a, 5 + h + 1)
                if h >= 1:
                    dve.wait_ge(setup_v, 3 + 4 * h)
                dve.scalar_tensor_tensor(out=altmp[:, 0, :], in0=logw[:, h % 2, 0, :], scalar=-1.0, in1=dmask[:, 0, :],
                                         op0=ALU.mult, op1=ALU.add).then_inc(setup_v, 1)
                dve.wait_ge(setup_v, 3 + 4 * h + 1)
                dve.tensor_copy(al[:, 0, h, :], altmp[:, 0, :]).then_inc(setup_v, 1)
                dve.wait_ge(setup_v, 3 + 4 * h + 2)
                dve.tensor_tensor(al[:, 1, h, :], altmp[:, 0, :], al[:, 0, h, :], ALU.subtract).then_inc(setup_v, 1)
                dve.wait_ge(setup_p, h + 1)
                dve.reciprocal(alw[:, h, :], logw[:, h % 2, 1, :]).then_inc(setup_v, 1)

            def layer_norm(b):
                xb = lambda t: g.x[:, b, t * D:(t + 1) * D]
                for t in range(TPB):
                    dve.bn_stats(stats[:, t, :], xb(t)).then_inc(ln_step.sem, 1)
                dve.wait_ge(ln_step.sem, ln_step.at(b, 2))
                dve.sem_inc(g.spare, 1)
                for t in range(TPB):
                    dve.bn_aggr(mv[:, t, :], stats[:, t, :]).then_inc(ln_step.sem, 1)
                dve.wait_ge(ln_step.sem, ln_step.at(b, 4))
                dve.tensor_scalar(var_eps[:, :], mv[:, :, 1], LN_EPS, None, ALU.add).then_inc(ln_step.sem, 1)

            def normalised(b):
                xb = lambda t: g.x[:, b, t * D:(t + 1) * D]
                dve.wait_ge(rstd_done.sem, rstd_done.at(b))
                dve.wait_ge(xnT_psum.sem, xnT_psum.at(b - 1))
                for t in range(TPB):
                    m = dve.tensor_scalar(xn[:, t, :], xb(t), mv[:, t, 0:1], rstd[:, t:t + 1], ALU.subtract, ALU.mult)
                m.then_inc(ln_step.sem, 1)

            def projections(b, stage=0):
                if stage == 1:
                    rotated(b)
                    return
                dve.wait_ge(proj.sem, proj.at(b, 1))
                dve.wait_ge(qk_done.sem, qk_done.at(b - 1))
                if rope:
                    for k, (bias, table) in enumerate([(w["bq"], g.cosq), (w["bk"], g.cosk)]):
                        dve.scalar_tensor_tensor(out=rot[:, k, :], in0=pa[:, k * S:(k + 1) * S], scalar=bias[:, 0:1], in1=table[:, :],
                                                 op0=ALU.add, op1=ALU.mult).then_inc(qk_done.sem, 1)
                else:
                    bias = (w["bq"][:, 0:1], w["bk"][:, 0:1]) if biased else (0.0, 0.0)
                    dve.tensor_scalar(qk[:, 0, :], pa[:, 0:S], bias[0], scale, ALU.add, ALU.mult).then_inc(qk_done.sem, 1)
                    dve.tensor_scalar(qk[:, 1, :], pa[:, S:2 * S], bias[1], None, ALU.add).then_inc(qk_done.sem, 1)

            def rotated(b):
                if rope:
                    dve.wait_ge(proj.sem, proj.at(b, 2))
                    for k, (bias, table) in enumerate([(w["bqr"], g.sinq), (w["bkr"], g.sink)]):
                        dve.scalar_tensor_tensor(out=rot[:, 2 + k, :], in0=pa[:, k * S:(k + 1) * S], scalar=bias[:, 0:1], in1=table[:, :],
                                                 op0=ALU.add, op1=ALU.mult).then_inc(qk_done.sem, 1)
                    dve.wait_ge(qk_done.sem, qk_done.at(b, 4))
                    dve.tensor_tensor(qk[:, :, :], rot[:, 0:2, :], rot[:, 2:4, :], ALU.add).then_inc(qk_done.sem, 2)

            def projected_v(b):
                dve.wait_ge(v_psum.sem, v_psum.at(b))
                dve.wait_ge(va_done.sem, va_done.at(b - 1))
                v = pb[:, S:2 * S].rearrange("p (t h c) -> p t h c", t=TPB, h=H)
                if biased:
                    dve.tensor_tensor(vt[:, :, :, :], v, w["bv"][:, :].rearrange("p (h c) -> p h c", h=H).unsqueeze(1).to_broadcast([P, TPB, H, DH]),
                                      ALU.add).then_inc(v_done.sem, 1)
                else:
                    dve.tensor_scalar(vt[:, :, :, :], v, 1.0, None, ALU.mult).then_inc(v_done.sem, 1)

            def split(b, i, k):
                if k == 0:
                    dve.wait_ge(s1_done.sem, s1_done.at(b - 2))
                dve.wait_ge(qk_done.sem, qk_done.at(b, EV + k))
                p = parts[i]
                if k % 2 == 0:
                    m = dve.tensor_scalar(p[:, :, k // 2, :], qk[:, :, :], 1.0, None, ALU.mult)
                elif k == 1:
                    m = dve.tensor_tensor(qk[:, :, :], qk[:, :, :], p[:, :, 0, :], ALU.subtract)
                else:
                    m = dve.tensor_tensor(p[:, :, 2, :], qk[:, :, :], p[:, :, 1, :], ALU.subtract)
                m.then_inc(qk_done.sem, 1)

            def maximum(b, h):
                dve.wait_ge(s1_done.sem, s1_done.at(b, h + 1))
                if causal:
                    dve.tensor_reduce(negm[:, 0, h:h + 1], s1[h % 2][:, 0:P], AX.X, ALU.max, negate=True)
                    m = dve.tensor_reduce(negm[:, 1, h:h + 1], s1[h % 2][:, P:KC], AX.X, ALU.max, negate=True)
                else:
                    m = dve.tensor_reduce(negm[:, :, h], s1[h % 2][:, :].rearrange("p (t c) -> p t c", t=TPB),
                                          AX.X, ALU.max, negate=True)
                m.then_inc(max_done.sem, 1)

            def maxima_parts(b):
                dve.wait_ge(max_done.sem, max_done.at(b))
                dve.tensor_scalar(mparts[:, :, 0, :], negm[:, :, :], 1.0, None, ALU.mult).then_inc(mparts_done.sem, 1)
                dve.wait_ge(mparts_done.sem, mparts_done.at(b, 1))
                dve.tensor_tensor(mparts[:, :, 1, :], negm[:, :, :], mparts[:, :, 0, :], ALU.subtract).then_inc(mparts_done.sem, 1)

            def maxima_out(b, i):
                dve.wait_ge(mT_psum.sem, mT_psum.at(b))
                dve.tensor_scalar(mT[i][:, :], mTp[0:2 * H, 0:S], 1.0, None, ALU.mult).then_inc(mT_done.sem, 1)

            def outputs(b):
                dve.wait_ge(ut_psum.sem, ut_psum.at(b))
                dve.reciprocal(rz[:, :, :], ut[:, :, :, DH]).then_inc(on_step.sem, 1)
                dve.wait_ge(on_step.sem, on_step.at(b, 1))
                dve.tensor_tensor(on[:, :, :, :], ut[:, :, :, 0:DH], rz[:, :, :].unsqueeze(3).to_broadcast([P, TPB, H, DH]),
                                  ALU.mult).then_inc(on_step.sem, 1)

            def residual(b):
                if biased:
                    dve.wait_ge(bo_done.sem, bo_done.at(b))
                dve.wait_ge(y_psum.sem, y_psum.at(b))
                dve.tensor_tensor(g.x[:, b, :], g.x[:, b, :], pa[:, 0:S], ALU.add).then_inc(x_done.sem, 1)

            def first():
                for b in range(2):
                    layer_norm(b)
                    normalised(b)
                    projections(b)
                    projected_v(b)
                    projections(b, 1)
                    for k in range(4):
                        split(b, b, k)
                if alibi:
                    distances()
                for h in range(H):
                    if alibi:
                        position_bias(h)
                    maximum(0, h)
                maxima_parts(0)
                maxima_out(0, 0)

            def body(b, i, prev, more1, more2):
                if more2:
                    layer_norm(b + 2)
                for h in range(H):
                    if more1:
                        for k in ahead(h):
                            maximum(b + 1, k)
                    if alibi and h not in POOL_HEADS:
                        weigh(dve, w_done, b, h)
                    if h == 0 and more2:
                        normalised(b + 2)
                    if h == 1 and prev:
                        outputs(b - 1)
                    if h == 7 and prev:
                        residual(b - 1)
                    if h == 3 and more2:
                        projections(b + 2)
                        projected_v(b + 2)
                    if h == LATE and more2 and rope:
                        projections(b + 2, 1)
                    if h in (LATE, LATE + 1) and more2:
                        split(b + 2, i, 2 * (h - LATE))
                        split(b + 2, i, 2 * (h - LATE) + 1)
                    if more1 and h == 13:
                        maxima_parts(b + 1)
                    if more1 and h == 15:
                        maxima_out(b + 1, 1 - i)

            def last():
                outputs(B - 1)
                residual(B - 1)

            turns(dve, first, body, last)

        @block.scalar
        def _(act):
            start(act, [xnT_done, exp_done, u_done, onT_done])
            if alibi:
                act.wait_ge(g.loaded[name], 16 * n_w)
                act.activation(decay[:, 0, :], w["decay"][:, :], ACT.Abs).then_inc(setup_a, 1)
                act.wait_ge(setup_a, 1)
                act.activation(decay[:, 0, :], decay[:, 0, :], ACT.Exp, scale=-1.0).then_inc(setup_a, 1)
                act.wait_ge(setup_a, 2)
                act.activation(decay[:, 0, :], decay[:, 0, :], ACT.Ln, bias=1.0).then_inc(setup_a, 1)

            def position_bias():
                act.wait_ge(setup_v, 3)
                for k in range(2):
                    act.activation(logd[:, k, :], dist0[:, k, :], ACT.Ln, bias=1.0).then_inc(setup_a, 1)
                act.wait_ge(setup_a, 5)
                for h in range(H):
                    if h >= 2:
                        act.wait_ge(setup_v, 3 + 4 * (h - 1))
                    act.activation(logw[:, h % 2, 0, :], logd[:, 0, :], ACT.Ln, bias=1.0,
                                   scale=decay[:, 1, h:h + 1]).then_inc(setup_a, 1)

            def transposed(b):
                act.wait_ge(xnT_psum.sem, xnT_psum.at(b))
                act.activation(xnT[:, :], pb[:, 0:S], ACT.Copy).then_inc(xnT_done.sem, 1)

            def sums(b, q):
                act.wait_ge(av_done.sem, av_done.at(b, 2 * q + 2))
                act.activation(u[:, 2 * q:2 * q + 2, :], up[:, 2 * q:2 * q + 2, :], ACT.Copy).then_inc(u_done.sem, 1)

            def outputs(b):
                act.wait_ge(onT_psum.sem, onT_psum.at(b))
                act.activation(onT[:, :], pb[:, 0:S], ACT.Copy).then_inc(onT_done.sem, 1)

            def first():
                transposed(0)
                transposed(1)
                if alibi:
                    position_bias()

            def body(b, i, prev, more1, more2):
                if prev:
                    sums(b - 1, 1)
                for h in range(H):
                    act.wait_ge(s2_done.sem, s2_done.at(b, h + 1))
                    if h % 4 == 0:
                        act.wait_ge(av_done.sem, av_done.at(b, h // 4 - 1))
                    act.activation(prob[:, h % 8, :], s2[h % 2][:, 0:KC], ACT.Exp).then_inc(exp_done.sem, 1)
                    if h == 1 and more2:
                        transposed(b + 2)
                    if h == 4 and prev:
                        outputs(b - 1)
                    if h == 13:
                        sums(b, 0)

            def last():
                sums(B - 1, 1)
                outputs(B - 1)

            turns(act, first, body, last)

        @block.tensor
        def _(pe):
            start(pe, [xnT_psum, proj, v_psum, s1_done, mT_psum, s2_done, av_done, ut_psum, onT_psum, y_psum])
            pe.wait_ge(g.loaded[name], 16 * n_w)

            def transposes(b):
                pe.wait_ge(ln_step.sem, ln_step.at(b))
                pe.wait_ge(v_done.sem, v_done.at(b - 1))
                pe.wait_ge(onT_done.sem, onT_done.at(b - 4))
                pe.wait_ge(xnT_done.sem, xnT_done.at(b - 1))
                for t in range(TPB):
                    m = pe.transpose(pb[:, t * P:(t + 1) * P], xn[:, t, :], g.ident[:, :])
                m.then_inc(xnT_psum.sem, 1)

            def projections(b, i, stage=0):
                kv = ctxT[:, i, :] if cross else xnT[:, :]
                if stage == 1:
                    pe.wait_ge(qk_done.sem, qk_done.at(b, 2))
                    pe.matmul(pa[:, 0:S], w["wqr"][:, :], xnT[:, :], start=True, stop=True)
                    pe.matmul(pa[:, S:2 * S], w["wkr"][:, :], kv, start=True, stop=True).then_inc(proj.sem, 1)
                    return
                pe.wait_ge(xnT_done.sem, xnT_done.at(b))
                if cross:
                    pe.wait_ge(ctx_in[i], 8 * (b - i) + 16)
                pe.wait_ge(v_done.sem, v_done.at(b - 1))
                pe.wait_ge(mT_done.sem, mT_done.at(b - 2))
                pe.wait_ge(x_done.sem, x_done.at(b - 4))
                pe.matmul(pa[:, 0:S], w["wq"][:, :], xnT[:, :], start=True, stop=True)
                pe.matmul(pa[:, S:2 * S], w["wk"][:, :], kv, start=True, stop=True).then_inc(proj.sem, 1)
                for t in range(TPB):
                    m = pe.matmul(pb[:, S + t * P:S + (t + 1) * P], kv[:, t * P:(t + 1) * P], w["wv"][:, :], start=True, stop=True)
                m.then_inc(v_psum.sem, 1)

            def add(out, lhsT, rhs, last=False):
                return pe.matmul(out, lhsT, rhs, start=False, stop=last)

            def scores_q(b, i, h):
                if h % HH == 0:
                    pe.wait_ge(stack_in[i][h // HH], 16 * STACK_DMAS // 2 * (b - i) + 16 * STACK_DMAS)
                if h == 0 and full_mask is not None:
                    pe.wait_ge(mask_done[0].sem, mask_done[0].at(b))
                pe.wait_ge(max_done.sem, max_done.at(b, h - 1))
                bank = s1[h % 2]
                plain = not (causal or full_mask is not None)
                for t in range(TPB):
                    c0, n = (t * S, S) if not causal else (t * P, (t + 1) * P)
                    out = bank[:, c0:c0 + n]
                    m = pe.matmul(out, stack[i][:, 0, h, t * P:(t + 1) * P], stack[i][:, 1, h, 0:n], start=True, stop=plain)
                    if alibi:
                        add(out, g.ident_bf[:, :], al[:, 0, h, S - n:S])
                        m = add(out, g.ident_bf[:, :], al[:, 1, h, S - n:S], last=True)
                    elif window is not None:
                        m = add(out, g.ident_bf[:, :], g.band_q[:, S - n:S], last=True)
                    elif causal:
                        m = add(out[:, n - P:n], g.ident_bf[:, :], g.tri_q[:, :], last=True)
                    elif full_mask is not None:
                        m = add(out, g.ident_bf[:, :], mb[0][i][:, t, :], last=True)
                m.then_inc(s1_done.sem, 1)

            def maxima(b):
                pe.wait_ge(mparts_done.sem, mparts_done.at(b))
                pe.wait_ge(v_done.sem, v_done.at(min(b + 1, B - 1) if isinstance(b, int) else b + 1))
                pe.wait_ge(x_done.sem, x_done.at(b - 2))
                for t in range(TPB):
                    m = pe.transpose(mTp[0:2 * H, t * P:(t + 1) * P], mparts[:, t, :, :].rearrange("p a h -> p (a h)"), g.ident_bf[:, :])
                m.then_inc(mT_psum.sem, 1)

            def scores_k(b, i, h):
                if h == 0 and full_mask is not None:
                    pe.wait_ge(mask_done[1].sem, mask_done[1].at(b))
                pe.wait_ge(exp_done.sem, exp_done.at(b, h - 1))
                bank = s2[h % 2]
                plain = not (causal or full_mask is not None)
                for t in range(TPB):
                    c0, q0 = (t * S, 0 if not causal else t * P)
                    n = S - q0
                    out = bank[:, c0:c0 + n]
                    pe.matmul(out, stack[i][:, 1, h, t * P:(t + 1) * P], stack[i][:, 0, h, q0:S], start=True, stop=False)
                    m = add(out, g.sel[:, h, :], mT[i][:, q0:S], last=plain)
                    if window is not None:
                        m = add(out, g.ident_bf[:, :], g.band_k[:, 0:n], last=True)
                    elif causal:
                        m = add(out[:, 0:P], g.ident_bf[:, :], g.tri_k[:, :], last=True)
                    elif full_mask is not None:
                        m = add(out, g.ident_bf[:, :], mb[1][i][:, t, :], last=True)
                m.then_inc(s2_done.sem, 1)

            def values(b, i, q):
                if q == 0:
                    pe.wait_ge(va_done.sem, va_done.at(b))
                    pe.wait_ge(on_step.sem, on_step.at(b - 1))
                if alibi:
                    pool_heads = len([h for h in POOL_HEADS if h < 4 * q + 4])
                    pe.wait_ge(w_done.sem, w_done.at(b, 4 * q + 4 - pool_heads))
                    pe.wait_ge(wp_done.sem, wp_done.at(b, pool_heads))
                else:
                    pe.wait_ge(exp_done.sem, exp_done.at(b, 4 * q + 4))
                spans = [(0, 0, S, 0, True, False), (1, 0, S, S, False, True)] if not causal else [
                    (0, 0, P, 0, True, True), (0, P, P, P, True, False), (1, P, P, S, False, True)]
                for kt, q0, n, p0, first, last in spans:
                    for j in range(4):
                        h = 4 * q + j
                        m = pe.matmul(up[HP * j:HP * (j + 1), q, q0:q0 + n], va[i][:, kt, h, :], prob[:, h % 8, p0:p0 + n],
                                      start=first, stop=last, tile_position=(0, HP * j))
                m.then_inc(av_done.sem, 1)

            def tail_transposes(b):
                pe.wait_ge(u_done.sem, u_done.at(b))
                for t in range(TPB):
                    for q in range(4):
                        m = pe.transpose(up[:, 2 * t + q // 2, (q % 2) * P:(q % 2 + 1) * P], u[:, q, t * P:(t + 1) * P], g.ident[:, :])
                m.then_inc(ut_psum.sem, 1)

            def tail_outputs(b, more):
                pe.wait_ge(on_step.sem, on_step.at(b))
                if more:
                    pe.wait_ge(v_done.sem, v_done.at(b + 3))
                    pe.wait_ge(xnT_done.sem, xnT_done.at(b + 3))
                for t in range(TPB):
                    m = pe.transpose(pb[:, t * P:(t + 1) * P], on[:, t, :, :].rearrange("p h c -> p (h c)"), g.ident[:, :])
                m.then_inc(onT_psum.sem, 1)

            def tail_projection(b, more):
                pe.wait_ge(onT_done.sem, onT_done.at(b))
                if more:
                    pe.wait_ge(qk_done.sem, qk_done.at(b + 3, 4 if rope else 2))
                for t in range(TPB):
                    m = pe.matmul(pa[:, t * P:(t + 1) * P], onT[:, t * P:(t + 1) * P], w["wo"][:, :], start=True, stop=True)
                m.then_inc(y_psum.sem, 1)

            def first():
                for b in range(2):
                    transposes(b)
                    projections(b, b)
                    if rope:
                        projections(b, b, 1)
                pe.wait_ge(setup, SETUP + 1)
                for h in range(H):
                    if alibi:
                        pe.wait_ge(setup_v, 3 + 4 * (h + 1))
                    scores_q(0, 0, h)
                maxima(0)

            def body(b, i, prev, more1, more2):
                pe.wait_ge(mT_done.sem, mT_done.at(b))
                for h in range(H):
                    scores_k(b, i, h)
                    if more1:
                        for k in ahead(h):
                            scores_q(b + 1, 1 - i, k)
                    if prev:
                        if h == 0:
                            tail_transposes(b - 1)
                        if h == 4:
                            tail_outputs(b - 1, more2)
                        if h == 6:
                            tail_projection(b - 1, more2)
                    if more2:
                        if h == 1:
                            transposes(b + 2)
                        if h == 2:
                            projections(b + 2, i)
                        if h == 4 and rope:
                            projections(b + 2, i, 1)
                    if h in (5, 9, 13):
                        values(b, i, (h - 5) // 4)
                    if more1 and h == 14:
                        maxima(b + 1)
                values(b, i, 3)

            def last():
                tail_transposes(B - 1)
                tail_outputs(B - 1, False)
                tail_projection(B - 1, False)

            turns(pe, first, body, last)


C_TOK = 4 * P
NC = B * S // C_TOK
TPC = C_TOK // P
CAPACITY = 2 * B * S // E
CHOSEN = 128


def experts(nc, g, name, w, hidden, act_fn, glu, routing, biased=False, prefetch=()):
    F = hidden // P
    NE = NT * E
    with ExitStack() as ctx:
        sb = lambda n, shape, dt=F32: ctx.enter_context(nc.sbuf_tensor(f"{name}_{n}", shape, dt))
        ps = lambda n, shape, dt=F32: ctx.enter_context(nc.psum_tensor(f"{name}_{n}", shape, dt))
        count = lambda n, per=1: Count(nc, f"{name}_{n}", per)
        sem = lambda n: nc.alloc_semaphore(f"{name}_{n}")
        xn = sb("xn", [P, NC, TPC, D])
        xnT = sb("xnT", [P, NC, C_TOK])
        stats = sb("stats", [P, NT, 6])
        mv = sb("mv", [P, NT, 2])
        var_eps = sb("var_eps", [P, NT])
        rstd = sb("rstd", [P, NT])
        logits = sb("logits", [P, NC, TPC * E])
        lg = logits[:, :, :].rearrange("p c (t e) -> p (c t) e", e=E)
        gate = sb("gate", [P, NT, E])
        h = [sb(f"h{i}", [P, F, C_TOK]) for i in range(2)]
        hg = [sb(f"hg{i}", [P, F, C_TOK]) for i in range(2)] if glu else None
        t1, t2, t3 = (sb(n, [P, NT, E]) for n in ("t1", "t2", "t3"))
        mask = sb("mask", [P, 2, NT, E])
        best = sb("best", [P, 3, NT])
        wt = sb("wt", [P, 2, NT])
        ub = [ps(f"ub{i}", [P, C_TOK]) for i in range(4)]
        yb = [ps(f"yb{i}", [P, C_TOK]) for i in range(2)]
        tp = ps("tp", [P, C_TOK])
        lp = ps("lp", [P, C_TOK])

        t_banks = [tp, *ub[1:]]
        ln = sem("ln")
        rstd_done = sem("rstd_done")
        xn_done = count("xn_done")
        xnT_psum = count("xnT_psum")
        xnT_done = count("xnT_done")
        logit_psum, logit_done = sem("logit_psum"), sem("logit_done")
        rv, ra, rp, rg, rdy = (sem(n) for n in ("route_dve", "route_act", "route_pe", "route_pool", "route_ready"))
        ups = 2 * F if glu else F
        up_done = count("up_done", ups * E)
        act_done = count("act_done", F * E)
        h_done = count("h_done", F * E)
        y_done = count("y_done", E)
        acc_done = count("acc_done", TPC * E)
        if routing == "capacity":
            tri = sb("tri", [P, P], BF16)
            mask_bf = sb("mask_bf", [P, 2 * NE], BF16)
            scan = [sb(f"scan{i}", [P, 2 * NT, E]) for i in range(2)]
            tot = sb("tot", [P, 2 * NT, E])
            loc = sb("loc", [P, 2 * NT, E])
        if routing == "choice":
            affT, left = sb("affT", [B * E, S]), sb("left", [B * E, S])
            top8 = sb("top8", [B * E, 8])
            aff = sb("aff", [P, TPB, B, E])
        if biased:
            gT = sb("gT", [NE, P])
            bm = sb("bm", [NE, NT, D])
        block = ctx.enter_context(nc.Block())

        @block.sync
        def _(sp):
            for dst, src, s in prefetch:
                sp.dma_start(dst, src).then_inc(s, 16)

        @block.gpsimd
        def _(pool):
            if routing == "capacity":
                pool.memset(tri[:, :], 1.0).then_inc(rg, 1)
                pool.wait_ge(rg, 1)
                pool.affine_select(out=tri[:, :], in_=tri[:, :], compare_op=ALU.is_gt, fill=0.0,
                                   base=0, pattern=[[1, P]], channel_multiplier=-1).then_inc(rg, 1)
            pool.wait_ge(ln, NC + NT + 1)
            for c in range(NC):
                tiles = slice(c * TPC, (c + 1) * TPC)
                pool.tensor_tensor(rstd[:, tiles], var_eps[:, tiles], g.half[:, 0:TPC], ALU.pow).then_inc(rstd_done, 1)

        @block.vector
        def _(dve):
            start(dve, [xn_done, h_done, acc_done])
            dve.wait_ge(g.loaded[name], 16 * g.n_loads[name])
            xt = g.x[:, :, :].rearrange("p b (t d) -> p (b t) d", t=TPB).rearrange("p (c t) d -> p c t d", c=NC)
            for c in range(NC):
                for t in range(TPC):
                    m = dve.bn_stats(stats[:, c * TPC + t, :], xt[:, c, t, :])
                m.then_inc(ln, 1)
            for t in range(NT):
                if t % TPC == 0:
                    dve.wait_ge(ln, t // TPC + 1)
                    dve.sem_inc(g.spare, 1)
                dve.bn_aggr(mv[:, t, :], stats[:, t, :]).then_inc(ln, 1)
            dve.wait_ge(ln, NC + NT)
            dve.tensor_scalar(var_eps[:, :], mv[:, :, 1], LN_EPS, None, ALU.add).then_inc(ln, 1)
            for c in range(NC):
                dve.wait_ge(rstd_done, c + 1)
                for t in range(TPC):
                    k = c * TPC + t
                    m = dve.tensor_scalar(xn[:, c, t, :], xt[:, c, t, :], mv[:, k, 0:1], rstd[:, k:k + 1], ALU.subtract, ALU.mult)
                m.then_inc(xn_done.sem, 1)
            dve.wait_ge(logit_psum, 1)
            dve.tensor_scalar(logits[:, :, :].rearrange("p c k -> p (c k)"), lp[:, 0:NE], 1.0, None, ALU.mult).then_inc(logit_done, 1)

            n = 0

            def step(m):
                nonlocal n
                m.then_inc(rv, 1)
                n += 1
                dve.wait_ge(rv, n)

            over_e = lambda a: a.unsqueeze(2).to_broadcast([P, NT, E])

            def first_max(values, k, m):
                step(dve.tensor_reduce(best[:, k, :], values, AX.X, ALU.max))
                step(dve.tensor_tensor(t1[:, :, :], values, over_e(best[:, k, :]), ALU.is_equal))
                step(dve.tensor_tensor(t1[:, :, :], t1[:, :, :], g.back_e[:, :].unsqueeze(1).to_broadcast([P, NT, E]), ALU.mult))
                step(dve.tensor_reduce(best[:, 2, :], t1[:, :, :], AX.X, ALU.max))
                step(dve.tensor_tensor(m, t1[:, :, :], over_e(best[:, 2, :]), ALU.is_equal))

            dve.wait_ge(logit_done, 1)
            if routing != "choice":
                first_max(lg, 0, mask[:, 0, :, :])
                step(dve.scalar_tensor_tensor(out=t2[:, :, :], in0=mask[:, 0, :, :], scalar=-3e38, in1=lg, op0=ALU.mult, op1=ALU.add))
                first_max(t2[:, :, :], 1, mask[:, 1, :, :])
                step(dve.tensor_tensor(wt[:, 1, :], best[:, 1, :], best[:, 0, :], ALU.subtract))
            if routing in ("choice", "probs"):
                if routing == "choice":
                    step(dve.tensor_reduce(best[:, 0, :], lg, AX.X, ALU.max))
                step(dve.tensor_tensor(t3[:, :, :], lg, over_e(best[:, 0, :]), ALU.subtract))
            dve.sem_inc(rdy, 1)
            dve.wait_ge(ra, 1)
            if routing in ("choice", "probs"):
                step(dve.reduce_sum(best[:, 2, :], t3[:, :, :], axis=AX.X))
            elif routing in ("pair", "capacity"):
                step(dve.tensor_scalar(best[:, 2, :], wt[:, 1, :], 1.0, None, ALU.add))
            step(dve.reciprocal(wt[:, 0, :], best[:, 2, :]))
            if routing == "choice":
                step(dve.tensor_tensor(aff[:, :, :, :].rearrange("p t b e -> p b t e"), t3[:, :, :].rearrange("p (b t) e -> p b t e", t=TPB),
                                       wt[:, 0, :].rearrange("p (b t) -> p b t", t=TPB).unsqueeze(3).to_broadcast([P, B, TPB, E]), ALU.mult))
                dve.sem_inc(rdy, 1)
                dve.wait_ge(rp, 1)
                step(dve.tensor_scalar(affT[:, :], tp[0:B * E, 0:S], 1.0, None, ALU.mult))
                step(dve.tensor_scalar(left[:, :], affT[:, :], 1.0, None, ALU.mult))
                for _ in range(CHOSEN // 8):
                    step(dve.max(top8[:, :], left[:, :]))
                    step(dve.match_replace(left[:, :], top8[:, :], left[:, :], -1.0))
                step(dve.scalar_tensor_tensor(out=affT[:, :], in0=left[:, :], scalar=-1.0, in1=affT[:, :], op0=ALU.is_equal, op1=ALU.mult))
                dve.sem_inc(rdy, 1)
                dve.wait_ge(rp, 2)
                step(dve.tensor_scalar(gate[:, :, :].rearrange("p (b t) e -> p t b e", t=TPB),
                                       lp[:, 0:NE].rearrange("p (t b e) -> p t b e", t=TPB, b=B), 1.0, None, ALU.mult))
            else:
                step(dve.tensor_tensor(wt[:, 1, :], wt[:, 1, :], wt[:, 0, :], ALU.mult))
                if routing == "capacity":
                    m2 = mask[:, :, :, :].rearrange("p k t e -> p (k t) e")
                    step(dve.tensor_scalar(mask_bf[:, :], mask[:, :, :, :].rearrange("p k t e -> p (k t e)"), 1.0, None, ALU.mult))
                    dve.sem_inc(rdy, 1)
                    dve.wait_ge(rp, 1)
                    step(dve.tensor_scalar(tot[:, :, :], lp[:, 0:2 * NE].rearrange("p (t e) -> p t e", e=E), 1.0, None, ALU.mult))
                    step(dve.tensor_scalar(scan[0][:, :, :], tot[:, :, :], 1.0, None, ALU.mult))
                    k, d = 0, 1
                    while d < 2 * NT:
                        step(dve.tensor_scalar(scan[1 - k][:, 0:d, :], scan[k][:, 0:d, :], 1.0, None, ALU.mult))
                        step(dve.tensor_tensor(scan[1 - k][:, d:2 * NT, :], scan[k][:, d:2 * NT, :], scan[k][:, 0:2 * NT - d, :], ALU.add))
                        k, d = 1 - k, 2 * d
                    step(dve.tensor_tensor(loc[:, :, :], scan[k][:, :, :], tot[:, :, :], ALU.subtract))
                    step(dve.tensor_tensor(loc[:, :, :], tp[:, 0:2 * NE].rearrange("p (t e) -> p t e", e=E), loc[:, :, :], ALU.add))
                    step(dve.scalar_tensor_tensor(out=m2, in0=loc[:, :, :], scalar=float(CAPACITY), in1=m2, op0=ALU.is_lt, op1=ALU.mult))
                step(dve.tensor_tensor(t1[:, :, :], mask[:, 0, :, :], over_e(wt[:, 0, :]), ALU.mult))
                step(dve.tensor_tensor(t2[:, :, :], mask[:, 1, :, :], over_e(wt[:, 1, :]), ALU.mult))
                step(dve.tensor_tensor(gate[:, :, :], t1[:, :, :], t2[:, :, :], ALU.add))
            if biased:
                dve.sem_inc(rdy, 1)
                for t in range(NT):
                    m = dve.tensor_scalar(bm[:, t, :], w["b_out"][:, :], g.rowmask[:, t:t + 1], None, ALU.mult)
                step(m)
                dve.wait_ge(rp, 1)
                step(dve.tensor_scalar(gT[:, :], tp[:, 0:P], 1.0, None, ALU.mult))
                dve.sem_inc(rdy, 1)
                dve.wait_ge(rp, 2)
                for c in range(NC):
                    m = dve.tensor_tensor(g.x[:, 2 * c:2 * c + 2, :], g.x[:, 2 * c:2 * c + 2, :],
                                          ub[c][:, :].rearrange("p (b n) -> p b n", b=2), ALU.add)
                step(m)
            dve.sem_inc(rdy, 1)

            gt = gate[:, :, :].rearrange("p (c t) e -> p c t e", c=NC)
            with dve.Fori(0, NC) as c:
                def products(e):
                    for f in range(F):
                        dve.wait_ge(act_done.sem, act_done.at(c, e * F + f + 1))
                        dve.wait_ge(up_done.sem, up_done.at(c, 2 * (e * F + f) + 2))
                        dve.wait_ge(y_done.sem, y_done.at(c, e - 1))
                        dve.tensor_tensor(h[e % 2][:, f, :], hg[e % 2][:, f, :], ub[(2 * (e * F + f) + 1) % 4][:, :],
                                          ALU.mult).then_inc(h_done.sem, 1)

                def accumulate(e):
                    dve.wait_ge(y_done.sem, y_done.at(c, e + 1))
                    dve.wait_ge(acc_done.sem, acc_done.at(c, TPC * e))
                    for t in range(TPC):
                        dve.scalar_tensor_tensor(out=xt[:, c, t, :], in0=yb[e % 2][:, t * P:(t + 1) * P], scalar=gt[:, c, t, e:e + 1],
                                                 in1=xt[:, c, t, :], op0=ALU.mult, op1=ALU.add).then_inc(acc_done.sem, 1)

                if glu:
                    products(0)
                for e in range(E):
                    if glu and e + 1 < E:
                        products(e + 1)
                    accumulate(e)

        @block.scalar
        def _(act):
            start(act, [xnT_done, act_done])
            act.wait_ge(g.loaded[name], 16 * g.n_loads[name])
            for c in range(NC):
                act.wait_ge(xnT_psum.sem, xnT_psum.at(c))
                act.activation(xnT[:, c, :], t_banks[c][:, :], ACT.Copy).then_inc(xnT_done.sem, 1)
            act.wait_ge(rdy, 1)
            if routing in ("choice", "probs"):
                m = act.activation(t3[:, :, :], t3[:, :, :], ACT.Exp)
            if routing != "choice":
                m = act.activation(wt[:, 1, :], wt[:, 1, :], ACT.Exp)
            m.then_inc(ra, 1)
            with act.Fori(0, NC) as c:
                for e in range(E):
                    for f in range(F):
                        k = e * F + f
                        b = 2 * k if glu else k
                        act.wait_ge(up_done.sem, up_done.at(c, (2 * k + 2) if glu else k + 1))
                        if glu:
                            act.wait_ge(h_done.sem, h_done.at(c, (e - 1) * F))
                            act.activation(hg[e % 2][:, f, :], ub[b % 4][:, :], act_fn).then_inc(act_done.sem, 1)
                        else:
                            act.wait_ge(y_done.sem, y_done.at(c, e - 1))
                            bias = w["b_in"][:, e:e + 1] if biased else 0.0
                            act.activation(h[e % 2][:, f, :], ub[b % 4][:, :], act_fn, bias=bias).then_inc(act_done.sem, 1)

        @block.tensor
        def _(pe):
            start(pe, [xnT_psum, up_done, y_done])
            pe.wait_ge(g.loaded[name], 16 * g.n_loads[name])
            for c in range(NC):
                pe.wait_ge(xn_done.sem, xn_done.at(c))
                for t in range(TPC):
                    m = pe.transpose(t_banks[c][:, t * P:(t + 1) * P], xn[:, c, t, :], g.ident[:, :])
                m.then_inc(xnT_psum.sem, 1)
            for c in range(NC):
                pe.wait_ge(xnT_done.sem, xnT_done.at(c))
                for t in range(TPC):
                    k = c * TPC + t
                    m = pe.matmul(lp[:, k * E:(k + 1) * E], xnT[:, c, t * P:(t + 1) * P], w["router"][:, :], start=True, stop=True)
            m.then_inc(logit_psum, 1)
            if routing == "capacity":
                pe.wait_ge(rdy, 2)
                pe.wait_ge(rg, 2)
                pe.matmul(tp[:, 0:2 * NE], tri[:, :], mask_bf[:, :], start=True, stop=True)
                pe.matmul(lp[:, 0:2 * NE], g.ones_bf[:, 0:P], mask_bf[:, :], start=True, stop=True).then_inc(rp, 1)
            if routing == "choice":
                pe.wait_ge(rdy, 2)
                for t in range(TPB):
                    m = pe.transpose(tp[0:B * E, t * P:(t + 1) * P], aff[:, t, :, :].rearrange("p b e -> p (b e)"), g.ident[:, :])
                m.then_inc(rp, 1)
                pe.wait_ge(rdy, 3)
                for t in range(TPB):
                    m = pe.transpose(lp[:, t * B * E:(t + 1) * B * E], affT[:, t * P:(t + 1) * P], g.ident[0:B * E, 0:B * E])
                m.then_inc(rp, 1)
            if biased:
                pe.wait_ge(rdy, 2)
                pe.transpose(tp[:, 0:P], gate[:, :, :].rearrange("p t e -> p (t e)"), g.ident[:, :]).then_inc(rp, 1)
                pe.wait_ge(rdy, 3)
                for t in range(NT):
                    m = pe.matmul(ub[t // TPC][:, t % TPC * P:(t % TPC + 1) * P], gT[:, :], bm[:, t, :], start=True, stop=True)
                m.then_inc(rp, 1)
                pe.wait_ge(rdy, 4)
            n_up = len(w["up"])

            with pe.Fori(0, NC) as c:
                def up(e):
                    for f in range(F):
                        for j in range(n_up):
                            k = (e * F + f) * n_up + j
                            if glu:
                                pe.wait_ge(h_done.sem, h_done.at(c, e * F + f - 1))
                            else:
                                pe.wait_ge(act_done.sem, act_done.at(c, k - 3))
                            pe.matmul(ub[k % 4][:, :], w["up"][j][:, e, f * P:(f + 1) * P], xnT[:, c, :], start=True,
                                      stop=True).then_inc(up_done.sem, 1)

                def down(e):
                    done = h_done if glu else act_done
                    pe.wait_ge(done.sem, done.at(c, (e + 1) * F))
                    pe.wait_ge(acc_done.sem, acc_done.at(c, TPC * (e - 1)))
                    for t in range(TPC):
                        for f in range(F):
                            m = pe.matmul(yb[e % 2][:, t * P:(t + 1) * P], h[e % 2][:, f, t * P:(t + 1) * P],
                                          w["down"][:, e, f, :], start=f == 0, stop=f == F - 1)
                    m.then_inc(y_done.sem, 1)

                up(0)
                for e in range(E):
                    if e + 1 < E:
                        up(e + 1)
                    down(e)


GH, GK, GV = 4, 32, 64
GV_ALL = GH * GV
LOW = 16
GATE_NORM = 16.0
RMS_EPS = 1e-5


def gated_linear(nc, g, name, w, prefetch=()):
    MID = P // 2 - 1
    BPC = C_TOK // S
    with ExitStack() as ctx:
        sb = lambda n, shape, dt=F32: ctx.enter_context(nc.sbuf_tensor(f"{name}_{n}", shape, dt))
        ps = lambda n, shape, dt=F32: ctx.enter_context(nc.psum_tensor(f"{name}_{n}", shape, dt))
        count = lambda n, per=1: Count(nc, f"{name}_{n}", per)
        xn = sb("xn", [P, TPC, D])
        stats = sb("stats", [P, TPC, 6])
        mv = sb("mv", [P, TPC, 2])
        var_eps = sb("var_eps", [P, TPC])
        rstd = sb("rstd", [P, TPC])
        xnT = sb("xnT", [P, C_TOK])
        z = sb("z", [LOW, C_TOK])
        gl, fa, lg, gsum, gmid = (sb(n, [P, C_TOK]) for n in ("gl", "fa", "lg", "gsum", "gmid"))
        restart = sb("restart", [P, C_TOK])
        eq, ek, qt, kt = (sb(n, [P, C_TOK]) for n in ("eq", "ek", "qt", "kt"))
        v = sb("v", [P, TPC, GV_ALL])
        silu = sb("silu", [P, TPC, GV_ALL])
        ktok = sb("ktok", [P, BPC, P])
        fac = sb("fac", [P, BPC])
        own = sb("own", [P, GH, GV])
        tri = sb("tri", [P, P])
        state = sb("state", [P, BPC, GV_ALL])
        am = sb("am", [P, GH, TPC, P])
        sq, on = sb("sq", [P, TPC, GV_ALL]), sb("on", [P, TPC, GV_ALL])
        ss, ms, rr = (sb(n, [P, TPC * GH]) for n in ("ss", "ms", "rr"))
        onT = sb("onT", [P, 2, C_TOK])
        bank = [ps(f"bank{i}", [P, C_TOK]) for i in range(8)]

        ln_step = count("ln_step", 2 * TPC + 2)
        rstd_done = count("rstd_done")
        xnT_psum = count("xnT_psum")
        xnT_done = count("xnT_done")
        z_psum, z_done = count("z_psum"), count("z_done")
        qk_psum = count("qk_psum")
        v_psum, v_done = count("v_psum", 2), count("v_done", 2)
        gl_psum = count("gl_psum")
        gate = count("gate", 6)
        fa_step = count("fa_step", 3)
        e_done = count("e_done", 3)
        qk_done = count("qk_done", 2)
        o_gate_psum = count("o_gate_psum", 2)
        silu_done = count("silu_done", 2)
        silu_w = count("silu_w")
        k_psum, k_done = count("k_psum"), count("k_done")
        kv_psum, state_done = count("kv_psum"), count("state_done", BPC)
        a_psum, a_done = count("a_psum", GH), count("a_done", GH)
        o_psum = count("o_psum", 2)
        sq_done = count("sq_done", 2)
        norm = count("norm", 4)
        on_done = count("on_done")
        rr_done = count("rr_done")
        onT_psum = count("onT_psum", 2)
        onT_done = count("onT_done", 2)
        y_psum, x_done = count("y_psum"), count("x_done")
        made = nc.alloc_semaphore(f"{name}_made")
        block = ctx.enter_context(nc.Block())
        loaded, n_w = g.loaded[name], 16 * g.n_loads[name]
        tiles = lambda a: a.rearrange("p (t n) -> p t n", n=P)

        @block.sync
        def _(sp):
            for dst, src, s in prefetch:
                sp.dma_start(dst, src).then_inc(s, 16)

        @block.gpsimd
        def _(pool):
            start(pool, [rstd_done, silu_w, rr_done])
            pool.memset(restart[:, :], 1.0).then_inc(made, 1)
            pool.memset(own[:, :, :], 1.0).then_inc(made, 1)
            pool.memset(tri[:, :], 1.0).then_inc(made, 1)
            pool.wait_ge(made, 3)
            pool.memset(tiles(restart[:, :])[:, :, 0:1], 0.0).then_inc(made, 1)
            pool.affine_select(out=own[:, :, :], in_=own[:, :, :], compare_op=ALU.is_ge, fill=0.0,
                               base=0, pattern=[[-GK, GH], [0, GV]], channel_multiplier=1).then_inc(made, 1)
            pool.affine_select(out=tri[:, :], in_=tri[:, :], compare_op=ALU.is_ge, fill=0.0,
                               base=0, pattern=[[1, P]], channel_multiplier=-1).then_inc(made, 1)
            pool.wait_ge(made, 6)
            pool.affine_select(out=own[:, :, :], in_=own[:, :, :], compare_op=ALU.is_ge, fill=0.0,
                               base=GK - 1, pattern=[[GK, GH], [0, GV]], channel_multiplier=-1).then_inc(made, 1)
            pool.wait_ge(loaded, n_w)
            with pool.Fori(0, NC) as c:
                pool.wait_ge(ln_step.sem, ln_step.at(c, 2 * TPC + 1))
                pool.tensor_tensor(rstd[:, :], var_eps[:, :], g.half[:, 0:TPC], ALU.pow).then_inc(rstd_done.sem, 1)
                pool.wait_ge(silu_done.sem, silu_done.at(c))
                pool.tensor_tensor(silu[:, :, :], silu[:, :, :], w["rms"][:, :].unsqueeze(1).to_broadcast([P, TPC, GV_ALL]),
                                   ALU.mult).then_inc(silu_w.sem, 1)
                pool.wait_ge(norm.sem, norm.at(c, 2))
                pool.tensor_tensor(rr[:, :], ms[:, :], g.half[:, 0:TPC * GH], ALU.pow).then_inc(rr_done.sem, 1)

        @block.vector
        def _(dve):
            start(dve, [ln_step, gate, qk_done, k_done, state_done, a_done, norm, on_done, x_done])
            dve.wait_ge(loaded, n_w)
            dve.wait_ge(made, 7)
            xt = g.x[:, :, :].rearrange("p b (t d) -> p (b t) d", t=TPB).rearrange("p (c t) d -> p c t d", c=NC)
            with dve.Fori(0, NC) as c:
                for t in range(TPC):
                    dve.bn_stats(stats[:, t, :], xt[:, c, t, :]).then_inc(ln_step.sem, 1)
                dve.wait_ge(ln_step.sem, ln_step.at(c, TPC))
                dve.sem_inc(g.spare, 1)
                for t in range(TPC):
                    dve.bn_aggr(mv[:, t, :], stats[:, t, :]).then_inc(ln_step.sem, 1)
                dve.wait_ge(ln_step.sem, ln_step.at(c, 2 * TPC))
                dve.tensor_scalar(var_eps[:, :], mv[:, :, 1], LN_EPS, None, ALU.add).then_inc(ln_step.sem, 1)
                dve.wait_ge(rstd_done.sem, rstd_done.at(c))
                for t in range(TPC):
                    m = dve.tensor_scalar(xn[:, t, :], xt[:, c, t, :], mv[:, t, 0:1], rstd[:, t:t + 1], ALU.subtract, ALU.mult)
                m.then_inc(ln_step.sem, 1)
                dve.wait_ge(gl_psum.sem, gl_psum.at(c))
                dve.tensor_scalar(gl[:, :], bank[2][:, :], w["b"][:, 0:1], None, ALU.add).then_inc(gate.sem, 1)
                dve.wait_ge(fa_step.sem, fa_step.at(c))
                dve.scalar_tensor_tensor(out=lg[:, :], in0=gl[:, :], scalar=0.0, in1=fa[:, :], op0=ALU.min,
                                         op1=ALU.subtract).then_inc(gate.sem, 1)
                dve.wait_ge(gate.sem, gate.at(c, 2))
                dve.tensor_tensor_scan(gsum[:, :], restart[:, :], lg[:, :], 0.0, ALU.mult, ALU.add).then_inc(gate.sem, 1)
                dve.wait_ge(gate.sem, gate.at(c, 3))
                gs = tiles(gsum[:, :])
                dve.tensor_tensor(tiles(gmid[:, :]), gs, gs[:, :, MID:MID + 1].to_broadcast([P, TPC, P]), ALU.subtract).then_inc(gate.sem, 1)
                two = gsum[:, :].rearrange("p (b t n) -> p b t n", b=BPC, t=TPB)
                dve.tensor_tensor(fac[:, :], two[:, :, 0, P - 1], two[:, :, 0, MID], ALU.subtract).then_inc(gate.sem, 1)
                dve.wait_ge(gate.sem, gate.at(c, 5))
                dve.tensor_tensor(fac[:, :], fac[:, :], two[:, :, 1, MID], ALU.add).then_inc(gate.sem, 1)
                dve.wait_ge(qk_psum.sem, qk_psum.at(c))
                dve.wait_ge(e_done.sem, e_done.at(c, 1))
                dve.scalar_tensor_tensor(out=qt[:, :], in0=bank[3][:, :], scalar=GK ** -0.5, in1=eq[:, :], op0=ALU.mult,
                                         op1=ALU.mult).then_inc(qk_done.sem, 1)
                dve.wait_ge(e_done.sem, e_done.at(c, 2))
                dve.tensor_tensor(kt[:, :], bank[4][:, :], ek[:, :], ALU.mult).then_inc(qk_done.sem, 1)
                dve.wait_ge(k_psum.sem, k_psum.at(c))
                dve.tensor_scalar(ktok[:, :, :], bank[1][:, 0:BPC * P].rearrange("p (b n) -> p b n", b=BPC), 1.0, None, ALU.mult).then_inc(k_done.sem, 1)
                for h in range(GH):
                    dve.wait_ge(a_psum.sem, a_psum.at(c, h + 1))
                    dve.scalar_tensor_tensor(out=am[:, h, :, :], in0=tiles(bank[3 + h][:, :]), scalar=3e38,
                                             in1=tri[:, :].unsqueeze(1).to_broadcast([P, TPC, P]), op0=ALU.min, op1=ALU.mult).then_inc(a_done.sem, 1)
                dve.wait_ge(kv_psum.sem, kv_psum.at(c))
                dve.wait_ge(e_done.sem, e_done.at(c, 3))
                for j in range(BPC):
                    dve.scalar_tensor_tensor(out=state[:, j, :], in0=bank[2][:, j * GV_ALL:(j + 1) * GV_ALL], scalar=fac[:, j:j + 1],
                                             in1=own[:, :, :].rearrange("p h n -> p (h n)"), op0=ALU.mult, op1=ALU.mult).then_inc(state_done.sem, 1)
                dve.wait_ge(sq_done.sem, sq_done.at(c))
                dve.tensor_reduce(ss[:, :], sq[:, :, :].rearrange("p t (h n) -> p (t h) n", n=GV), AX.X, ALU.add).then_inc(norm.sem, 1)
                dve.wait_ge(norm.sem, norm.at(c, 1))
                dve.tensor_scalar(ms[:, :], ss[:, :], 1.0 / GV, RMS_EPS, ALU.mult, ALU.add).then_inc(norm.sem, 1)
                dve.wait_ge(rr_done.sem, rr_done.at(c))
                for j in range(2):
                    dve.tensor_tensor(on[:, 2 * j:2 * j + 2, :].rearrange("p t (h n) -> p (t h) n", n=GV),
                                      bank[(7, 0)[j]][:, :].rearrange("p (k n) -> p k n", n=GV),
                                      rr[:, 8 * j:8 * j + 8].unsqueeze(2).to_broadcast([P, 8, GV]), ALU.mult).then_inc(norm.sem, 1)
                dve.wait_ge(norm.sem, norm.at(c, 4))
                dve.wait_ge(silu_w.sem, silu_w.at(c))
                dve.tensor_tensor(on[:, :, :], on[:, :, :], silu[:, :, :], ALU.mult).then_inc(on_done.sem, 1)
                dve.wait_ge(y_psum.sem, y_psum.at(c))
                dve.tensor_tensor(xt[:, c, :, :], xt[:, c, :, :], tiles(bank[3][:, :]), ALU.add).then_inc(x_done.sem, 1)

        @block.scalar
        def _(act):
            start(act, [xnT_done, z_done, v_done, fa_step, e_done, silu_done, sq_done, onT_done])
            with act.Fori(0, NC) as c:
                act.wait_ge(xnT_psum.sem, xnT_psum.at(c))
                act.activation(xnT[:, :], bank[0][:, :], ACT.Copy).then_inc(xnT_done.sem, 1)
                act.wait_ge(z_psum.sem, z_psum.at(c))
                act.activation(z[:, :], bank[1][0:LOW, :], ACT.Copy).then_inc(z_done.sem, 1)
                for j in range(2):
                    act.wait_ge(v_psum.sem, v_psum.at(c, j + 1))
                    act.activation(v[:, 2 * j:2 * j + 2, :].rearrange("p t n -> p (t n)"), bank[5 + j][:, :], ACT.Copy).then_inc(v_done.sem, 1)
                act.wait_ge(gate.sem, gate.at(c, 1))
                act.activation(fa[:, :], gl[:, :], ACT.Abs).then_inc(fa_step.sem, 1)
                act.wait_ge(fa_step.sem, fa_step.at(c, 1))
                act.activation(fa[:, :], fa[:, :], ACT.Exp, scale=-1.0).then_inc(fa_step.sem, 1)
                act.wait_ge(fa_step.sem, fa_step.at(c, 2))
                act.activation(fa[:, :], fa[:, :], ACT.Ln, bias=1.0).then_inc(fa_step.sem, 1)
                act.wait_ge(gate.sem, gate.at(c, 4))
                act.activation(eq[:, :], gmid[:, :], ACT.Exp, scale=1.0 / GATE_NORM).then_inc(e_done.sem, 1)
                act.activation(ek[:, :], gmid[:, :], ACT.Exp, scale=-1.0 / GATE_NORM).then_inc(e_done.sem, 1)
                act.wait_ge(gate.sem, gate.at(c, 6))
                act.activation(fac[:, :], fac[:, :], ACT.Exp, scale=1.0 / GATE_NORM).then_inc(e_done.sem, 1)
                for j in range(2):
                    act.wait_ge(o_gate_psum.sem, o_gate_psum.at(c, j + 1))
                    act.activation(silu[:, 2 * j:2 * j + 2, :].rearrange("p t n -> p (t n)"), bank[(7, 0)[j]][:, :], ACT.Silu).then_inc(silu_done.sem, 1)
                for j in range(2):
                    act.wait_ge(o_psum.sem, o_psum.at(c, j + 1))
                    act.activation(sq[:, 2 * j:2 * j + 2, :].rearrange("p t n -> p (t n)"), bank[(7, 0)[j]][:, :], ACT.Square).then_inc(sq_done.sem, 1)
                for j in range(2):
                    act.wait_ge(onT_psum.sem, onT_psum.at(c, j + 1))
                    act.activation(onT[:, j, :], bank[1 + j][:, :], ACT.Copy).then_inc(onT_done.sem, 1)

        @block.tensor
        def _(pe):
            start(pe, [xnT_psum, z_psum, qk_psum, v_psum, gl_psum, o_gate_psum, k_psum, kv_psum, a_psum, o_psum, onT_psum, y_psum])
            pe.wait_ge(loaded, n_w)
            with pe.Fori(0, NC) as c:
                pe.wait_ge(ln_step.sem, ln_step.at(c))
                pe.wait_ge(norm.sem, norm.at(c - 1))
                for t in range(TPC):
                    m = pe.transpose(bank[0][:, t * P:(t + 1) * P], xn[:, t, :], g.ident[:, :])
                m.then_inc(xnT_psum.sem, 1)
                pe.wait_ge(xnT_done.sem, xnT_done.at(c))
                pe.wait_ge(onT_done.sem, onT_done.at(c - 1))
                pe.matmul(bank[1][0:LOW, :], w["w1"][:, :], xnT[:, :], start=True, stop=True).then_inc(z_psum.sem, 1)
                pe.wait_ge(x_done.sem, x_done.at(c - 1))
                pe.matmul(bank[3][:, :], w["wq"][:, :], xnT[:, :], start=True, stop=True)
                pe.matmul(bank[4][:, :], w["wk"][:, :], xnT[:, :], start=True, stop=True).then_inc(qk_psum.sem, 1)
                pe.wait_ge(z_done.sem, z_done.at(c))
                pe.sem_inc(g.spare, 1)
                pe.matmul(bank[2][:, :], w["w2"][:, :], z[:, :], start=True, stop=True).then_inc(gl_psum.sem, 1)
                for j in range(2):
                    for t in range(2):
                        tok = (2 * j + t) * P
                        m = pe.matmul(bank[5 + j][:, t * GV_ALL:(t + 1) * GV_ALL], xnT[:, tok:tok + P], w["wv"][:, :], start=True, stop=True)
                    m.then_inc(v_psum.sem, 1)
                for j in range(2):
                    for t in range(2):
                        tok = (2 * j + t) * P
                        m = pe.matmul(bank[(7, 0)[j]][:, t * GV_ALL:(t + 1) * GV_ALL], xnT[:, tok:tok + P], w["wg"][:, :], start=True, stop=True)
                    m.then_inc(o_gate_psum.sem, 1)
                pe.wait_ge(qk_done.sem, qk_done.at(c))
                for j in range(BPC):
                    m = pe.transpose(bank[1][:, j * P:(j + 1) * P], kt[:, 2 * j * P:(2 * j + 1) * P], g.ident[:, :])
                m.then_inc(k_psum.sem, 1)
                pe.wait_ge(v_done.sem, v_done.at(c))
                pe.sem_inc(g.spare, 1)
                for t in range(TPC):
                    for h in range(GH):
                        rows = slice(h * GK, (h + 1) * GK)
                        m = pe.matmul(bank[3 + h][:, t * P:(t + 1) * P], kt[rows, t * P:(t + 1) * P], qt[rows, t * P:(t + 1) * P],
                                      start=True, stop=True, tile_position=(h * GK, 0))
                        if t == TPC - 1:
                            m.then_inc(a_psum.sem, 1)
                pe.wait_ge(k_done.sem, k_done.at(c))
                for j in range(BPC):
                    m = pe.matmul(bank[2][:, j * GV_ALL:(j + 1) * GV_ALL], ktok[:, j, :], v[:, 2 * j, :], start=True, stop=True)
                m.then_inc(kv_psum.sem, 1)
                for t in range(TPC):
                    j, second = t // 2, t % 2
                    if not second:
                        pe.wait_ge(silu_done.sem, silu_done.at(c, j + 1))
                    pe.wait_ge(a_done.sem, a_done.at(c))
                    out = bank[(7, 0)[j]][:, second * GV_ALL:(second + 1) * GV_ALL]
                    if second:
                        pe.wait_ge(state_done.sem, state_done.at(c, j + 1))
                        pe.matmul(out, qt[:, t * P:(t + 1) * P], state[:, j, :], start=True, stop=False)
                    for h in range(GH):
                        m = pe.matmul(out[:, h * GV:(h + 1) * GV], am[:, h, t, :], v[:, t, h * GV:(h + 1) * GV],
                                      start=not second, stop=not second or h == GH - 1)
                    if second:
                        m.then_inc(o_psum.sem, 1)
                pe.wait_ge(on_done.sem, on_done.at(c))
                for j in range(2):
                    for t in range(TPC):
                        m = pe.transpose(bank[1 + j][:, t * P:(t + 1) * P], on[:, t, j * P:(j + 1) * P], g.ident[:, :])
                    m.then_inc(onT_psum.sem, 1)
                pe.wait_ge(onT_done.sem, onT_done.at(c))
                for t in range(TPC):
                    for j in range(2):
                        m = pe.matmul(bank[3][:, t * P:(t + 1) * P], onT[:, j, t * P:(t + 1) * P], w["wo"][:, j, :], start=j == 0, stop=j == 1)
                m.then_inc(y_psum.sem, 1)


MH, MD = 8, 16
SOFT_CAP = 15.0
MLSTM_EPS, MLSTM_NORM_EPS = 5e-5, 1e-6


def matrix_lstm(nc, g, name, w, ctx_tokens, prefetch=()):
    K2 = 384
    R = TPB * B * MH
    with ExitStack() as ctx:
        sb = lambda n, shape, dt=F32: ctx.enter_context(nc.sbuf_tensor(f"{name}_{n}", shape, dt))
        ps = lambda n, shape, dt=F32: ctx.enter_context(nc.psum_tensor(f"{name}_{n}", shape, dt))
        count = lambda n, per=1: Count(nc, f"{name}_{n}", per)
        sem = lambda n: nc.alloc_semaphore(f"{name}_{n}")
        xn = sb("xn", [P, NC, TPC, D])
        xnT = sb("xnT", [P, NC, C_TOK])
        ctxT = sb("ctxT", [P, NC, C_TOK])
        ctx_tok = sb("ctx_tok", [P, B, TPB * D])
        stats = sb("stats", [P, NT, 6])
        mv = sb("mv", [P, NT, 2])
        var_eps = sb("var_eps", [P, NT])
        rstd = sb("rstd", [P, NT])
        bias15 = sb("bias15", [2 * MH, 1])
        thT = sb("thT", [2 * MH, NC, C_TOK])
        th = sb("th", [P, NC, TPC * 2 * MH])
        ig, lf, fa, a_sb, c_tok, em = (sb(n, [P, TPB, B, MH]) for n in ("ig", "lf", "fa", "a_sb", "c_tok", "em"))
        c_row, m_row, rest = (sb(n, [R, P]) for n in ("c_row", "m_row", "rest"))
        carry = sb("carry", [P, 1])
        part = sb("part", [R, 3, P], BF16)
        gain = sb("gain", [P, D])
        mparts = sb("mparts", [96, B, S], BF16)
        sel3 = sb("sel3", [96, MH, P], BF16)
        trif = sb("trif", [P, P])
        rowmask = sb("rowmask", [P, MH])
        kTm = [sb(f"kTm{i}", [P, MH, S]) for i in range(2)]
        va = [sb(f"va{i}", [P, TPB, MH, HP]) for i in range(2)]
        cs = [sb(f"cs{i}", [P, TPB, MH]) for i in range(2)]
        dmat = sb("dmat", [P, 2, K2])
        smat = sb("smat", [P, 8, K2])
        u = sb("u", [P, 2, S])
        den = sb("den", [P, TPB, MH])
        hv, sq = sb("hv", [P, TPB, MH, MD]), sb("sq", [P, TPB, MH, MD])
        ms, rr, rz = (sb(n, [P, TPB, MH]) for n in ("ms", "rr", "rz"))
        eb = [ps(f"eb{i}", [P, 512]) for i in range(2)]
        s2 = [ps(f"s2_{i}", [P, 512]) for i in range(2)]
        up = ps("up", [P, 2, S])
        utp = ps("utp", [P, 512])
        tp = ps("tp", [P, C_TOK])
        lp = ps("lp", [P, C_TOK])
        ut = utp[:, :].rearrange("p (t h c) -> p t h c", t=TPB, c=HP)

        t_banks = [tp, *s2, utp]
        ln = sem("ln")
        rstd_done = sem("rstd_done")
        xn_done = count("xn_done")
        xnT_psum = count("xnT_psum")
        xnT_done = count("xnT_done")
        gates_psum = count("gates_psum")
        tanh_done = count("tanh_done")
        th_psum, th_done = sem("th_psum"), sem("th_done")
        rv, ra, rp, setup = (sem(n) for n in ("scan_dve", "scan_act", "scan_pe", "setup"))
        rdy = sem("scan_ready")
        parts_out, parts_in = sem("parts_out"), sem("parts_in")
        k_done = count("k_done", MH)
        c_done = count("c_done")
        va_done = count("va_done")
        e_psum = count("e_psum", MH)
        d_done = count("d_done", MH)
        s_psum = count("s_psum", MH)
        s_done = count("s_done", MH)
        av_done = count("av_done", 2)
        u_done = count("u_done")
        ut_psum = count("ut_psum")
        tail = count("tail", 12)
        rr_done = count("rr_done")
        block = ctx.enter_context(nc.Block())

        def turns(e, first, body, last):
            first()
            body(0, 0, True, False)
            body(1, 1, True, True)
            with e.Fori(2, B - 3, 2) as b:
                body(b, 0, True, True)
                body(b + 1, 1, True, True)
            body(B - 2, 0, True, True)
            body(B - 1, 1, False, True)
            last()

        @block.sync
        def _(sp):
            sp.dma_start(ctxT[:, :, :], g.ctxT_dram.rearrange("d b s -> d (b s)").rearrange("d (c n) -> d c n", c=NC)).then_inc(g.ctx_loaded, 16)
            sp.dma_start(ctx_tok[:, :, :].rearrange("p b (t d) -> p b t d", t=TPB),
                         ctx_tokens.rearrange("b (t p) d -> p b t d", p=P)).then_inc(g.ctx_loaded, 16)
            for dst, src, s in prefetch:
                sp.dma_start(dst, src).then_inc(s, 16)
            sp.wait_ge(rdy, 5)
            sp.wait_ge(setup, 1)
            sp.dma_start(g.scratch, part[:, :, :]).then_inc(parts_out, 16)
            sp.wait_ge(parts_out, 16)
            for k in range(3):
                for t in range(TPB):
                    sp.dma_start(mparts[32 * k:32 * k + MH, :, t * P:(t + 1) * P],
                                 g.scratch.rearrange("(t b h) k s -> t k h b s", t=TPB, b=B)[t, k]).then_inc(parts_in, 16)
            sp.wait_ge(parts_in, 16 * 6)

        @block.gpsimd
        def _(pool):
            start(pool, [va_done, rr_done])
            pool.memset(mparts[:, :, :], 0.0).then_inc(setup, 1)
            pool.wait_ge(ln, NC + NT + 1)
            for c in range(NC):
                tiles = slice(c * TPC, (c + 1) * TPC)
                pool.tensor_tensor(rstd[:, tiles], var_eps[:, tiles], g.half[:, 0:TPC], ALU.pow).then_inc(rstd_done, 1)
            pool.memset(trif[:, :], 1.0).then_inc(setup, 1)
            pool.memset(rowmask[:, :], 1.0).then_inc(setup, 1)
            pool.memset(sel3[:, :, :], 0.0).then_inc(setup, 1)
            for i in range(2):
                pool.memset(va[i][:, :, :, :], 1.0).then_inc(setup, 1)
            pool.wait_ge(setup, 6)
            pool.affine_select(out=trif[:, :], in_=trif[:, :], compare_op=ALU.is_ge, fill=0.0,
                               base=0, pattern=[[1, P]], channel_multiplier=-1).then_inc(setup, 1)
            pool.affine_select(out=rowmask[:, :], in_=rowmask[:, :], compare_op=ALU.is_ge, fill=0.0,
                               base=0, pattern=[[-MD, MH]], channel_multiplier=1).then_inc(setup, 1)
            pool.wait_ge(setup, 8)
            pool.affine_select(out=rowmask[:, :], in_=rowmask[:, :], compare_op=ALU.is_ge, fill=0.0,
                               base=MD - 1, pattern=[[MD, MH]], channel_multiplier=-1).then_inc(setup, 1)
            for k in range(3):
                pool.affine_select(out=sel3[:, :, :], in_=sel3[:, :, :], compare_op=ALU.not_equal, fill=1.0,
                                   base=-32 * k, pattern=[[-1, MH], [0, P]], channel_multiplier=1).then_inc(setup, 1)
                pool.wait_ge(setup, 10 + k)
            pool.wait_ge(g.ctx_loaded, 32)

            def values(b, i):
                pool.wait_ge(av_done.sem, av_done.at(b - 2))
                pool.sem_inc(g.spare, 1)
                pool.tensor_copy(va[i][:, :, :, 0:MD], ctx_tok[:, b, :].rearrange("p (t h c) -> p t h c", t=TPB, h=MH)).then_inc(va_done.sem, 1)

            def norm(b):
                pool.wait_ge(tail.sem, tail.at(b, 9))
                pool.tensor_tensor(rr[:, :, :], ms[:, :, :], g.half[:, 0:TPB * MH].rearrange("p (t h) -> p t h", t=TPB), ALU.pow).then_inc(rr_done.sem, 1)

            def body(b, i, more, tail_too):
                if tail_too:
                    norm(b - 1)
                if more:
                    values(b + 1, 1 - i)

            turns(pool, lambda: values(0, 0), body, lambda: norm(B - 1))

        @block.vector
        def _(dve):
            start(dve, [xn_done, k_done, c_done, s_done, tail])
            dve.wait_ge(g.loaded[name], 16 * g.n_loads[name])
            dve.tensor_scalar(bias15[:, :], w["bias"][:, :], 1.0 / SOFT_CAP, None, ALU.mult).then_inc(rdy, 1)
            dve.tensor_scalar(gain[:, :], w["outnorm"][:, :], 1.0, None, ALU.add)
            xt = g.x[:, :, :].rearrange("p b (t d) -> p (b t) d", t=TPB).rearrange("p (c t) d -> p c t d", c=NC)
            for c in range(NC):
                for t in range(TPC):
                    m = dve.bn_stats(stats[:, c * TPC + t, :], xt[:, c, t, :])
                m.then_inc(ln, 1)
            for t in range(NT):
                if t % TPC == 0:
                    dve.wait_ge(ln, t // TPC + 1)
                    dve.sem_inc(g.spare, 1)
                dve.bn_aggr(mv[:, t, :], stats[:, t, :]).then_inc(ln, 1)
            dve.wait_ge(ln, NC + NT)
            dve.tensor_scalar(var_eps[:, :], mv[:, :, 1], LN_EPS, None, ALU.add).then_inc(ln, 1)
            for c in range(NC):
                dve.wait_ge(rstd_done, c + 1)
                for t in range(TPC):
                    k = c * TPC + t
                    m = dve.tensor_scalar(xn[:, c, t, :], xt[:, c, t, :], mv[:, k, 0:1], rstd[:, k:k + 1], ALU.subtract, ALU.mult)
                m.then_inc(xn_done.sem, 1)
            dve.wait_ge(th_psum, 1)
            dve.tensor_scalar(th[:, :, :].rearrange("p c k -> p (c k)"), lp[:, 0:NT * 2 * MH], SOFT_CAP, None, ALU.mult).then_inc(th_done, 1)

            n = 0

            def step(m):
                nonlocal n
                m.then_inc(rv, 1)
                n += 1
                dve.wait_ge(rv, n)

            gates = th[:, :, :].rearrange("p c (a k) -> p (c a) k", k=2 * MH).rearrange("p (b t) k -> p t b k", t=TPB)
            flat = lambda a: a[:, :, :, :].rearrange("p t b h -> p (t b h)")
            dve.wait_ge(th_done, 1)
            step(dve.tensor_scalar(ig[:, :, :, :], gates[:, :, :, 0:MH], 1.0, None, ALU.mult))
            step(dve.tensor_scalar(lf[:, :, :, :], gates[:, :, :, MH:2 * MH], 1.0, None, ALU.mult))
            dve.sem_inc(rdy, 1)
            dve.wait_ge(ra, 3)
            step(dve.scalar_tensor_tensor(out=flat(lf), in0=flat(lf), scalar=0.0, in1=flat(fa), op0=ALU.min, op1=ALU.subtract))
            dve.sem_inc(rdy, 1)
            dve.wait_ge(rp, 1)
            step(dve.tensor_scalar(flat(a_sb), tp[:, 0:R], 1.0, None, ALU.mult))
            step(dve.tensor_tensor(flat(c_tok), flat(ig), flat(a_sb), ALU.subtract))
            dve.sem_inc(rdy, 1)
            dve.wait_ge(rp, 2)
            step(dve.tensor_scalar(c_row[:, :], lp[:, 0:P], 1.0, None, ALU.mult))
            step(dve.tensor_tensor_scan(m_row[:, :], c_row[:, :], c_row[:, :], -3e38, ALU.max, ALU.max))
            half = R // 2
            step(dve.tensor_scalar(carry[half:R, :], m_row[0:half, P - 1:P], 1.0, None, ALU.mult))
            step(dve.tensor_scalar(m_row[half:R, :], m_row[half:R, :], carry[half:R, 0:1], None, ALU.max))
            step(dve.tensor_scalar(rest[:, :], m_row[:, :], -1.0, None, ALU.mult))
            for k in range(3):
                step(dve.tensor_scalar(part[:, k, :], rest[:, :], 1.0, None, ALU.mult))
                if k < 2:
                    step(dve.tensor_tensor(rest[:, :], rest[:, :], part[:, k, :], ALU.subtract))
            dve.sem_inc(rdy, 1)
            dve.wait_ge(rp, 3)
            step(dve.tensor_tensor(flat(em), tp[:, 0:R], flat(a_sb), ALU.add))
            dve.sem_inc(rdy, 1)
            dve.wait_ge(ra, 4)
            dve.wait_ge(setup, 12)
            dve.wait_ge(g.ctx_loaded, 32)

            def keys(b, i):
                dve.wait_ge(av_done.sem, av_done.at(b - 2))
                for h in range(MH):
                    dve.tensor_scalar(kTm[i][:, h, :], ctxT[:, :, :].rearrange("p c n -> p (c n)").rearrange("p (b n) -> p b n", b=B)[:, b, :],
                                      rowmask[:, h:h + 1], MD ** -0.5, ALU.mult, ALU.mult).then_inc(k_done.sem, 1)
                dve.tensor_scalar(cs[i][:, :, :], c_tok[:, :, b, :], 1.0, None, ALU.mult).then_inc(c_done.sem, 1)

            def weigh(b, lo, hi):
                for h in range(lo, hi):
                    dve.wait_ge(d_done.sem, d_done.at(b, h + 1))
                    dve.wait_ge(s_psum.sem, s_psum.at(b, h + 1))
                    dve.tensor_tensor(smat[:, h, :], s2[h % 2][:, 0:K2], dmat[:, h % 2, :], ALU.mult).then_inc(s_done.sem, 1)

            def finish(b):
                over_d = lambda a: a[:, :, :].unsqueeze(3).to_broadcast([P, TPB, MH, MD])
                k = 0

                def chain(m):
                    nonlocal k
                    m.then_inc(tail.sem, 1)
                    k += 1
                    dve.wait_ge(tail.sem, tail.at(b, k))

                dve.wait_ge(ut_psum.sem, ut_psum.at(b))
                chain(dve.tensor_scalar(den[:, :, :], ut[:, :, :, MD], 1.0, None, ALU.mult))
                chain(dve.scalar_tensor_tensor(out=den[:, :, :], in0=den[:, :, :], scalar=-1.0, in1=den[:, :, :], op0=ALU.mult, op1=ALU.max))
                chain(dve.tensor_tensor(den[:, :, :], den[:, :, :], em[:, :, b, :], ALU.max))
                chain(dve.tensor_scalar(den[:, :, :], den[:, :, :], MLSTM_EPS, None, ALU.add))
                chain(dve.reciprocal(rz[:, :, :], den[:, :, :]))
                chain(dve.tensor_tensor(hv[:, :, :, :], ut[:, :, :, 0:MD], over_d(rz), ALU.mult))
                chain(dve.tensor_tensor(sq[:, :, :, :], hv[:, :, :, :], hv[:, :, :, :], ALU.mult))
                chain(dve.tensor_reduce(den[:, :, :], sq[:, :, :, :], AX.X, ALU.add))
                chain(dve.tensor_scalar(ms[:, :, :], den[:, :, :], 1.0 / MD, MLSTM_NORM_EPS, ALU.mult, ALU.add))
                dve.wait_ge(rr_done.sem, rr_done.at(b))
                chain(dve.tensor_tensor(hv[:, :, :, :], hv[:, :, :, :], over_d(rr), ALU.mult))
                chain(dve.tensor_tensor(hv[:, :, :, :], hv[:, :, :, :], gain[:, :].rearrange("p (h c) -> p h c", h=MH).unsqueeze(1).to_broadcast([P, TPB, MH, MD]), ALU.mult))
                dve.tensor_tensor(g.x[:, b, :], g.x[:, b, :], hv[:, :, :, :].rearrange("p t h c -> p (t h c)"), ALU.add).then_inc(tail.sem, 1)

            def body(b, i, more, tail_too):
                weigh(b, 0, 3)
                if more:
                    keys(b + 1, 1 - i)
                weigh(b, 3, 5)
                if tail_too:
                    finish(b - 1)
                weigh(b, 5, MH)

            turns(dve, lambda: keys(0, 0), body, lambda: finish(B - 1))

        @block.scalar
        def _(act):
            start(act, [xnT_done, tanh_done, d_done, u_done])
            act.wait_ge(rdy, 1)
            for c in range(NC):
                act.wait_ge(xnT_psum.sem, xnT_psum.at(c))
                act.activation(xnT[:, c, :], t_banks[c][:, :], ACT.Copy).then_inc(xnT_done.sem, 1)
            for c in range(NC):
                act.wait_ge(gates_psum.sem, gates_psum.at(c))
                act.activation(thT[:, c, :], eb[c % 2][0:2 * MH, :], ACT.Tanh, bias=bias15[:, 0:1], scale=1.0 / SOFT_CAP).then_inc(tanh_done.sem, 1)
            act.wait_ge(rdy, 2)
            act.activation(fa[:, :, :, :], lf[:, :, :, :], ACT.Abs).then_inc(ra, 1)
            act.wait_ge(ra, 1)
            act.activation(fa[:, :, :, :], fa[:, :, :, :], ACT.Exp, scale=-1.0).then_inc(ra, 1)
            act.wait_ge(ra, 2)
            act.activation(fa[:, :, :, :], fa[:, :, :, :], ACT.Ln, bias=1.0).then_inc(ra, 1)
            act.wait_ge(rdy, 6)
            act.activation(em[:, :, :, :], em[:, :, :, :], ACT.Exp, scale=-1.0).then_inc(ra, 1)

            def sums(b):
                act.wait_ge(av_done.sem, av_done.at(b))
                act.wait_ge(ut_psum.sem, ut_psum.at(b - 1))
                act.activation(u[:, :, :], up[:, :, :], ACT.Copy).then_inc(u_done.sem, 1)

            def body(b, i, more, tail_too):
                act.wait_ge(c_done.sem, c_done.at(b))
                for h in range(MH):
                    act.wait_ge(e_psum.sem, e_psum.at(b, h + 1))
                    act.wait_ge(s_done.sem, s_done.at(b, h - 1))
                    act.activation(dmat[:, h % 2, 0:S], eb[h % 2][:, 0:S], ACT.Exp, bias=cs[i][:, 0, h:h + 1])
                    act.activation(dmat[:, h % 2, S:K2], eb[h % 2][:, S:K2], ACT.Exp, bias=cs[i][:, 1, h:h + 1]).then_inc(d_done.sem, 1)
                    if h == 2 and tail_too:
                        sums(b - 1)

            turns(act, lambda: None, body, lambda: sums(B - 1))

        @block.tensor
        def _(pe):
            start(pe, [xnT_psum, gates_psum, e_psum, s_psum, av_done, ut_psum])
            pe.wait_ge(g.loaded[name], 16 * g.n_loads[name])
            pe.wait_ge(g.ctx_loaded, 32)
            for c in range(NC):
                pe.wait_ge(xn_done.sem, xn_done.at(c))
                for t in range(TPC):
                    m = pe.transpose(t_banks[c][:, t * P:(t + 1) * P], xn[:, c, t, :], g.ident[:, :])
                m.then_inc(xnT_psum.sem, 1)
            for c in range(NC):
                pe.wait_ge(xnT_done.sem, xnT_done.at(c))
                pe.wait_ge(tanh_done.sem, tanh_done.at(c - 2))
                out = eb[c % 2][0:2 * MH, :]
                pe.matmul(out, w["gq"][:, :], xnT[:, c, :], start=True, stop=False)
                pe.matmul(out, w["gk"][:, :], ctxT[:, c, :], start=False, stop=False)
                pe.matmul(out, w["gv"][:, :], ctxT[:, c, :], start=False, stop=True).then_inc(gates_psum.sem, 1)
            for c in range(NC):
                pe.wait_ge(tanh_done.sem, tanh_done.at(c))
                for t in range(TPC):
                    k = c * TPC + t
                    m = pe.transpose(lp[:, k * 2 * MH:(k + 1) * 2 * MH], thT[:, c, t * P:(t + 1) * P], g.ident[0:2 * MH, 0:2 * MH])
            m.then_inc(th_psum, 1)
            pe.wait_ge(rdy, 3)
            pe.wait_ge(setup, 12)
            ls = lf[:, :, :, :].rearrange("p t b h -> p t (b h)")
            pe.matmul(tp[:, 0:R // 2], trif[:, :], ls[:, 0, :], start=True, stop=True)
            pe.matmul(tp[:, R // 2:R], trif[:, :], ls[:, 1, :], start=True, stop=False)
            pe.matmul(tp[:, R // 2:R], g.ones[:, :], ls[:, 0, :], start=False, stop=True).then_inc(rp, 1)
            pe.wait_ge(rdy, 4)
            pe.transpose(lp[:, 0:P], c_tok[:, :, :, :].rearrange("p t b h -> p (t b h)"), g.ident[:, :]).then_inc(rp, 1)
            pe.wait_ge(rdy, 5)
            pe.transpose(tp[:, 0:R], m_row[:, :], g.ident[:, :]).then_inc(rp, 1)
            pe.wait_ge(parts_in, 16 * 6)
            xb = xnT[:, :, :].rearrange("p c n -> p (c n)").rearrange("p (b n) -> p b n", b=B)

            def head(b, i, h):
                pe.wait_ge(d_done.sem, d_done.at(b, h - 1))
                e = eb[h % 2]
                for t, (c0, n) in enumerate([(0, S), (S, P)]):
                    pe.matmul(e[:, c0:c0 + n], sel3[:, h, :], mparts[:, b, S - n:S], start=True, stop=False)
                    m = pe.matmul(e[:, c0:c0 + P], g.ident_bf[:, :], g.tri_k[:, :], start=False, stop=True)
                m.then_inc(e_psum.sem, 1)
                pe.wait_ge(k_done.sem, k_done.at(b, h + 1))
                pe.wait_ge(s_done.sem, s_done.at(b, h - 1))
                for t, (c0, n) in enumerate([(0, S), (S, P)]):
                    m = pe.matmul(s2[h % 2][:, c0:c0 + n], kTm[i][:, h, t * P:(t + 1) * P], xb[:, b, S - n:S], start=True, stop=True)
                m.then_inc(s_psum.sem, 1)

            def values(b, i, q):
                if q == 0:
                    pe.wait_ge(u_done.sem, u_done.at(b - 1))
                    pe.wait_ge(va_done.sem, va_done.at(b))
                pe.wait_ge(s_done.sem, s_done.at(b, 4 * q + 4))
                for kt, q0, n, p0, first, last in [(0, 0, P, 0, True, True), (0, P, P, P, True, False), (1, P, P, S, False, True)]:
                    for j in range(4):
                        h = 4 * q + j
                        m = pe.matmul(up[HP * j:HP * (j + 1), q, q0:q0 + n], va[i][:, kt, h, :], smat[:, h, p0:p0 + n],
                                      start=first, stop=last, tile_position=(0, HP * j))
                m.then_inc(av_done.sem, 1)

            def sums(b):
                pe.wait_ge(u_done.sem, u_done.at(b))
                pe.wait_ge(tail.sem, tail.at(b - 1, 6))
                for t in range(TPB):
                    for q in range(2):
                        m = pe.transpose(utp[:, (2 * t + q) * P:(2 * t + q + 1) * P], u[:, q, t * P:(t + 1) * P], g.ident[:, :])
                m.then_inc(ut_psum.sem, 1)

            def body(b, i, more, tail_too):
                for h in range(MH):
                    head(b, i, h)
                    if h == 4 and tail_too:
                        sums(b - 1)
                    if h == 5:
                        values(b, i, 0)
                values(b, i, 1)

            turns(pe, lambda: None, body, lambda: sums(B - 1))


WH, WD = 16, 64
INNER = WH * WD
WFF = 512


def decoder(nc, g, name, w, mask, prefetch=()):
    CH = INNER // P
    JOBS = 4
    FC = WFF // P
    LAG = 4
    with ExitStack() as ctx:
        sb = lambda n, shape, dt=F32: ctx.enter_context(nc.sbuf_tensor(f"{name}_{n}", shape, dt))
        ps = lambda n, shape, dt=F32: ctx.enter_context(nc.psum_tensor(f"{name}_{n}", shape, dt))
        count = lambda n, per=1: Count(nc, f"{name}_{n}", per)
        y0, y = sb("y0", [P, 2, TPB, D]), sb("y", [P, 2, TPB, D])
        y0T, yT = sb("y0T", [P, 2, S]), sb("yT", [P, 2, S])
        ctxT = sb("ctxT", [P, 2, S])
        stats = sb("stats", [P, TPB, 6])
        mv = sb("mv", [P, TPB, 2])
        var_eps = sb("var_eps", [P, TPB])
        rstd = sb("rstd", [P, TPB])
        qT = sb("qT", [P, CH, S])
        kTm = sb("kTm", [P, WH, S])
        va = sb("va", [P, TPB, WH, WD])
        negm = sb("negm", [P, 2, TPB])
        prob = sb("prob", [P, 4, TPB, S])
        probT = sb("probT", [P, 4, TPB, S])
        rowsum, rz = sb("rowsum", [P, 2, TPB]), sb("rz", [P, 2, TPB])
        onT = [sb(f"onT{i}", [P, CH, S]) for i in range(2)]
        hT = sb("hT", [P, FC, S])
        mu = sb("mu", [1, B * S], mybir.dt.uint8)
        mb = sb("mb", [1, B, S], BF16)
        s1 = [ps(f"s1_{i}", [P, 512]) for i in range(2)]
        pt = [ps(f"pt_{i}", [P, 512]) for i in range(2)]
        pr = [ps(f"pr_{i}", [P, 512]) for i in range(2)]
        ob = [ps(f"ob_{i}", [P, 512]) for i in range(2)]

        round_banks = [pr, pt, ob, pr]

        N_CA1, N_FF0, N_SA0, N_FF1, N_SA1, N_CA0, N_IN0, N_IN1 = range(8)
        T_CA1, T_SA0, T_SA1, T_CA0, T_IN0, T_IN1 = range(6)
        NORM_OF, T_OF = (N_CA1, N_SA0, N_SA1, N_CA0), (T_CA1, T_SA0, T_SA1, T_CA0)
        ln_step = count("ln_step", 8 * 8)
        rstd_done = count("rstd_done", 8)
        yT_psum, yT_done = count("yT_psum", 6), count("yT_done", 6)
        bias_done = count("bias_done", 6)
        added = count("added", 6)
        qk_psum = count("qk_psum", 4 * JOBS)
        q_done, k_done = count("q_done", 4 * JOBS), count("k_done", 4 * JOBS)
        v_psum, v_done = count("v_psum", 4 * JOBS), count("v_done", 4 * JOBS)
        s1_psum = count("s1_psum", WH * JOBS)
        max_done = count("max_done", WH * JOBS)
        exp_done = count("exp_done", WH * JOBS)
        pt_psum = count("pt_psum", WH * JOBS)
        pt_done = [count(f"pt_done{i}", WH // 2 * JOBS) for i in range(2)]
        rz_done, scaled = count("rz_done", WH * JOBS), count("scaled", WH * JOBS)
        av_done = count("av_done", CH * JOBS)
        onT_done = count("onT_done", CH * JOBS)
        a_psum = count("a_psum", JOBS)
        h_psum, h_done = count("h_psum", 4), count("h_done", 4)
        f_psum = count("f_psum", 2)
        x_done = count("x_done", 2)

        def skip(e, c, p, k, n):
            e.wait_ge(c.sem, c.at(p, k))
            e.sem_inc(c.sem, n)

        def turns(e, first, body, last):
            first()
            body(0, False, True)
            with e.Fori(1, B // 2 - 1) as p:
                body(p, True, True)
            body(B // 2 - 1, True, False)
            last(B // 2)

        ctx_in = [nc.alloc_semaphore(f"{name}_ctx_in{i}") for i in range(2)]
        mask_in = nc.alloc_semaphore(f"{name}_mask_in")
        made = nc.alloc_semaphore(f"{name}_made")
        masked = nc.alloc_semaphore(f"{name}_masked")
        block = ctx.enter_context(nc.Block())
        loaded, n_w = g.loaded[name], 16 * g.n_loads[name]

        @block.sync
        def _(sp):
            sp.dma_start(mu[:, :], mask).then_inc(mask_in, 16)
            for dst, src, s in prefetch:
                sp.dma_start(dst, src).then_inc(s, 16)
            with sp.Fori(0, B // 2) as p:
                for i in range(2):
                    sp.wait_ge(v_psum.sem, v_psum.at(p - 1, 4 * (2 + i) + 4))
                    sp.dma_start(ctxT[:, i, :], g.ctxT_dram[:, 2 * p + i, :]).then_inc(ctx_in[i], 16)

        @block.gpsimd
        def _(pool):
            N_IN = 2
            pool.sem_inc(rstd_done.sem, rstd_done.per - N_IN)
            pool.sem_inc(bias_done.sem, bias_done.per - N_IN)
            pool.memset(kTm[:, :, :], 0.0).then_inc(made, 1)
            pool.memset(va[:, :, :, :], 1.0).then_inc(made, 1)
            pool.wait_ge(loaded, n_w)

            def rstds(p, n):
                pool.wait_ge(ln_step.sem, ln_step.at(p, 8 * n + 5))
                pool.tensor_tensor(rstd[:, :], var_eps[:, :], g.half[:, 0:TPB], ALU.pow).then_inc(rstd_done.sem, 1)

            def bias(p, n, buf, i, row):
                pool.wait_ge(yT_psum.sem, yT_psum.at(p, n + 1))
                pool.tensor_tensor(buf[:, i, :, :], buf[:, i, :, :], row[:, :].unsqueeze(1).to_broadcast([P, TPB, D]),
                                   ALU.add).then_inc(bias_done.sem, 1)

            def inputs(p):
                rstds(p, N_IN0)
                rstds(p, N_IN1)
                bias(p, T_IN0, y0, 0, w["sa_bo"])
                bias(p, T_IN1, y0, 1, w["sa_bo"])

            def body(p, prev, more):
                if prev:
                    rstds(p, N_CA1)
                    rstds(p, N_FF0)
                    bias(p, T_CA1, y, 1, w["fc2_b"])
                else:
                    skip(pool, rstd_done, p, 0, 2)
                    skip(pool, bias_done, p, 0, 1)
                rstds(p, N_SA0)
                if prev:
                    rstds(p, N_FF1)
                else:
                    skip(pool, rstd_done, p, 3, 1)
                bias(p, T_SA0, y, 0, w["ca_bo"])
                rstds(p, N_SA1)
                bias(p, T_SA1, y, 1, w["ca_bo"])
                rstds(p, N_CA0)
                if more:
                    rstds(p, N_IN0)
                    rstds(p, N_IN1)
                bias(p, T_CA0, y, 0, w["fc2_b"])
                if more:
                    bias(p, T_IN0, y0, 0, w["sa_bo"])
                    bias(p, T_IN1, y0, 1, w["sa_bo"])
                else:
                    skip(pool, rstd_done, p, 6, 2)
                    skip(pool, bias_done, p, 4, 2)

            def last(p):
                rstds(p, N_CA1)
                rstds(p, N_FF0)
                bias(p, T_CA1, y, 1, w["fc2_b"])
                skip(pool, rstd_done, p, 2, 1)
                rstds(p, N_FF1)

            turns(pool, lambda: inputs(-1), body, last)

        @block.vector
        def _(dve):
            start(dve, [k_done, max_done, rz_done, scaled, pt_done[0], added, x_done])
            dve.sem_inc(ln_step.sem, 8 * N_IN0)
            dve.wait_ge(mask_in, 16)
            dve.tensor_scalar(mb[:, :, :].rearrange("p b s -> p (b s)"), mu[:, :], NEG, None, ALU.mult).then_inc(masked, 1)
            dve.wait_ge(loaded, n_w)
            dve.wait_ge(made, 2)

            def norm_start(p, n, src):
                at = lambda k: ln_step.at(p, 8 * n + k)
                for t in range(TPB):
                    dve.bn_stats(stats[:, t, :], src(t)).then_inc(ln_step.sem, 1)
                dve.wait_ge(ln_step.sem, at(2))
                dve.sem_inc(g.spare, 1)
                for t in range(TPB):
                    dve.bn_aggr(mv[:, t, :], stats[:, t, :]).then_inc(ln_step.sem, 1)
                dve.wait_ge(ln_step.sem, at(4))
                dve.tensor_scalar(var_eps[:, :], mv[:, :, 1], LN_EPS, None, ALU.add).then_inc(ln_step.sem, 1)

            def norm_end(p, n, out, src, gain=None):
                at = lambda k: ln_step.at(p, 8 * n + k)
                dve.wait_ge(rstd_done.sem, rstd_done.at(p, n + 1))
                for t in range(TPB):
                    m = dve.tensor_scalar(out[:, t, :], src(t), mv[:, t, 0:1], rstd[:, t:t + 1], ALU.subtract, ALU.mult)
                if gain is None:
                    m.then_inc(ln_step.sem, 3)
                    return
                m.then_inc(ln_step.sem, 1)
                for k, op in enumerate((ALU.mult, ALU.add)):
                    dve.wait_ge(ln_step.sem, at(6 + k))
                    dve.tensor_tensor(out, out, w[gain + "gb"[k]][:, :].unsqueeze(1).to_broadcast([P, TPB, D]),
                                      op).then_inc(ln_step.sem, 1)

            def of_x(p, i):
                return lambda t: g.x[:, 2 * p + i, t * D:(t + 1) * D]

            def of_y(i):
                return lambda t: y[:, i, t, :]

            def keys(p, a):
                for r in range(4):
                    dve.wait_ge(qk_psum.sem, qk_psum.at(p, 4 * a + r + 1))
                    kb = round_banks[r][1][:, :].rearrange("p (c n) -> p c n", c=2)
                    for j in range(2):
                        rows = slice(j * WD, (j + 1) * WD)
                        m = dve.tensor_scalar(kTm[rows, :, :].rearrange("p (c j) n -> p c j n", j=2)[:, 2 * r:2 * r + 2, j, :], kb[rows, :, :],
                                              1.0, None, ALU.mult)
                    m.then_inc(k_done.sem, 1)

            def add(p, n, i, src, biased_at):
                dve.wait_ge(bias_done.sem, biased_at)
                dve.tensor_tensor(y[:, i, :, :], src[:, i, :, :], pr[0][:, 0:S].rearrange("p (t d) -> p t d", t=TPB),
                                  ALU.add).then_inc(added.sem, 1)
                dve.wait_ge(added.sem, added.at(p, n + 1))
                norm_start(p, n, of_y(i))

            def output_add(p, a):
                i, src, at = [(1, y, (p - 1, T_SA1)), (0, y0, (p - 1, T_IN0)), (1, y0, (p - 1, T_IN1)), (0, y, (p, T_SA0))][a]
                dve.wait_ge(a_psum.sem, a_psum.at(p, a + 1))
                add(p, NORM_OF[a], i, src, bias_done.at(at[0], at[1] + 1))

            def output_norm(p, a):
                i = (a + 1) % 2
                norm_end(p, NORM_OF[a], y[:, i, :, :], of_y(i), ("ln2_", "ln1_", "ln1_", "ln2_")[a])

            def ff_add(p, i):
                dve.wait_ge(f_psum.sem, f_psum.at(p, i + 1))
                add(p, (N_FF0, N_FF1)[i], i, y, bias_done.at(p - 1, T_CA0 + 1) if i == 0 else bias_done.at(p, T_CA1 + 1))

            def ff_end(p, i):
                n = (N_FF0, N_FF1)[i]
                norm_end(p, n, y[:, i, :, :], of_y(i), "ln3_")
                dve.wait_ge(ln_step.sem, ln_step.at(p, 8 * (n + 1)))
                dve.tensor_tensor(g.x[:, 2 * (p - 1) + i, :], g.x[:, 2 * (p - 1) + i, :], y[:, i, :, :].rearrange("p t d -> p (t d)"),
                                  ALU.add).then_inc(x_done.sem, 1)

            def heads(p, a, output, ff, inputs):
                for h in range(WH + LAG):
                    if h < WH:
                        dve.wait_ge(s1_psum.sem, s1_psum.at(p, WH * a + h + 1))
                        dve.tensor_reduce(negm[:, h % 2, :], s1[h % 2][:, :].rearrange("p (t c) -> p t c", t=TPB), AX.X, ALU.max,
                                          negate=True).then_inc(max_done.sem, 1)
                    k = h - 1
                    if 0 <= k < WH:
                        dve.wait_ge(exp_done.sem, exp_done.at(p, WH * a + k + 1))
                        dve.reciprocal(rz[:, k % 2, :], rowsum[:, k % 2, :]).then_inc(rz_done.sem, 1)
                        dve.wait_ge(rz_done.sem, rz_done.at(p, WH * a + k + 1))
                        dve.tensor_tensor(prob[:, k % 4, :, :], prob[:, k % 4, :, :], rz[:, k % 2, :].unsqueeze(2).to_broadcast([P, TPB, S]),
                                          ALU.mult).then_inc(scaled.sem, 1)
                    k = h - 2
                    if 0 <= k < WH and k % 2 == 0:
                        dve.wait_ge(pt_psum.sem, pt_psum.at(p, WH * a + k + 1))
                        dve.wait_ge(av_done.sem, av_done.at(p, CH * a + k // 2 - 1))
                        dve.tensor_scalar(probT[:, k % 4, :, :].rearrange("p t n -> p (t n)"), pt[0][:, :], 1.0, None, ALU.mult).then_inc(pt_done[0].sem, 1)
                    if output and h == 8:
                        output_add(p, a)
                    if output and h == 10:
                        output_norm(p, a)
                    if ff and h == 18:
                        ff_add(p, a)
                    if ff and h == 19:
                        ff_end(p, a)
                    if inputs and h in (11, 13):
                        norm_start(p, N_IN0 + (h - 11) // 2, of_x(p + 1, (h - 11) // 2))
                    if inputs and h in (12, 14):
                        i = (h - 12) // 2
                        norm_end(p, N_IN0 + i, y0[:, i, :, :], of_x(p + 1, i))

            def first():
                for i in range(2):
                    norm_start(-1, N_IN0 + i, of_x(0, i))
                    norm_end(-1, N_IN0 + i, y0[:, i, :, :], of_x(0, i))

            def body(p, prev, more):
                if not prev:
                    skip(dve, ln_step, p, 0, 8 * 2)
                    skip(dve, added, p, 0, 2)
                    skip(dve, x_done, p, 0, 2)
                for a in range(JOBS):
                    keys(p, a)
                    heads(p, a, prev or a > 0, prev and a < 2, more and a == 3)
                    if a == 1 and not prev:
                        skip(dve, ln_step, p, 8 * N_FF1, 8)
                        skip(dve, added, p, N_FF1, 1)
                if not more:
                    skip(dve, ln_step, p, 8 * N_IN0, 8 * 2)

            def last(p):
                output_add(p, 0)
                output_norm(p, 0)
                ff_add(p, 0)
                ff_end(p, 0)
                skip(dve, ln_step, p, 8 * N_SA0, 8)
                skip(dve, added, p, N_SA0, 1)
                ff_add(p, 1)
                ff_end(p, 1)

            turns(dve, first, body, last)

        @block.scalar
        def _(act):
            start(act, [q_done, v_done, exp_done, pt_done[1], onT_done, h_done])
            act.sem_inc(yT_done.sem, T_IN0)
            act.wait_ge(loaded, n_w)
            act.wait_ge(made, 2)

            def transposed(p, n, out, i, bank):
                act.wait_ge(yT_psum.sem, yT_psum.at(p, n + 1))
                act.activation(out[:, i, :], bank[:, 0:S], ACT.Copy).then_inc(yT_done.sem, 1)

            def projected(p, a):
                for r in range(4):
                    act.wait_ge(qk_psum.sem, qk_psum.at(p, 4 * a + r + 1))
                    act.activation(qT[:, 2 * r:2 * r + 2, :].rearrange("p c n -> p (c n)"), round_banks[r][0][:, :], ACT.Copy,
                                   scale=WD ** -0.5).then_inc(q_done.sem, 1)

            def values(p, a, t):
                for u in range(2):
                    act.wait_ge(v_psum.sem, v_psum.at(p, 4 * a + 2 * t + u + 1))
                    act.activation(va[:, t, 8 * u:8 * u + 8, :], ob[u][:, :].rearrange("p (h c) -> p h c", h=8),
                                   ACT.Copy).then_inc(v_done.sem, 1)

            def hidden(p, i):
                for k in range(FC):
                    if k % 2 == 0:
                        act.wait_ge(h_psum.sem, h_psum.at(p, 2 * i + k // 2 + 1))
                    if k == 0:
                        act.wait_ge(f_psum.sem, f_psum.at(p, i))
                    m = act.activation(hT[:, k, :], pr[k // 2][:, k % 2 * S:(k % 2 + 1) * S], ACT.Gelu, bias=w["fc1_b"][:, k:k + 1])
                    if k % 2:
                        m.then_inc(h_done.sem, 1)

            def heads(p, a, output, ff, inputs):
                for h in range(WH + LAG):
                    if h < WH:
                        act.wait_ge(max_done.sem, max_done.at(p, WH * a + h + 1))
                        act.wait_ge(pt_psum.sem, pt_psum.at(p, WH * a + h - 3))
                        act.wait_ge(rz_done.sem, rz_done.at(p, WH * a + h - 1))
                        for t in range(TPB):
                            m = act.activation(prob[:, h % 4, t, :], s1[h % 2][:, t * S:(t + 1) * S], ACT.Exp, bias=negm[:, h % 2, t:t + 1],
                                               accum_out=rowsum[:, h % 2, t:t + 1])
                        m.then_inc(exp_done.sem, 1)
                        if h < TPB:
                            values(p, a, h)
                    k = h - 2
                    if 0 < k < WH and k % 2:
                        act.wait_ge(pt_psum.sem, pt_psum.at(p, WH * a + k + 1))
                        act.wait_ge(av_done.sem, av_done.at(p, CH * a + k // 2 - 1))
                        act.activation(probT[:, k % 4, :, :].rearrange("p t n -> p (t n)"), pt[1][:, :], ACT.Copy).then_inc(pt_done[1].sem, 1)
                    if h >= LAG and h % 2 == 0:
                        q = (h - LAG) // 2
                        act.wait_ge(av_done.sem, av_done.at(p, CH * a + q + 1))
                        act.activation(onT[a % 2][:, q, :], ob[q % 2][:, 0:S], ACT.Copy).then_inc(onT_done.sem, 1)
                    if ff and h == 14:
                        hidden(p, a)
                    if output and h == 12:
                        transposed(p, T_OF[a], yT, (a + 1) % 2, pr[1])
                    if inputs and h in (17, 18):
                        transposed(p, T_IN0 + h - 17, y0T, h - 17, pr[h - 17])

            def first():
                for i in range(2):
                    transposed(-1, T_IN0 + i, y0T, i, pr[i])

            def body(p, prev, more):
                if not prev:
                    skip(act, yT_done, p, 0, 1)
                    skip(act, h_done, p, 0, 4)
                for a in range(JOBS):
                    projected(p, a)
                    heads(p, a, prev or a > 0, prev and a < 2, more and a == 3)
                if not more:
                    skip(act, yT_done, p, T_IN0, 2)

            def last(p):
                transposed(p, T_CA1, yT, 1, pr[1])
                skip(act, yT_done, p, T_SA0, 1)
                hidden(p, 0)
                hidden(p, 1)

            turns(act, first, body, last)

        @block.tensor
        def _(pe):
            start(pe, [qk_psum, v_psum, s1_psum, pt_psum, av_done, a_psum, h_psum, f_psum])
            pe.sem_inc(yT_psum.sem, T_IN0)
            pe.wait_ge(loaded, n_w)
            pe.wait_ge(masked, 1)

            def transposes(p, n, norm, src, i, bank):
                pe.wait_ge(ln_step.sem, ln_step.at(p, 8 * (norm + 1)))
                pe.wait_ge(yT_done.sem, yT_done.at(p, n))
                for t in range(TPB):
                    m = pe.transpose(bank[:, t * P:(t + 1) * P], src[:, i, t, :], g.ident[:, :])
                m.then_inc(yT_psum.sem, 1)

            def projections(p, a):
                i, kind = a % 2, ("sa_w", "ca_w")[a // 2]
                qs = (y0T, yT)[a // 2][:, i, :]
                kv = y0T[:, i, :] if a < 2 else ctxT[:, i, :]
                pe.wait_ge(yT_done.sem, yT_done.at(p, a))
                pe.wait_ge(added.sem, added.at(p, (0, N_FF0, N_FF1, N_SA1)[a] + (a > 0)))
                if a >= 2:
                    pe.wait_ge(ctx_in[i], 16 * (p + 1))
                for r in range(4):
                    banks = round_banks[r]
                    if r == 1:
                        for c in pt_done:
                            pe.wait_ge(c.sem, c.at(p, WH // 2 * a))
                    if r == 2:
                        pe.wait_ge(onT_done.sem, onT_done.at(p, CH * a))
                    if r == 3:
                        pe.wait_ge(q_done.sem, q_done.at(p, 4 * a + 1))
                        pe.wait_ge(k_done.sem, k_done.at(p, 4 * a + 1))
                    for c in range(2):
                        cols = slice((2 * r + c) * P, (2 * r + c + 1) * P)
                        pe.matmul(banks[0][:, c * S:(c + 1) * S], w[kind + "q"][:, cols], qs, start=True, stop=True)
                        m = pe.matmul(banks[1][:, c * S:(c + 1) * S], w[kind + "k"][:, cols], kv, start=True, stop=True)
                    m.then_inc(qk_psum.sem, 1)

            def values(p, a, t):
                kv = y0T[:, a % 2, :] if a < 2 else ctxT[:, a % 2, :]
                if t == 0:
                    pe.wait_ge(q_done.sem, q_done.at(p, 4 * a + 3))
                    pe.wait_ge(k_done.sem, k_done.at(p, 4 * a + 3))
                else:
                    pe.wait_ge(v_done.sem, v_done.at(p, 4 * a + 2 * t))
                for u in range(2):
                    pe.matmul(ob[u][:, :], kv[:, t * P:(t + 1) * P], w[("sa_wv", "ca_wv")[a // 2]][:, u * 512:(u + 1) * 512], start=True,
                              stop=True).then_inc(v_psum.sem, 1)

            def output(p, a, part):
                if part == 0:
                    pe.wait_ge(onT_done.sem, onT_done.at(p, CH * a))
                t, ks = part // 2, range(part % 2 * CH // 2, (part % 2 + 1) * CH // 2)
                for k in ks:
                    m = pe.matmul(pr[0][:, t * P:(t + 1) * P], onT[(a + 1) % 2][:, k, t * P:(t + 1) * P], w[("ca_wo", "sa_wo", "sa_wo", "ca_wo")[a]][:, k, :],
                                  start=k == 0, stop=k == CH - 1)
                if part == 3:
                    m.then_inc(a_psum.sem, 1)

            def hidden(p, i):
                pe.wait_ge(added.sem, added.at(p, (N_CA1, N_SA0)[i] + 1))
                pe.wait_ge(yT_done.sem, yT_done.at(p, i + 1))
                for k in range(FC):
                    m = pe.matmul(pr[k // 2][:, k % 2 * S:(k % 2 + 1) * S], w["fc1"][:, k * P:(k + 1) * P], yT[:, i, :], start=True, stop=True)
                    if k % 2:
                        m.then_inc(h_psum.sem, 1)

            def ff_output(p, i, t):
                if t == 0:
                    pe.wait_ge(h_done.sem, h_done.at(p, 2 * i + 2))
                for k in range(FC):
                    m = pe.matmul(pr[0][:, t * P:(t + 1) * P], hT[:, k, t * P:(t + 1) * P], w["fc2"][:, k, :], start=k == 0, stop=k == FC - 1)
                if t == TPB - 1:
                    m.then_inc(f_psum.sem, 1)

            def heads(p, a, with_output, ff, inputs):
                i = a % 2
                for h in range(WH + LAG):
                    if h < WH:
                        if h in (0, 2):
                            pe.wait_ge(q_done.sem, q_done.at(p, 4 * a + (1 if h == 0 else 4)))
                            pe.wait_ge(k_done.sem, k_done.at(p, 4 * a + (1 if h == 0 else 4)))
                        pe.wait_ge(exp_done.sem, exp_done.at(p, WH * a + h - 1))
                        for t in range(TPB):
                            out = s1[h % 2][:, t * S:(t + 1) * S]
                            pe.matmul(out, qT[:, h // 2, t * P:(t + 1) * P], kTm[:, h, :], start=True, stop=False)
                            m = pe.matmul(out, g.ones_bf[0:1, 0:P], mb[:, 2 * p + i, :], start=False, stop=True)
                        m.then_inc(s1_psum.sem, 1)
                        if h < TPB:
                            values(p, a, h)
                    k = h - 2
                    if 0 <= k < WH:
                        pe.wait_ge(scaled.sem, scaled.at(p, WH * a + k + 1))
                        done = pt_done[k % 2]
                        pe.wait_ge(done.sem, done.at(p, WH // 2 * a + k // 2))
                        for kt in range(TPB):
                            for t in range(TPB):
                                m = pe.transpose(pt[k % 2][:, kt * S + t * P:kt * S + (t + 1) * P], prob[:, k % 4, t, kt * P:(kt + 1) * P],
                                                 g.ident[:, :])
                        m.then_inc(pt_psum.sem, 1)
                    if h >= LAG and h % 2 == 0:
                        q = (h - LAG) // 2
                        if q == 0:
                            pe.wait_ge(v_done.sem, v_done.at(p, 4 * a + 4))
                        for done in pt_done:
                            pe.wait_ge(done.sem, done.at(p, WH // 2 * a + q + 1))
                        pe.wait_ge(onT_done.sem, onT_done.at(p, CH * a + q - 1))
                        for kt in range(TPB):
                            for j in range(2):
                                k = 2 * q + j
                                m = pe.matmul(ob[q % 2][j * WD:(j + 1) * WD, 0:S], va[:, kt, k, :], probT[:, k % 4, kt, :],
                                              start=kt == 0, stop=kt == TPB - 1, tile_position=(0, j * WD))
                        m.then_inc(av_done.sem, 1)
                    if with_output and 3 <= h < 7:
                        output(p, a, h - 3)
                    if with_output and h == 11:
                        transposes(p, T_OF[a], NORM_OF[a], y, (a + 1) % 2, pr[1])
                    if ff and h == 13:
                        hidden(p, a)
                    if ff and h in (17, 18):
                        ff_output(p, a, h - 17)
                    if inputs and h in (16, 17):
                        transposes(p, T_IN0 + h - 16, N_IN0 + h - 16, y0, h - 16, pr[h - 16])

            def first():
                for i in range(2):
                    transposes(-1, T_IN0 + i, N_IN0 + i, y0, i, pr[i])

            def body(p, prev, more):
                if not prev:
                    skip(pe, yT_psum, p, 0, 1)
                    skip(pe, a_psum, p, 0, 1)
                    skip(pe, h_psum, p, 0, 4)
                    skip(pe, f_psum, p, 0, 2)
                for a in range(JOBS):
                    projections(p, a)
                    heads(p, a, prev or a > 0, prev and a < 2, more and a == 3)
                if not more:
                    skip(pe, yT_psum, p, T_IN0, 2)

            def last(p):
                pe.wait_ge(yT_done.sem, yT_done.at(p, 0))
                pe.wait_ge(added.sem, added.at(p, 0))
                for part in range(4):
                    output(p, 0, part)
                transposes(p, T_CA1, N_CA1, y, 1, pr[1])
                for i in range(2):
                    if i:
                        pe.wait_ge(added.sem, added.at(p, N_FF0 + 1))
                    hidden(p, i)
                    for t in range(TPB):
                        ff_output(p, i, t)

            turns(pe, first, body, last)


class Shared:
    pass


def rope_tables():
    half = DH // 2
    freq = (1.0 / 10000.0 ** (np.arange(half, dtype=np.float32) / half)).astype(np.float32)
    ang = np.arange(S, dtype=np.float32)[None, :] * np.tile(freq, 2 * H)[:, None]
    sign = np.tile(np.repeat(np.array([-1.0, 1.0], np.float32), half), H)[:, None]
    return np.cos(ang).astype(np.float32), (np.sin(ang) * sign).astype(np.float32)


def small_weights():
    dd, col = [P, D], [P, 1]
    cross = lambda L: dict(wq=(f"{L}_xattn_WqT", dd), wk=(f"{L}_xattn_WkT", dd), wv=(f"{L}_xattn_WvT", dd), wo=(f"{L}_xattn_WoT", dd),
                           bq=(f"{L}_xattn_bq", col), bk=(f"{L}_xattn_bk", col), bv=(f"{L}_xattn_bv", dd), bo=(f"{L}_xattn_bo", dd))
    return {
        "l0a": dict(w1=("L0_attn_gk_w1", [P, LOW]), w2=("L0_attn_gk_w2", [LOW, P]), b=("L0_attn_gk_b", col), wo=("L0_attn_Wo", [P, 2, D]),
                    rms=("L0_attn_rms_w", [P, GV_ALL])),
        "l0x": dict(gq=("L0_xattn_gq", [P, 2 * MH]), gk=("L0_xattn_gk", [P, 2 * MH]), gv=("L0_xattn_gv", [P, 2 * MH]),
                    bias=("L0_xattn_bias", [2 * MH, 1]), outnorm=("L0_xattn_outnorm", dd)),
        "l0f": dict(router=("L0_ffn_wg", [P, E])),
        "l1a": dict(wq=("L1_attn_WqT", dd), wk=("L1_attn_WkT", dd), wqr=("L1_attn_WqrT", dd), wkr=("L1_attn_WkrT", dd),
                    wv=("L1_attn_WvT", dd), wo=("L1_attn_WoT", dd), bq=("L1_attn_bq", col), bk=("L1_attn_bk", col),
                    bqr=("L1_attn_bqr", col), bkr=("L1_attn_bkr", col), bv=("L1_attn_bv", dd), bo=("L1_attn_bo", dd)),
        "l1x": cross("L1"),
        "l1f": dict(router=("L1_ffn_gate_w", [P, E])),
        "l2a": dict(wq=("L2_attn_Wq", dd), wk=("L2_attn_Wk", dd), wv=("L2_attn_Wv", dd), wo=("L2_attn_w_proj", dd),
                    decay=("L2_attn_decay", [P, H])),
        "l2x": dict(fc1_b=("L2_xattn_fc1_b", [P, WFF // P]), **{n: (f"L2_xattn_{n}", dd) for n in (
            "sa_bo", "ca_bo", "fc2_b", "ln1_g", "ln1_b", "ln2_g", "ln2_b", "ln3_g", "ln3_b")}),
        "l2f": dict(router=("L2_ffn_router_w", [P, E]), b_in=("L2_ffn_b_in", [P, E]), b_out=("L2_ffn_b_out", dd)),
        "l3a": dict(wq=("L3_attn_WqT", dd), wk=("L3_attn_WkT", dd), wv=("L3_attn_WvT", dd), wo=("L3_attn_WoT", dd)),
        "l3x": cross("L3"),
        "l3f": dict(router=("L3_ffn_Wg", [P, E])),
    }


def build(nc, ins, out, layers=range(12)):
    g = Shared()
    with ExitStack() as ctx:
        sb = lambda n, shape, dt=F32: ctx.enter_context(nc.sbuf_tensor(n, shape, dt))
        g.x = sb("x", [P, B, TPB * D])
        g.ident = sb("ident", [P, P])
        g.ident_bf = sb("ident_bf", [P, P], BF16)
        g.half = sb("half", [P, NT])
        g.rowmask = sb("rowmask", [P, H])
        g.sel = sb("sel", [2 * H, H, P], BF16)
        g.ones_bf = sb("ones_bf", [P, S], BF16)
        g.ones = sb("ones", [P, P])
        g.iota_e = sb("iota_e", [P, E])
        g.back_e = sb("back_e", [P, E])
        g.tri_q, g.tri_k = sb("tri_q", [P, P], BF16), sb("tri_k", [P, P], BF16)
        g.band_q, g.band_k = sb("band_q", [P, S], BF16), sb("band_k", [P, S], BF16)
        g.cosq, g.cosk, g.sinq, g.sink = (sb(n, [P, S]) for n in ("cosq", "cosk", "sinq", "sink"))
        g.ctxT_dram = ins["ctxT"]
        g.x_load = (g.x[:, :, :].rearrange("p b (t d) -> p b t d", t=TPB), ins["x"].rearrange("b (t p) d -> p b t d", p=P))
        g.loaded = {"x": ctx.enter_context(nc.semaphore("x_loaded"))}
        g.weight_loads, g.n_loads = [], {}
        g.spare = ctx.enter_context(nc.semaphore("spare"))

        def weights(name):
            table = small_weights()[name]
            widths = [int(np.prod(shape[1:])) for _, shape in table.values()]
            pack, w, at = sb(f"w_{name}", [P, sum(widths)]), {}, 0
            for (n, (_, shape)), width in zip(table.items(), widths):
                w[n] = pack[0:shape[0], at:at + width]
                if len(shape) == 3:
                    w[n] = w[n].rearrange("p (a b) -> p a b", a=shape[1])
                at += width
            g.loaded[name] = ctx.enter_context(nc.semaphore(f"{name}_loaded"))
            g.n_loads[name] = 1
            g.weight_loads.append((pack[:, :], ins[f"small_{name}"], g.loaded[name]))
            return w

        w_l0a, w_l0x, w_l0f, w_l1a, w_l1x, w_l1f, w_l2a, w_l2x, w_l2f, w_l3a, w_l3x, w_l3f = (weights(n) for n in small_weights())
        for t, n in ((g.cosq, "cosq"), (g.cosk, "cosk"), (g.sinq, "sinq"), (g.sink, "sink")):
            g.weight_loads.append((t[:, :], ins[n], g.loaded["l1a"]))
        g.n_loads["l1a"] += 4
        area_a, area_b = sb("area_a", [P, 9216]), sb("area_b", [P, 6144])

        def parts(area, name, *shapes):
            got, at = [], 0
            g.loaded[name] = g.loaded.get(name) or ctx.enter_context(nc.semaphore(f"{name}_loaded"))
            pairs = []
            for src, shape in shapes:
                n = int(np.prod(shape))
                names = "abc"[:len(shape)]
                flat = area[:, at:at + n]
                dims = dict(zip(names, shape))
                t = flat.rearrange(f"p ({' '.join(names)}) -> p {' '.join(names)}", **dims)
                got.append(t)
                pairs.append((t, ins[src]))
                at += n
            g.n_loads[name] = g.n_loads.get(name, 0) + len(pairs)
            return got, [(d, s_, g.loaded[name]) for d, s_ in pairs]

        g.ctx_loaded = ctx.enter_context(nc.semaphore("ctx_loaded"))
        g.parts_dram = [nc.dram_tensor(f"qk_parts{i}", [2, 3, DH, H, S], BF16, kind="Internal").ap() for i in range(2)]
        g.scratch = nc.dram_tensor("m_parts", [P, 3, P], BF16, kind="Internal").ap()
        (up0, w_l0f["down"]), load_l0f = parts(area_a, "l0f", ("L0_ffn_w_gate", (E, 512)), ("L0_ffn_w_down", (E, 4, D)))
        proj0, load_l0a = parts(area_a[:, 8192:9216], "l0a", *[(f"L0_attn_{n}", (m,)) for n, m in
                                                               (("Wq", D), ("Wk", D), ("Wv", GV_ALL), ("Wg", GV_ALL))])
        w_l0a.update(zip(("wq", "wk", "wv", "wg"), proj0))
        (g1, u1, w_l1f["down"]), load_l1f = parts(area_b, "l1f", ("L1_ffn_Wg", (E, 256)), ("L1_ffn_Wu", (E, 256)), ("L1_ffn_Wd", (E, 2, D)))
        (up2, w_l2f["down"]), load_l2f = parts(area_b, "l2f", ("L2_ffn_w_in", (E, 128)), ("L2_ffn_w_out", (E, 1, D)))
        (g3, u3, w_l3f["down"]), load_l3f = parts(area_a, "l3f", ("L3_ffn_W1", (E, 256)), ("L3_ffn_W2", (E, 256)), ("L3_ffn_W3", (E, 2, D)))
        big = ["sa_wq", "sa_wk", "sa_wv", "ca_wq", "ca_wk", "ca_wv"]
        got, load_l2x = parts(area_a, "l2x", *[(f"L2_xattn_{n}", (INNER,)) for n in big], ("L2_xattn_fc1", (WFF,)),
                              ("L2_xattn_sa_wo", (INNER // P, D)), ("L2_xattn_ca_wo", (INNER // P, D)), ("L2_xattn_fc2", (WFF // P, D)))
        w_l2x.update(zip(big + ["fc1", "sa_wo", "ca_wo", "fc2"], got))
        w_l0f["up"], w_l1f["up"], w_l2f["up"], w_l3f["up"] = [up0], [g1, u1], [up2], [g3, u3]
        loads = {"l0a": (0, None, load_l0a), "l0f": (2, None, load_l0f), "l1f": (5, None, load_l1f), "l2x": (7, 3, load_l2x), "l2f": (8, 6, load_l2f),
                 "l3f": (11, 8, load_l3f)}
        area_loads = [l for user, at, ls in loads.values() if user in layers and at not in layers for l in ls]
        first = {0: load_l0a}.get(layers[0], area_loads)
        g.first_loads = [l for l in g.weight_loads if l[2] is g.loaded["l0a"]] + first if layers[0] == 0 else g.weight_loads + first
        rest = [l for l in g.weight_loads + area_loads if not any(l is m for m in g.first_loads)]
        constants(nc, g)
        for n in layers:
            fetch = [l for user, at, ls in loads.values() if at == n and user in layers for l in ls]
            with nc.cleanup_on_exit():
                if n == 0:
                    gated_linear(nc, g, "l0a", w_l0a, prefetch=rest)
                if n == 1:
                    matrix_lstm(nc, g, "l0x", w_l0x, ins["ctx"])
                if n == 2:
                    experts(nc, g, "l0f", w_l0f, 512, ACT.Gelu, False, "capacity")
                if n == 3:
                    attention(nc, g, "l1a", w_l1a, rope=True, window=WINDOW, prefetch=fetch)
                if n == 4:
                    attention(nc, g, "l1x", w_l1x, cross=True, key_mask=ins["key_mask"])
                if n == 5:
                    experts(nc, g, "l1f", w_l1f, 256, ACT.Silu, True, "choice")
                if n == 6:
                    attention(nc, g, "l2a", w_l2a, causal=True, alibi=True, prefetch=fetch)
                if n == 7:
                    decoder(nc, g, "l2x", w_l2x, ins["bool_mask"])
                if n == 8:
                    experts(nc, g, "l2f", w_l2f, 128, ACT.Gelu_apprx_tanh, False, "probs", biased=True, prefetch=fetch)
                if n == 9:
                    attention(nc, g, "l3a", w_l3a, causal=True)
                if n == 10:
                    attention(nc, g, "l3x", w_l3x, cross=True, full_mask=(ins["mask_q"], ins["mask_k"]))
                if n == 11:
                    experts(nc, g, "l3f", w_l3f, 256, ACT.Silu, True, "pair")

        stored = ctx.enter_context(nc.semaphore("stored"))
        block = ctx.enter_context(nc.Block())

        @block.sync
        def _(sp):
            sp.dma_start(out.rearrange("b (t p) d -> p b t d", p=P),
                         g.x[:, :, :].rearrange("p b (t d) -> p b t d", t=TPB)).then_inc(stored, 16)
            sp.wait_ge(stored, 16)


def layout(i):
    a = {"x": i["x"]}
    a["ctx"] = i["ctx_1024"]
    for n in ("Wq", "Wk", "Wv", "Wg", "gk_w1", "gk_w2"):
        a[f"L0_attn_{n}"] = i[f"L0_attn_{n}"]
    a["L0_attn_gk_b"] = i["L0_attn_gk_b"].reshape(P, 1)
    a["L0_attn_Wo"] = i["L0_attn_Wo"].reshape(2, P, D).transpose(1, 0, 2)
    a["L0_attn_rms_w"] = np.tile(i["L0_attn_rms_w"], (P, GH))
    for n, o in (("gq", 0), ("gk", D), ("gv", 2 * D)):
        a[f"L0_xattn_{n}"] = i["L0_xattn_ifgate_w"][:, o:o + D].T
    a["L0_xattn_bias"] = i["L0_xattn_ifgate_b"].reshape(2 * MH, 1)
    a["L0_xattn_outnorm"] = np.repeat(i["L0_xattn_outnorm_w"].reshape(1, D), P, 0)
    a["ctxT"] = np.transpose(i["ctx_1024"], (2, 0, 1))
    cos, sin = rope_tables()
    scale = np.float32(DH ** -0.5)
    a["cosq"], a["cosk"], a["sinq"], a["sink"] = cos * scale, cos, sin * scale, sin
    swap = np.arange(D).reshape(H, 2, DH // 2)[:, ::-1].reshape(D)
    rows = lambda v: np.repeat(v.reshape(1, -1), P, 0)
    for L, kind in (("L1", "attn"), ("L1", "xattn"), ("L3", "xattn")):
        for n in "qkvo":
            a[f"{L}_{kind}_W{n}T"] = i[f"{L}_{kind}_W{n}"].T
        for n in "qk":
            a[f"{L}_{kind}_b{n}"] = i[f"{L}_{kind}_b{n}"].reshape(D, 1)
        for n in "vo":
            a[f"{L}_{kind}_b{n}"] = rows(i[f"{L}_{kind}_b{n}"])
    for n in "qk":
        a[f"L1_attn_W{n}rT"] = i[f"L1_attn_W{n}"][swap].T
        a[f"L1_attn_b{n}r"] = i[f"L1_attn_b{n}"][swap].reshape(D, 1)
    for k, n in enumerate("qkv"):
        a[f"L2_attn_W{n}"] = i["L2_attn_w_attn"][:, k * D:(k + 1) * D]
        a[f"L3_attn_W{n}T"] = i["L3_attn_in_proj_weight"][k * D:(k + 1) * D].T
    a["L2_attn_w_proj"] = i["L2_attn_w_proj"]
    a["L3_attn_WoT"] = i["L3_attn_out_proj_weight"].T
    for n, src in (("L0_ffn_w_gate", 0), ("L1_ffn_Wg", 0), ("L1_ffn_Wu", 0), ("L2_ffn_w_in", 0), ("L3_ffn_W1", 0), ("L3_ffn_W2", 0)):
        a[n] = i[n].transpose(1, 0, 2)
    for n in ("L0_ffn_w_down", "L1_ffn_Wd", "L2_ffn_w_out", "L3_ffn_W3"):
        a[n] = i[n].reshape(E, -1, P, D).transpose(2, 0, 1, 3)
    for n in ("L0_ffn_wg", "L1_ffn_gate_w", "L2_ffn_router_w", "L3_ffn_Wg"):
        a[n] = i[n]
    a["L2_ffn_b_in"] = i["L2_ffn_b_in"].T
    a["L2_ffn_b_out"] = np.tile(i["L2_ffn_b_out"], (NT, 1))
    a["L2_attn_decay"] = rows(i["L2_attn_decay_raw"])
    for n in ("sa", "ca"):
        for k in ("wq", "wk", "wv"):
            a[f"L2_xattn_{n}_{k}"] = i[f"L2_xattn_{n}_{k}"]
        a[f"L2_xattn_{n}_wo"] = i[f"L2_xattn_{n}_wo"].reshape(-1, P, D).transpose(1, 0, 2)
    a["L2_xattn_fc1"] = i["L2_xattn_fc1_w"]
    a["L2_xattn_fc2"] = i["L2_xattn_fc2_w"].reshape(-1, P, D).transpose(1, 0, 2)
    a["L2_xattn_fc1_b"] = i["L2_xattn_fc1_b"].reshape(-1, P).T
    for n in ("sa_bo", "ca_bo", "fc2_b", "ln1_g", "ln1_b", "ln2_g", "ln2_b", "ln3_g", "ln3_b"):
        a[f"L2_xattn_{n}"] = rows(i[f"L2_xattn_{n}"])
    a["bool_mask"] = i["mask_BxS2_bk0"].reshape(1, B * S)
    a["key_mask"] = i["mask_Bx1x1xS2_if1"].reshape(1, B * S)
    m = i["mask_BxSxS2_if1"]
    a["mask_q"] = m.reshape(B, TPB, P, S).transpose(0, 2, 1, 3)
    a["mask_k"] = m.transpose(0, 2, 1).reshape(B, TPB, P, S).transpose(0, 2, 1, 3)
    for name, table in small_weights().items():
        pack = [np.concatenate([v, np.zeros((P - len(v), v.shape[1]), v.dtype)]) for v in (a[n].reshape(len(a[n]), -1) for n, _ in table.values())]
        a[f"small_{name}"] = np.concatenate(pack, 1)
    for table in small_weights().values():
        for n, _ in table.values():
            del a[n]
    return {k: np.ascontiguousarray(v) for k, v in a.items()}


def kernel(**inputs):
    import concourse.bacc as bacc
    from concourse.bass_utils import run_bass_kernel_spmd

    arrays = layout({n: np.asarray(v) for n, v in inputs.items()})
    nc = bacc.Bacc("TRN2", target_bir_lowering=False, num_devices=1)
    ins = {n: nc.dram_tensor(f"in_{n}", a.shape, mybir.dt.from_np(a.dtype), kind="ExternalInput").ap() for n, a in arrays.items()}
    out = nc.dram_tensor("out", (B, S, D), F32, kind="ExternalOutput").ap()
    build(nc, ins, out)
    r = run_bass_kernel_spmd(nc, [{f"in_{n}": a for n, a in arrays.items()}], core_ids=[0])
    return r.results[0]["out"]
```
